# Optimizing a Trainium2 kernel written in Bass

```python
import numpy as np
import jax
import jax.numpy as jnp

def _softmax(x, axis=-1):
    return jax.nn.softmax(x, axis=axis)

def _gelu(x):
    return jax.nn.gelu(x, approximate=True)

def _silu(x):
    return jax.nn.silu(x)

def _sigmoid(x):
    return jax.nn.sigmoid(x)

def _layernorm(x, axis=-1, eps=1e-05):
    m = jnp.mean(x, axis=axis, keepdims=True)
    v = jnp.var(x, axis=axis, keepdims=True)
    return (x - m) / jnp.sqrt(v + eps)

def _scatter_add(tgt, idx, src, axis=0):
    return tgt.at[idx].add(src)

def _segment_sum(src, seg, n):
    return jax.ops.segment_sum(src, seg, n)
kernel_name = 'mk_recurrent_d4_jaxref_r8_427dd6'

def setup_inputs(seed: int=0):
    np.random.seed(seed)
    _w = jnp.asarray

    def _L0_attn_setup():
        import jax, jax.numpy as jnp
        import numpy as np
        B, S, H_HID, H = (4, 512, 128, 16)
        D = H_HID // H

        def _gated_deltanet(x, Wq, bq, Wk, bk, Wv, bv, Wbeta, bbeta, Wo, bo):
            batch, seq, _ = x.shape
            q = (x @ Wq + bq).reshape(batch, seq, H, D)
            k = (x @ Wk + bk).reshape(batch, seq, H, D)
            v = (x @ Wv + bv).reshape(batch, seq, H, D)
            k = k / (jnp.linalg.norm(k, axis=-1, keepdims=True) + 1e-06)
            beta = jax.nn.sigmoid(x @ Wbeta + bbeta)[..., None]
            q = jnp.transpose(q, (1, 0, 2, 3))
            k = jnp.transpose(k, (1, 0, 2, 3))
            v = jnp.transpose(v, (1, 0, 2, 3))
            beta = jnp.transpose(beta, (1, 0, 2, 3))

            def _step(Sm, inputs):
                q_t, k_t, v_t, beta_t = inputs
                Sk = jnp.einsum('bhde,bhe->bhd', Sm, k_t)
                delta = v_t - Sk
                Sm = Sm + beta_t[..., None] * jnp.einsum('bhd,bhe->bhde', delta, k_t)
                o_t = jnp.einsum('bhde,bhe->bhd', Sm, q_t)
                return (Sm, o_t)
            S0 = jnp.zeros((batch, H, D, D), dtype=x.dtype)
            _, outputs = jax.lax.scan(_step, S0, (q, k, v, beta))
            outputs = jnp.transpose(outputs, (1, 0, 2, 3)).reshape(batch, seq, H_HID)
            return outputs @ Wo + bo
        key = jax.random.key(seed)
        ks = jax.random.split(key, 12)
        sc = 1.0 / np.sqrt(H_HID)
        return {'x': jax.random.normal(ks[0], (B, S, H_HID), jnp.float32), 'Wq': jax.random.normal(ks[1], (H_HID, H_HID), jnp.float32) * sc, 'bq': jnp.zeros((H_HID,), jnp.float32), 'Wk': jax.random.normal(ks[2], (H_HID, H_HID), jnp.float32) * sc, 'bk': jnp.zeros((H_HID,), jnp.float32), 'Wv': jax.random.normal(ks[3], (H_HID, H_HID), jnp.float32) * sc, 'bv': jnp.zeros((H_HID,), jnp.float32), 'Wbeta': jax.random.normal(ks[4], (H_HID, H), jnp.float32) * sc, 'bbeta': jnp.zeros((H,), jnp.float32), 'Wo': jax.random.normal(ks[5], (H_HID, H_HID), jnp.float32) * sc, 'bo': jnp.zeros((H_HID,), jnp.float32)}
    _L0_attn_in = _L0_attn_setup()

    def _L0_ffn_setup():
        import jax, jax.numpy as jnp
        import numpy as np

        def _bitlinear(x, w_latent):
            scale = jax.lax.stop_gradient(jnp.clip(jnp.mean(jnp.abs(w_latent), axis=1, keepdims=True), 1e-05, None))
            tern = jnp.clip(jnp.round(w_latent / scale), -1.0, 1.0)
            w = w_latent + jax.lax.stop_gradient(tern - w_latent)
            return x @ (w * scale).T
        key = jax.random.key(seed)
        ks = jax.random.split(key, 6)
        dim, hidden, rank = (128, 512, 16)
        B, S = (4, 512)
        x = jax.random.normal(ks[0], (B, S, dim), dtype=jnp.float32)
        w_fc = 0.02 * jax.random.normal(ks[1], (hidden, dim), dtype=jnp.float32)
        w_proj = 0.02 * jax.random.normal(ks[2], (dim, hidden), dtype=jnp.float32)
        u = 0.02 * jax.random.normal(ks[3], (hidden, rank), dtype=jnp.float32)
        v = 0.02 * jax.random.normal(ks[4], (rank, dim), dtype=jnp.float32)
        fast_b = jax.random.normal(ks[5], (rank, rank), dtype=jnp.float32)
        gate = jnp.float32(0.05)
        return {'x': x, 'fast_b': fast_b, 'w_fc': w_fc, 'w_proj': w_proj, 'u': u, 'v': v, 'gate': gate}
    _L0_ffn_in = _L0_ffn_setup()

    def _L1_attn_setup():
        import jax, jax.numpy as jnp
        import numpy as np
        import math
        B, T, D = (4, 512, 128)
        K, H, KH, C = (64, 4, 16, 64)
        MLP = 512
        EPS = 1e-05

        def _layernorm(x, g, b):
            m = jnp.mean(x, axis=-1, keepdims=True)
            v = jnp.mean((x - m) ** 2, axis=-1, keepdims=True)
            return (x - m) / jnp.sqrt(v + EPS) * g + b

        def _chunked_eigenstate(log_decay, frequency, beta_r, beta_i):
            Bt, Tt, Kt = beta_r.shape
            T_pad = (Tt + C - 1) // C * C
            if T_pad > Tt:
                beta_r = jnp.pad(beta_r, ((0, 0), (0, T_pad - Tt), (0, 0)))
                beta_i = jnp.pad(beta_i, ((0, 0), (0, T_pad - Tt), (0, 0)))
            n_chunks = T_pad // C
            mag = jax.nn.sigmoid(log_decay)
            powers = jnp.arange(C, dtype=log_decay.dtype)
            mag_pow = mag[:, None] ** powers[None, :]
            phases = frequency[:, None] * powers[None, :]
            kr = mag_pow * jnp.cos(phases)
            ki = mag_pow * jnp.sin(phases)
            ii = jnp.arange(C)
            idx = ii[None, :] - ii[:, None]
            mask = (idx >= 0).astype(kr.dtype)
            idxc = jnp.clip(idx, 0, C - 1)
            L_r = kr[:, idxc] * mask[None]
            L_i = ki[:, idxc] * mask[None]
            br = beta_r.reshape(Bt, n_chunks, C, Kt)
            bi = beta_i.reshape(Bt, n_chunks, C, Kt)
            intra_r = jnp.einsum('kjs,bnsk->bnjk', L_r, br) - jnp.einsum('kjs,bnsk->bnjk', L_i, bi)
            intra_i = jnp.einsum('kjs,bnsk->bnjk', L_r, bi) + jnp.einsum('kjs,bnsk->bnjk', L_i, br)
            first_col_r = L_r[:, :, 0]
            first_col_i = L_i[:, :, 0]

            def step(carry, intra):
                sr, si = carry
                ir, im = intra
                cr = first_col_r[None] * sr[:, :, None] - first_col_i[None] * si[:, :, None]
                ci = first_col_r[None] * si[:, :, None] + first_col_i[None] * sr[:, :, None]
                o_r = ir + jnp.transpose(cr, (0, 2, 1))
                o_i = im + jnp.transpose(ci, (0, 2, 1))
                return ((o_r[:, -1, :], o_i[:, -1, :]), (o_r, o_i))
            xs = (jnp.transpose(intra_r, (1, 0, 2, 3)), jnp.transpose(intra_i, (1, 0, 2, 3)))
            init = (jnp.zeros((Bt, Kt), beta_r.dtype), jnp.zeros((Bt, Kt), beta_r.dtype))
            _, (out_r, out_i) = jax.lax.scan(step, init, xs)
            c_r = jnp.transpose(out_r, (1, 0, 2, 3)).reshape(Bt, T_pad, Kt)[:, :Tt]
            c_i = jnp.transpose(out_i, (1, 0, 2, 3)).reshape(Bt, T_pad, Kt)[:, :Tt]
            return (c_r, c_i)
        key = jax.random.key(seed)
        ks = jax.random.split(key, 8)

        def n(k, shape, scale):
            return jax.random.normal(k, shape, dtype=jnp.float32) * scale
        return {'x': jax.random.normal(ks[0], (B, T, D), dtype=jnp.float32), 'w_in': n(ks[1], (2 * K, D), D ** (-0.5)), 'w_out': n(ks[2], (D, 2 * K), (2 * K) ** (-0.5)), 'w_gate': n(ks[3], (D, D), D ** (-0.5)), 'b_gate': jnp.full((D,), -2.0, dtype=jnp.float32), 'log_decay': jax.random.uniform(ks[4], (K,), minval=-3.0, maxval=-0.1, dtype=jnp.float32), 'frequency': jnp.linspace(0.0, 2.0 * math.pi * (1.0 - 1.0 / K), K, dtype=jnp.float32), 'coupling': jnp.eye(KH, dtype=jnp.float32)[None] + 0.01 * jax.random.normal(ks[5], (H, KH, KH), dtype=jnp.float32) / math.sqrt(KH), 'w_mlp1': n(ks[6], (MLP, D), D ** (-0.5)), 'b_mlp1': jnp.zeros((MLP,), jnp.float32), 'w_mlp2': n(ks[7], (D, MLP), MLP ** (-0.5)), 'b_mlp2': jnp.zeros((D,), jnp.float32), 'ln1_g': jnp.ones((D,), jnp.float32), 'ln1_b': jnp.zeros((D,), jnp.float32), 'ln2_g': jnp.ones((D,), jnp.float32), 'ln2_b': jnp.zeros((D,), jnp.float32)}
    _L1_attn_in = _L1_attn_setup()

    def _L1_ffn_setup():
        import jax, jax.numpy as jnp
        import numpy as np
        NUM_EXPERTS = 8
        TOP_K = 2
        CAPACITY_FACTOR = 1.0

        def _dispatch_compute(xf, top_expert, w1, w2, capacity):
            tokens, hs = xf.shape
            tpe = jnp.bincount(top_expert, length=NUM_EXPERTS)
            indices = jnp.argsort(top_expert)
            offsets = jnp.concatenate([jnp.zeros((1,), tpe.dtype), jnp.cumsum(tpe)[:-1]])
            slot = jnp.arange(capacity)
            pos = offsets[:, None] + slot[None, :]
            valid = slot[None, :] < tpe[:, None]
            tok_idx = indices[jnp.minimum(pos, tokens - 1)]
            xe = jnp.where(valid[..., None], xf[tok_idx], 0.0)
            h = jax.nn.gelu(jnp.einsum('ech,ehf->ecf', xe, w1), approximate=True)
            ye = jnp.einsum('ecf,efh->ech', h, w2)
            tok_safe = jnp.where(valid, tok_idx, tokens)
            out = jnp.zeros((tokens + 1, hs), xf.dtype).at[tok_safe.reshape(-1)].add(ye.reshape(-1, hs))
            return out[:tokens]
        key = jax.random.key(seed)
        k1, k2, k3, k4 = jax.random.split(key, 4)
        hs, ffn = (128, 512)
        x = jax.random.normal(k1, (256, 2, hs), dtype=jnp.float32)
        router_w = jax.random.normal(k2, (hs, NUM_EXPERTS), dtype=jnp.float32) * hs ** (-0.5)
        w1 = jax.random.normal(k3, (NUM_EXPERTS, hs, ffn), dtype=jnp.float32) * 0.02
        w2 = jax.random.normal(k4, (NUM_EXPERTS, ffn, hs), dtype=jnp.float32) * 0.02
        bias = jnp.zeros((1, 1, hs), dtype=jnp.float32)
        return {'x': x, 'router_w': router_w, 'w1': w1, 'w2': w2, 'bias': bias}
    _L1_ffn_in = _L1_ffn_setup()

    def _L2_attn_setup():
        import jax, jax.numpy as jnp
        import numpy as np
        EPS = 1e-05
        N_HEADS, KV_HEADS = (16, 4)

        def layernorm(x, g, b):
            m = jnp.mean(x, -1, keepdims=True)
            v = jnp.var(x, -1, keepdims=True)
            return (x - m) / jnp.sqrt(v + EPS) * g + b

        def mamba_block(x, ln_g, ln_b, in_w, conv_w, conv_b, xp_w, dt_w, dt_b, A_log, D_skip, out_w):
            Bsz, L, _ = x.shape
            d_inner = D_skip.shape[0]
            d_conv = conv_w.shape[-1]
            res = x
            h = layernorm(x, ln_g, ln_b)
            xs, gate = jnp.split(h @ in_w, 2, axis=-1)
            xc = jnp.pad(xs.transpose(0, 2, 1), ((0, 0), (0, 0), (d_conv - 1, 0)))
            xc = jax.lax.conv_general_dilated(xc, conv_w, (1,), 'VALID', dimension_numbers=('NCH', 'OIH', 'NCH'), feature_group_count=d_inner)
            xs = jax.nn.silu(xc.transpose(0, 2, 1) + conv_b)
            Bm, Cm = jnp.split(xs @ xp_w, 2, axis=-1)
            dt = jax.nn.softplus(Bm @ dt_w + dt_b)
            A = -jnp.exp(A_log)

            def step(hst, inp):
                xt, dtt, Bt, Ct = inp
                dA = jnp.exp(dtt[..., None] * A)
                hst = hst * dA + dtt[..., None] * Bt[:, None, :] * xt[..., None]
                yt = jnp.sum(hst * Ct[:, None, :], -1)
                return (hst, yt)
            h0 = jnp.zeros((Bsz, d_inner, A.shape[-1]), xs.dtype)
            _, y = jax.lax.scan(step, h0, (xs.transpose(1, 0, 2), dt.transpose(1, 0, 2), Bm.transpose(1, 0, 2), Cm.transpose(1, 0, 2)))
            y = y.transpose(1, 0, 2)
            y = (y + D_skip * xs) * jax.nn.silu(gate)
            return y @ out_w + res

        def attn_block(x, ln_g, ln_b, q_w, k_w, v_w, o_w):
            Bsz, L, D = x.shape
            H, KV = (N_HEADS, KV_HEADS)
            dh = D // H
            res = x
            h = layernorm(x, ln_g, ln_b)
            q = (h @ q_w).reshape(Bsz, L, H, dh).transpose(0, 2, 1, 3)
            k = (h @ k_w).reshape(Bsz, L, KV, dh).transpose(0, 2, 1, 3)
            v = (h @ v_w).reshape(Bsz, L, KV, dh).transpose(0, 2, 1, 3)
            inv = 1.0 / 10000.0 ** (jnp.arange(0, dh, 2, dtype=jnp.float32) / dh)
            fr = jnp.arange(L, dtype=jnp.float32)[:, None] * inv
            emb = jnp.concatenate([fr, fr], -1)
            cos, sin = (jnp.cos(emb), jnp.sin(emb))

            def rot(t):
                t1, t2 = jnp.split(t, 2, -1)
                return jnp.concatenate([-t2, t1], -1)
            q = q * cos + rot(q) * sin
            k = k * cos + rot(k) * sin
            g = H // KV
            k = jnp.repeat(k, g, axis=1)
            v = jnp.repeat(v, g, axis=1)
            sc = jnp.einsum('bhqd,bhkd->bhqk', q, k) / jnp.sqrt(jnp.float32(dh))
            mask = jnp.where(jnp.tril(jnp.ones((L, L), bool)), 0.0, -1000000000.0)
            p = jax.nn.softmax((sc + mask).astype(jnp.float32), -1).astype(q.dtype)
            o = jnp.einsum('bhqk,bhkd->bhqd', p, v).transpose(0, 2, 1, 3).reshape(Bsz, L, D)
            return o @ o_w + res
        key = jax.random.key(seed)
        B, L, D = (4, 128, 128)
        d_inner, d_state, d_conv = (256, 16, 4)
        H, KV, dh = (N_HEADS, KV_HEADS, D // N_HEADS)
        dff = 512
        ks = jax.random.split(key, 16)
        w = lambda k, shape: jax.random.normal(k, shape, jnp.float32) * 0.02
        return {'x': jax.random.normal(ks[0], (B, L, D), jnp.float32), 'ln1_g': jnp.ones(D), 'ln1_b': jnp.zeros(D), 'in_proj_w': w(ks[1], (D, 2 * d_inner)), 'conv_w': w(ks[2], (d_inner, 1, d_conv)), 'conv_b': jnp.zeros(d_inner), 'x_proj_w': w(ks[3], (d_inner, 2 * d_state)), 'dt_proj_w': w(ks[4], (d_state, d_inner)), 'dt_proj_b': jnp.zeros(d_inner), 'A_log': jnp.log(jnp.tile(jnp.arange(1, d_state + 1, dtype=jnp.float32), (d_inner, 1))), 'D_skip': jnp.ones(d_inner), 'out_proj_w': w(ks[5], (d_inner, D)), 'ln2_g': jnp.ones(D), 'ln2_b': jnp.zeros(D), 'q_w': w(ks[6], (D, H * dh)), 'k_w': w(ks[7], (D, KV * dh)), 'v_w': w(ks[8], (D, KV * dh)), 'o_w': w(ks[9], (H * dh, D)), 'ln3_g': jnp.ones(D), 'ln3_b': jnp.zeros(D), 'w1': w(ks[10], (D, dff)), 'w2': w(ks[11], (dff, D)), 'w3': w(ks[12], (D, dff))}
    _L2_attn_in = _L2_attn_setup()

    def _L2_ffn_setup():
        import jax, jax.numpy as jnp
        import numpy as np
        B, S, D, H, E = (8, 256, 128, 512, 8)
        CAPACITY_FACTOR = 2.0
        LN_EPS = 1e-05

        def _layernorm(x, g, b):
            mu = jnp.mean(x, axis=-1, keepdims=True)
            var = jnp.mean(jnp.square(x - mu), axis=-1, keepdims=True)
            return (x - mu) * jax.lax.rsqrt(var + LN_EPS) * g + b
        if __name__ == '__main__':
            out = reference(**setup_inputs())
            print(out.shape, out.dtype)
        key = jax.random.key(seed)
        ks = jax.random.split(key, 6)
        s = 0.02
        return {'x': jax.random.normal(ks[0], (B, S, D), jnp.float32), 'W_proj': jax.random.normal(ks[1], (D, D), jnp.float32) * s, 'b_proj': jnp.zeros((D,), jnp.float32), 'W_gate': jax.random.normal(ks[2], (D, E), jnp.float32) * s, 'W1': jax.random.normal(ks[3], (E, D, H), jnp.float32) * s, 'b1': jnp.zeros((E, H), jnp.float32), 'ln1_g': jnp.ones((E, H), jnp.float32), 'ln1_b': jnp.zeros((E, H), jnp.float32), 'W2': jax.random.normal(ks[4], (E, H, D), jnp.float32) * s, 'b2': jnp.zeros((E, D), jnp.float32), 'ln_g': jnp.ones((D,), jnp.float32), 'ln_b': jnp.zeros((D,), jnp.float32)}
    _L2_ffn_in = _L2_ffn_setup()

    def _L3_attn_setup():
        import jax, jax.numpy as jnp
        import numpy as np
        from jax import lax
        D_MODEL = 128
        D_STATE = 16
        D_CONV = 4
        EXPAND = 2
        D_INNER = D_MODEL * EXPAND
        DT_RANK = 64
        BATCH = 2
        SEQ = 512
        DT_MIN, DT_MAX = (0.001, 0.1)
        key = jax.random.key(seed)
        ks = jax.random.split(key, 12)
        xavier = lambda k, shape: jax.random.normal(k, shape, jnp.float32) * np.float32(np.sqrt(2.0 / (shape[0] + shape[1])))
        x = jax.random.normal(ks[0], (BATCH, SEQ, D_MODEL), jnp.float32)
        in_proj_w = xavier(ks[1], (2 * D_INNER, D_MODEL))
        in_proj_b = jnp.zeros((2 * D_INNER,), jnp.float32)
        conv_w = jax.random.normal(ks[2], (D_INNER, D_CONV), jnp.float32) * 0.02
        conv_b = jnp.zeros((D_INNER,), jnp.float32)
        A_log = jnp.log(jnp.tile(jnp.arange(1, D_STATE + 1, dtype=jnp.float32)[:, None], (1, D_INNER)))
        D = jnp.ones((D_INNER,), jnp.float32)
        x_proj_w = xavier(ks[3], (DT_RANK + 2 * D_STATE, D_INNER))
        dt_proj_w = jax.random.normal(ks[4], (D_INNER, DT_RANK), jnp.float32) * np.float32(DT_RANK ** (-0.5))
        dt = jnp.exp(jax.random.uniform(ks[5], (D_INNER,), jnp.float32) * np.float32(np.log(DT_MAX) - np.log(DT_MIN)) + np.float32(np.log(DT_MIN)))
        dt_proj_b = dt + jnp.log(-jnp.expm1(-dt))
        out_proj_w = xavier(ks[6], (D_MODEL, D_INNER))
        out_proj_b = jnp.zeros((D_MODEL,), jnp.float32)
        return {'x': x, 'in_proj_w': in_proj_w, 'in_proj_b': in_proj_b, 'conv_w': conv_w, 'conv_b': conv_b, 'A_log': A_log, 'D': D, 'x_proj_w': x_proj_w, 'dt_proj_w': dt_proj_w, 'dt_proj_b': dt_proj_b, 'out_proj_w': out_proj_w, 'out_proj_b': out_proj_b}
    _L3_attn_in = _L3_attn_setup()

    def _L3_ffn_setup():
        import jax, jax.numpy as jnp
        import numpy as np
        EPS = 1e-08

        def _ternary_linear(x, w):
            alpha = jnp.mean(jnp.abs(w))
            w_t = jnp.sign(w) * (jnp.abs(w) > 0.5 * alpha).astype(w.dtype)
            w_q = w + jax.lax.stop_gradient(w_t - w)
            d = x.shape[-1]
            rms = jnp.sqrt(jnp.sum(x * x, axis=-1, keepdims=True)) / jnp.sqrt(jnp.asarray(d, x.dtype))
            x_norm = x / (rms + EPS)
            return jnp.einsum('bsd,fd->bsf', x_norm, w_q)
        key = jax.random.key(seed)
        k1, k2, k3 = jax.random.split(key, 3)
        d_model, d_ff = (128, 512)
        B, S = (4, 512)
        x = jax.random.normal(k1, (B, S, d_model), dtype=jnp.float32)
        w_up = jax.random.normal(k2, (d_ff, d_model), dtype=jnp.float32) * 0.02
        w_down = jax.random.normal(k3, (d_model, d_ff), dtype=jnp.float32) * 0.02
        return {'x': x, 'w_up': w_up, 'w_down': w_down}
    _L3_ffn_in = _L3_ffn_setup()
    _d = {'L0_attn_x': _L0_attn_in['x'], 'L0_attn_Wq': _L0_attn_in['Wq'], 'L0_attn_bq': _L0_attn_in['bq'], 'L0_attn_Wk': _L0_attn_in['Wk'], 'L0_attn_bk': _L0_attn_in['bk'], 'L0_attn_Wv': _L0_attn_in['Wv'], 'L0_attn_bv': _L0_attn_in['bv'], 'L0_attn_Wbeta': _L0_attn_in['Wbeta'], 'L0_attn_bbeta': _L0_attn_in['bbeta'], 'L0_attn_Wo': _L0_attn_in['Wo'], 'L0_attn_bo': _L0_attn_in['bo'], 'L0_ffn_fast_b': _L0_ffn_in['fast_b'], 'L0_ffn_w_fc': _L0_ffn_in['w_fc'], 'L0_ffn_w_proj': _L0_ffn_in['w_proj'], 'L0_ffn_u': _L0_ffn_in['u'], 'L0_ffn_v': _L0_ffn_in['v'], 'L0_ffn_gate': _L0_ffn_in['gate'], 'L1_attn_w_in': _L1_attn_in['w_in'], 'L1_attn_w_out': _L1_attn_in['w_out'], 'L1_attn_w_gate': _L1_attn_in['w_gate'], 'L1_attn_b_gate': _L1_attn_in['b_gate'], 'L1_attn_log_decay': _L1_attn_in['log_decay'], 'L1_attn_frequency': _L1_attn_in['frequency'], 'L1_attn_coupling': _L1_attn_in['coupling'], 'L1_attn_w_mlp1': _L1_attn_in['w_mlp1'], 'L1_attn_b_mlp1': _L1_attn_in['b_mlp1'], 'L1_attn_w_mlp2': _L1_attn_in['w_mlp2'], 'L1_attn_b_mlp2': _L1_attn_in['b_mlp2'], 'L1_attn_ln1_g': _L1_attn_in['ln1_g'], 'L1_attn_ln1_b': _L1_attn_in['ln1_b'], 'L1_attn_ln2_g': _L1_attn_in['ln2_g'], 'L1_attn_ln2_b': _L1_attn_in['ln2_b'], 'L1_ffn_router_w': _L1_ffn_in['router_w'], 'L1_ffn_w1': _L1_ffn_in['w1'], 'L1_ffn_w2': _L1_ffn_in['w2'], 'L1_ffn_bias': _L1_ffn_in['bias'], 'L2_attn_ln1_g': _L2_attn_in['ln1_g'], 'L2_attn_ln1_b': _L2_attn_in['ln1_b'], 'L2_attn_in_proj_w': _L2_attn_in['in_proj_w'], 'L2_attn_conv_w': _L2_attn_in['conv_w'], 'L2_attn_conv_b': _L2_attn_in['conv_b'], 'L2_attn_x_proj_w': _L2_attn_in['x_proj_w'], 'L2_attn_dt_proj_w': _L2_attn_in['dt_proj_w'], 'L2_attn_dt_proj_b': _L2_attn_in['dt_proj_b'], 'L2_attn_A_log': _L2_attn_in['A_log'], 'L2_attn_D_skip': _L2_attn_in['D_skip'], 'L2_attn_out_proj_w': _L2_attn_in['out_proj_w'], 'L2_attn_ln2_g': _L2_attn_in['ln2_g'], 'L2_attn_ln2_b': _L2_attn_in['ln2_b'], 'L2_attn_q_w': _L2_attn_in['q_w'], 'L2_attn_k_w': _L2_attn_in['k_w'], 'L2_attn_v_w': _L2_attn_in['v_w'], 'L2_attn_o_w': _L2_attn_in['o_w'], 'L2_attn_ln3_g': _L2_attn_in['ln3_g'], 'L2_attn_ln3_b': _L2_attn_in['ln3_b'], 'L2_attn_w1': _L2_attn_in['w1'], 'L2_attn_w2': _L2_attn_in['w2'], 'L2_attn_w3': _L2_attn_in['w3'], 'L2_ffn_W_proj': _L2_ffn_in['W_proj'], 'L2_ffn_b_proj': _L2_ffn_in['b_proj'], 'L2_ffn_W_gate': _L2_ffn_in['W_gate'], 'L2_ffn_W1': _L2_ffn_in['W1'], 'L2_ffn_b1': _L2_ffn_in['b1'], 'L2_ffn_ln1_g': _L2_ffn_in['ln1_g'], 'L2_ffn_ln1_b': _L2_ffn_in['ln1_b'], 'L2_ffn_W2': _L2_ffn_in['W2'], 'L2_ffn_b2': _L2_ffn_in['b2'], 'L2_ffn_ln_g': _L2_ffn_in['ln_g'], 'L2_ffn_ln_b': _L2_ffn_in['ln_b'], 'L3_attn_in_proj_w': _L3_attn_in['in_proj_w'], 'L3_attn_in_proj_b': _L3_attn_in['in_proj_b'], 'L3_attn_conv_w': _L3_attn_in['conv_w'], 'L3_attn_conv_b': _L3_attn_in['conv_b'], 'L3_attn_A_log': _L3_attn_in['A_log'], 'L3_attn_D': _L3_attn_in['D'], 'L3_attn_x_proj_w': _L3_attn_in['x_proj_w'], 'L3_attn_dt_proj_w': _L3_attn_in['dt_proj_w'], 'L3_attn_dt_proj_b': _L3_attn_in['dt_proj_b'], 'L3_attn_out_proj_w': _L3_attn_in['out_proj_w'], 'L3_attn_out_proj_b': _L3_attn_in['out_proj_b'], 'L3_ffn_w_up': _L3_ffn_in['w_up'], 'L3_ffn_w_down': _L3_ffn_in['w_down']}
    _x0 = _d['L0_attn_x']
    _d['L0_attn_x'] = jax.random.normal(jax.random.fold_in(jax.random.key(seed), 1), (32, 256, 128), dtype=_x0.dtype)
    del _x0
    return _d

def reference(L0_attn_x, L0_attn_Wq, L0_attn_bq, L0_attn_Wk, L0_attn_bk, L0_attn_Wv, L0_attn_bv, L0_attn_Wbeta, L0_attn_bbeta, L0_attn_Wo, L0_attn_bo, L0_ffn_fast_b, L0_ffn_w_fc, L0_ffn_w_proj, L0_ffn_u, L0_ffn_v, L0_ffn_gate, L1_attn_w_in, L1_attn_w_out, L1_attn_w_gate, L1_attn_b_gate, L1_attn_log_decay, L1_attn_frequency, L1_attn_coupling, L1_attn_w_mlp1, L1_attn_b_mlp1, L1_attn_w_mlp2, L1_attn_b_mlp2, L1_attn_ln1_g, L1_attn_ln1_b, L1_attn_ln2_g, L1_attn_ln2_b, L1_ffn_router_w, L1_ffn_w1, L1_ffn_w2, L1_ffn_bias, L2_attn_ln1_g, L2_attn_ln1_b, L2_attn_in_proj_w, L2_attn_conv_w, L2_attn_conv_b, L2_attn_x_proj_w, L2_attn_dt_proj_w, L2_attn_dt_proj_b, L2_attn_A_log, L2_attn_D_skip, L2_attn_out_proj_w, L2_attn_ln2_g, L2_attn_ln2_b, L2_attn_q_w, L2_attn_k_w, L2_attn_v_w, L2_attn_o_w, L2_attn_ln3_g, L2_attn_ln3_b, L2_attn_w1, L2_attn_w2, L2_attn_w3, L2_ffn_W_proj, L2_ffn_b_proj, L2_ffn_W_gate, L2_ffn_W1, L2_ffn_b1, L2_ffn_ln1_g, L2_ffn_ln1_b, L2_ffn_W2, L2_ffn_b2, L2_ffn_ln_g, L2_ffn_ln_b, L3_attn_in_proj_w, L3_attn_in_proj_b, L3_attn_conv_w, L3_attn_conv_b, L3_attn_A_log, L3_attn_D, L3_attn_x_proj_w, L3_attn_dt_proj_w, L3_attn_dt_proj_b, L3_attn_out_proj_w, L3_attn_out_proj_b, L3_ffn_w_up, L3_ffn_w_down):

    def _L0_attn_ref(x, Wq, bq, Wk, bk, Wv, bv, Wbeta, bbeta, Wo, bo):
        import jax, jax.numpy as jnp
        import numpy as np
        B, S, H_HID, H = (4, 512, 128, 16)
        D = H_HID // H

        def _gated_deltanet(x, Wq, bq, Wk, bk, Wv, bv, Wbeta, bbeta, Wo, bo):
            batch, seq, _ = x.shape
            q = (x @ Wq + bq).reshape(batch, seq, H, D)
            k = (x @ Wk + bk).reshape(batch, seq, H, D)
            v = (x @ Wv + bv).reshape(batch, seq, H, D)
            k = k / (jnp.linalg.norm(k, axis=-1, keepdims=True) + 1e-06)
            beta = jax.nn.sigmoid(x @ Wbeta + bbeta)[..., None]
            q = jnp.transpose(q, (1, 0, 2, 3))
            k = jnp.transpose(k, (1, 0, 2, 3))
            v = jnp.transpose(v, (1, 0, 2, 3))
            beta = jnp.transpose(beta, (1, 0, 2, 3))

            def _step(Sm, inputs):
                q_t, k_t, v_t, beta_t = inputs
                Sk = jnp.einsum('bhde,bhe->bhd', Sm, k_t)
                delta = v_t - Sk
                Sm = Sm + beta_t[..., None] * jnp.einsum('bhd,bhe->bhde', delta, k_t)
                o_t = jnp.einsum('bhde,bhe->bhd', Sm, q_t)
                return (Sm, o_t)
            S0 = jnp.zeros((batch, H, D, D), dtype=x.dtype)
            _, outputs = jax.lax.scan(_step, S0, (q, k, v, beta))
            outputs = jnp.transpose(outputs, (1, 0, 2, 3)).reshape(batch, seq, H_HID)
            return outputs @ Wo + bo
        return _gated_deltanet(x, Wq, bq, Wk, bk, Wv, bv, Wbeta, bbeta, Wo, bo)

    def _L0_ffn_ref(x, fast_b, w_fc, w_proj, u, v, gate):
        import jax, jax.numpy as jnp
        import numpy as np

        def _bitlinear(x, w_latent):
            scale = jax.lax.stop_gradient(jnp.clip(jnp.mean(jnp.abs(w_latent), axis=1, keepdims=True), 1e-05, None))
            tern = jnp.clip(jnp.round(w_latent / scale), -1.0, 1.0)
            w = w_latent + jax.lax.stop_gradient(tern - w_latent)
            return x @ (w * scale).T
        h = _bitlinear(x, w_fc) + gate * (x @ v.T @ fast_b.T @ u.T)
        r = jnp.maximum(h, 0.0)
        return _bitlinear(r * r, w_proj)

    def _L1_attn_ref(x, w_in, w_out, w_gate, b_gate, log_decay, frequency, coupling, w_mlp1, b_mlp1, w_mlp2, b_mlp2, ln1_g, ln1_b, ln2_g, ln2_b):
        import jax, jax.numpy as jnp
        import numpy as np
        import math
        B, T, D = (4, 512, 128)
        K, H, KH, C = (64, 4, 16, 64)
        MLP = 512
        EPS = 1e-05

        def _layernorm(x, g, b):
            m = jnp.mean(x, axis=-1, keepdims=True)
            v = jnp.mean((x - m) ** 2, axis=-1, keepdims=True)
            return (x - m) / jnp.sqrt(v + EPS) * g + b

        def _chunked_eigenstate(log_decay, frequency, beta_r, beta_i):
            Bt, Tt, Kt = beta_r.shape
            T_pad = (Tt + C - 1) // C * C
            if T_pad > Tt:
                beta_r = jnp.pad(beta_r, ((0, 0), (0, T_pad - Tt), (0, 0)))
                beta_i = jnp.pad(beta_i, ((0, 0), (0, T_pad - Tt), (0, 0)))
            n_chunks = T_pad // C
            mag = jax.nn.sigmoid(log_decay)
            powers = jnp.arange(C, dtype=log_decay.dtype)
            mag_pow = mag[:, None] ** powers[None, :]
            phases = frequency[:, None] * powers[None, :]
            kr = mag_pow * jnp.cos(phases)
            ki = mag_pow * jnp.sin(phases)
            ii = jnp.arange(C)
            idx = ii[None, :] - ii[:, None]
            mask = (idx >= 0).astype(kr.dtype)
            idxc = jnp.clip(idx, 0, C - 1)
            L_r = kr[:, idxc] * mask[None]
            L_i = ki[:, idxc] * mask[None]
            br = beta_r.reshape(Bt, n_chunks, C, Kt)
            bi = beta_i.reshape(Bt, n_chunks, C, Kt)
            intra_r = jnp.einsum('kjs,bnsk->bnjk', L_r, br) - jnp.einsum('kjs,bnsk->bnjk', L_i, bi)
            intra_i = jnp.einsum('kjs,bnsk->bnjk', L_r, bi) + jnp.einsum('kjs,bnsk->bnjk', L_i, br)
            first_col_r = L_r[:, :, 0]
            first_col_i = L_i[:, :, 0]

            def step(carry, intra):
                sr, si = carry
                ir, im = intra
                cr = first_col_r[None] * sr[:, :, None] - first_col_i[None] * si[:, :, None]
                ci = first_col_r[None] * si[:, :, None] + first_col_i[None] * sr[:, :, None]
                o_r = ir + jnp.transpose(cr, (0, 2, 1))
                o_i = im + jnp.transpose(ci, (0, 2, 1))
                return ((o_r[:, -1, :], o_i[:, -1, :]), (o_r, o_i))
            xs = (jnp.transpose(intra_r, (1, 0, 2, 3)), jnp.transpose(intra_i, (1, 0, 2, 3)))
            init = (jnp.zeros((Bt, Kt), beta_r.dtype), jnp.zeros((Bt, Kt), beta_r.dtype))
            _, (out_r, out_i) = jax.lax.scan(step, init, xs)
            c_r = jnp.transpose(out_r, (1, 0, 2, 3)).reshape(Bt, T_pad, Kt)[:, :Tt]
            c_i = jnp.transpose(out_i, (1, 0, 2, 3)).reshape(Bt, T_pad, Kt)[:, :Tt]
            return (c_r, c_i)
        residual = x
        x_norm = _layernorm(x, ln1_g, ln1_b)
        beta = x_norm @ w_in.T
        beta_r, beta_i = jnp.split(beta, 2, axis=-1)
        c_r, c_i = _chunked_eigenstate(log_decay, frequency, beta_r, beta_i)
        c_rh = c_r.reshape(x.shape[0], x.shape[1], H, KH)
        c_ih = c_i.reshape(x.shape[0], x.shape[1], H, KH)
        c_r = jnp.einsum('hjk,bthk->bthj', coupling, c_rh).reshape(x.shape[0], x.shape[1], K)
        c_i = jnp.einsum('hjk,bthk->bthj', coupling, c_ih).reshape(x.shape[0], x.shape[1], K)
        h = jnp.concatenate([c_r, c_i], axis=-1) @ w_out.T
        gate = jax.nn.sigmoid(x_norm @ w_gate.T + b_gate)
        x1 = residual + gate * h
        x2n = _layernorm(x1, ln2_g, ln2_b)
        mlp = jax.nn.silu(x2n @ w_mlp1.T + b_mlp1) @ w_mlp2.T + b_mlp2
        return x1 + mlp

    def _L1_ffn_ref(x, router_w, w1, w2, bias):
        import jax, jax.numpy as jnp
        import numpy as np
        NUM_EXPERTS = 8
        TOP_K = 2
        CAPACITY_FACTOR = 1.0

        def _dispatch_compute(xf, top_expert, w1, w2, capacity):
            tokens, hs = xf.shape
            tpe = jnp.bincount(top_expert, length=NUM_EXPERTS)
            indices = jnp.argsort(top_expert)
            offsets = jnp.concatenate([jnp.zeros((1,), tpe.dtype), jnp.cumsum(tpe)[:-1]])
            slot = jnp.arange(capacity)
            pos = offsets[:, None] + slot[None, :]
            valid = slot[None, :] < tpe[:, None]
            tok_idx = indices[jnp.minimum(pos, tokens - 1)]
            xe = jnp.where(valid[..., None], xf[tok_idx], 0.0)
            h = jax.nn.gelu(jnp.einsum('ech,ehf->ecf', xe, w1), approximate=True)
            ye = jnp.einsum('ecf,efh->ech', h, w2)
            tok_safe = jnp.where(valid, tok_idx, tokens)
            out = jnp.zeros((tokens + 1, hs), xf.dtype).at[tok_safe.reshape(-1)].add(ye.reshape(-1, hs))
            return out[:tokens]
        sl, bs, hs = x.shape
        tokens = sl * bs
        capacity = int(CAPACITY_FACTOR * tokens / NUM_EXPERTS)
        xf = x.reshape(tokens, hs)
        scores = jax.nn.softmax(xf @ router_w, axis=-1)
        expert_weights, top_experts = jax.lax.top_k(scores, TOP_K)
        out = jnp.zeros_like(xf)
        for k in range(TOP_K):
            y = _dispatch_compute(xf, top_experts[:, k].astype(jnp.int32), w1, w2, capacity)
            out = out + y * expert_weights[:, k][:, None]
        return out.reshape(sl, bs, hs) + bias

    def _L2_attn_ref(x, ln1_g, ln1_b, in_proj_w, conv_w, conv_b, x_proj_w, dt_proj_w, dt_proj_b, A_log, D_skip, out_proj_w, ln2_g, ln2_b, q_w, k_w, v_w, o_w, ln3_g, ln3_b, w1, w2, w3):
        import jax, jax.numpy as jnp
        import numpy as np
        EPS = 1e-05
        N_HEADS, KV_HEADS = (16, 4)

        def layernorm(x, g, b):
            m = jnp.mean(x, -1, keepdims=True)
            v = jnp.var(x, -1, keepdims=True)
            return (x - m) / jnp.sqrt(v + EPS) * g + b

        def mamba_block(x, ln_g, ln_b, in_w, conv_w, conv_b, xp_w, dt_w, dt_b, A_log, D_skip, out_w):
            Bsz, L, _ = x.shape
            d_inner = D_skip.shape[0]
            d_conv = conv_w.shape[-1]
            res = x
            h = layernorm(x, ln_g, ln_b)
            xs, gate = jnp.split(h @ in_w, 2, axis=-1)
            xc = jnp.pad(xs.transpose(0, 2, 1), ((0, 0), (0, 0), (d_conv - 1, 0)))
            xc = jax.lax.conv_general_dilated(xc, conv_w, (1,), 'VALID', dimension_numbers=('NCH', 'OIH', 'NCH'), feature_group_count=d_inner)
            xs = jax.nn.silu(xc.transpose(0, 2, 1) + conv_b)
            Bm, Cm = jnp.split(xs @ xp_w, 2, axis=-1)
            dt = jax.nn.softplus(Bm @ dt_w + dt_b)
            A = -jnp.exp(A_log)

            def step(hst, inp):
                xt, dtt, Bt, Ct = inp
                dA = jnp.exp(dtt[..., None] * A)
                hst = hst * dA + dtt[..., None] * Bt[:, None, :] * xt[..., None]
                yt = jnp.sum(hst * Ct[:, None, :], -1)
                return (hst, yt)
            h0 = jnp.zeros((Bsz, d_inner, A.shape[-1]), xs.dtype)
            _, y = jax.lax.scan(step, h0, (xs.transpose(1, 0, 2), dt.transpose(1, 0, 2), Bm.transpose(1, 0, 2), Cm.transpose(1, 0, 2)))
            y = y.transpose(1, 0, 2)
            y = (y + D_skip * xs) * jax.nn.silu(gate)
            return y @ out_w + res

        def attn_block(x, ln_g, ln_b, q_w, k_w, v_w, o_w):
            Bsz, L, D = x.shape
            H, KV = (N_HEADS, KV_HEADS)
            dh = D // H
            res = x
            h = layernorm(x, ln_g, ln_b)
            q = (h @ q_w).reshape(Bsz, L, H, dh).transpose(0, 2, 1, 3)
            k = (h @ k_w).reshape(Bsz, L, KV, dh).transpose(0, 2, 1, 3)
            v = (h @ v_w).reshape(Bsz, L, KV, dh).transpose(0, 2, 1, 3)
            inv = 1.0 / 10000.0 ** (jnp.arange(0, dh, 2, dtype=jnp.float32) / dh)
            fr = jnp.arange(L, dtype=jnp.float32)[:, None] * inv
            emb = jnp.concatenate([fr, fr], -1)
            cos, sin = (jnp.cos(emb), jnp.sin(emb))

            def rot(t):
                t1, t2 = jnp.split(t, 2, -1)
                return jnp.concatenate([-t2, t1], -1)
            q = q * cos + rot(q) * sin
            k = k * cos + rot(k) * sin
            g = H // KV
            k = jnp.repeat(k, g, axis=1)
            v = jnp.repeat(v, g, axis=1)
            sc = jnp.einsum('bhqd,bhkd->bhqk', q, k) / jnp.sqrt(jnp.float32(dh))
            mask = jnp.where(jnp.tril(jnp.ones((L, L), bool)), 0.0, -1000000000.0)
            p = jax.nn.softmax((sc + mask).astype(jnp.float32), -1).astype(q.dtype)
            o = jnp.einsum('bhqk,bhkd->bhqd', p, v).transpose(0, 2, 1, 3).reshape(Bsz, L, D)
            return o @ o_w + res
        x = mamba_block(x, ln1_g, ln1_b, in_proj_w, conv_w, conv_b, x_proj_w, dt_proj_w, dt_proj_b, A_log, D_skip, out_proj_w)
        x = attn_block(x, ln2_g, ln2_b, q_w, k_w, v_w, o_w)
        h = layernorm(x, ln3_g, ln3_b)
        return x + jax.nn.silu(h @ w1) * (h @ w3) @ w2

    def _L2_ffn_ref(x, W_proj, b_proj, W_gate, W1, b1, ln1_g, ln1_b, W2, b2, ln_g, ln_b):
        import jax, jax.numpy as jnp
        import numpy as np
        B, S, D, H, E = (8, 256, 128, 512, 8)
        CAPACITY_FACTOR = 2.0
        LN_EPS = 1e-05

        def _layernorm(x, g, b):
            mu = jnp.mean(x, axis=-1, keepdims=True)
            var = jnp.mean(jnp.square(x - mu), axis=-1, keepdims=True)
            return (x - mu) * jax.lax.rsqrt(var + LN_EPS) * g + b
        if __name__ == '__main__':
            out = reference(**setup_inputs())
            print(out.shape, out.dtype)
        b_, s_, d_ = x.shape
        N = b_ * s_
        capacity = max(int(CAPACITY_FACTOR * N / E), 1)
        x_flat = (jnp.einsum('bsd,de->bse', x, W_proj) + b_proj).reshape(N, d_)
        router_logits = x_flat @ W_gate
        routing_weights = jax.nn.softmax(router_logits, axis=-1)
        ew, ei = jax.lax.top_k(routing_weights, 1)
        ew = ew / jnp.sum(ew, axis=-1, keepdims=True)
        tok_weight = ew[:, 0]
        tok_expert = ei[:, 0]
        assigned = tok_expert[None, :] == jnp.arange(E)[:, None]
        masked = jnp.where(assigned, tok_weight[None, :], -1.0)
        top_scores, top_idx = jax.lax.top_k(masked, capacity)
        valid = top_scores > 0.0
        tok = x_flat[top_idx]
        h = jnp.einsum('ecd,edh->ech', tok, W1) + b1[:, None, :]
        h = _layernorm(h, ln1_g[:, None, :], ln1_b[:, None, :])
        h = jax.nn.gelu(h, approximate=False)
        out_e = jnp.einsum('ech,ehd->ecd', h, W2) + b2[:, None, :]
        w = jnp.where(valid, top_scores, 0.0)[..., None]
        weighted = out_e * w
        outputs = jnp.zeros((N, d_), x.dtype).at[top_idx.reshape(-1)].add(weighted.reshape(-1, d_))
        final = _layernorm(outputs.reshape(b_, s_, d_), ln_g, ln_b)
        return final

    def _L3_attn_ref(x, in_proj_w, in_proj_b, conv_w, conv_b, A_log, D, x_proj_w, dt_proj_w, dt_proj_b, out_proj_w, out_proj_b):
        import jax, jax.numpy as jnp
        import numpy as np
        from jax import lax
        D_MODEL = 128
        D_STATE = 16
        D_CONV = 4
        EXPAND = 2
        D_INNER = D_MODEL * EXPAND
        DT_RANK = 64
        BATCH = 2
        SEQ = 512
        DT_MIN, DT_MAX = (0.001, 0.1)
        b, L, _ = x.shape
        xz = x @ in_proj_w.T + in_proj_b
        x_in, z = jnp.split(xz, 2, axis=-1)
        x_pad = jnp.pad(x_in, ((0, 0), (D_CONV - 1, 0), (0, 0)))
        x_conv = conv_b
        x_conv = sum((x_pad[:, k:k + L, :] * conv_w[None, None, :, k] for k in range(D_CONV))) + conv_b
        x_conv = jax.nn.silu(x_conv)
        x_dbl = x_conv @ x_proj_w.T
        dt_low = x_dbl[..., :DT_RANK]
        Bm = x_dbl[..., DT_RANK:DT_RANK + D_STATE]
        Cm = x_dbl[..., DT_RANK + D_STATE:]
        dt = jax.nn.softplus(dt_low @ dt_proj_w.T + dt_proj_b)
        A = -jnp.exp(A_log).T
        safe_A = jnp.where(jnp.abs(A) < 1e-06, jnp.ones_like(A), A)

        def step(h, inp):
            xt, dtt, Bt, Ct = inp
            A_bar = jnp.exp(dtt[..., None] * A)
            B_bar = (A_bar - 1.0) / safe_A * Bt[:, None, :]
            h = A_bar * h + B_bar * xt[..., None]
            y = jnp.einsum('bds,bs->bd', h, Ct) + D * xt
            return (h, y)
        xs = (jnp.swapaxes(x_conv, 0, 1), jnp.swapaxes(dt, 0, 1), jnp.swapaxes(Bm, 0, 1), jnp.swapaxes(Cm, 0, 1))
        h0 = jnp.zeros((b, D_INNER, D_STATE), x.dtype)
        _, ys = lax.scan(step, h0, xs)
        y = jnp.swapaxes(ys, 0, 1) * jax.nn.silu(z)
        return y @ out_proj_w.T + out_proj_b

    def _L3_ffn_ref(x, w_up, w_down):
        import jax, jax.numpy as jnp
        import numpy as np
        EPS = 1e-08

        def _ternary_linear(x, w):
            alpha = jnp.mean(jnp.abs(w))
            w_t = jnp.sign(w) * (jnp.abs(w) > 0.5 * alpha).astype(w.dtype)
            w_q = w + jax.lax.stop_gradient(w_t - w)
            d = x.shape[-1]
            rms = jnp.sqrt(jnp.sum(x * x, axis=-1, keepdims=True)) / jnp.sqrt(jnp.asarray(d, x.dtype))
            x_norm = x / (rms + EPS)
            return jnp.einsum('bsd,fd->bsf', x_norm, w_q)
        h = jax.nn.gelu(_ternary_linear(x, w_up), approximate=False)
        return _ternary_linear(h, w_down)
    x = L0_attn_x
    xn = _layernorm(x, axis=-1)
    s = _L0_attn_ref(xn, L0_attn_Wq, L0_attn_bq, L0_attn_Wk, L0_attn_bk, L0_attn_Wv, L0_attn_bv, L0_attn_Wbeta, L0_attn_bbeta, L0_attn_Wo, L0_attn_bo)
    g = _silu(_L0_ffn_ref(xn, L0_ffn_fast_b, L0_ffn_w_fc, L0_ffn_w_proj, L0_ffn_u, L0_ffn_v, L0_ffn_gate))
    x = x + s * g
    xn = _layernorm(x, axis=-1)
    s = _L1_attn_ref(xn, L1_attn_w_in, L1_attn_w_out, L1_attn_w_gate, L1_attn_b_gate, L1_attn_log_decay, L1_attn_frequency, L1_attn_coupling, L1_attn_w_mlp1, L1_attn_b_mlp1, L1_attn_w_mlp2, L1_attn_b_mlp2, L1_attn_ln1_g, L1_attn_ln1_b, L1_attn_ln2_g, L1_attn_ln2_b)
    g = _silu(_L1_ffn_ref(xn, L1_ffn_router_w, L1_ffn_w1, L1_ffn_w2, L1_ffn_bias))
    x = x + s * g
    xn = _layernorm(x, axis=-1)
    s = _L2_attn_ref(xn, L2_attn_ln1_g, L2_attn_ln1_b, L2_attn_in_proj_w, L2_attn_conv_w, L2_attn_conv_b, L2_attn_x_proj_w, L2_attn_dt_proj_w, L2_attn_dt_proj_b, L2_attn_A_log, L2_attn_D_skip, L2_attn_out_proj_w, L2_attn_ln2_g, L2_attn_ln2_b, L2_attn_q_w, L2_attn_k_w, L2_attn_v_w, L2_attn_o_w, L2_attn_ln3_g, L2_attn_ln3_b, L2_attn_w1, L2_attn_w2, L2_attn_w3)
    g = _silu(_L2_ffn_ref(xn, L2_ffn_W_proj, L2_ffn_b_proj, L2_ffn_W_gate, L2_ffn_W1, L2_ffn_b1, L2_ffn_ln1_g, L2_ffn_ln1_b, L2_ffn_W2, L2_ffn_b2, L2_ffn_ln_g, L2_ffn_ln_b))
    x = x + s * g
    xn = _layernorm(x, axis=-1)
    s = _L3_attn_ref(xn, L3_attn_in_proj_w, L3_attn_in_proj_b, L3_attn_conv_w, L3_attn_conv_b, L3_attn_A_log, L3_attn_D, L3_attn_x_proj_w, L3_attn_dt_proj_w, L3_attn_dt_proj_b, L3_attn_out_proj_w, L3_attn_out_proj_b)
    g = _silu(_L3_ffn_ref(xn, L3_ffn_w_up, L3_ffn_w_down))
    x = x + s * g
    return x

_drawn_inputs = setup_inputs


def setup_inputs(seed=0):
    import zlib

    import numpy as np

    out = dict(_drawn_inputs(seed))
    spreads = {'L0_attn_bq': (0.0, 0.429),
     'L0_attn_bk': (0.0, 0.324),
     'L0_attn_bv': (0.0, 0.363),
     'L0_attn_bbeta': (0.0, 0.599),
     'L0_attn_bo': (0.0, 0.698),
     'L1_attn_b_gate': (-2.0, 0.2),
     'L1_attn_b_mlp1': (0.0, 0.1),
     'L1_attn_b_mlp2': (0.0, 0.1),
     'L1_attn_ln1_g': (1.0, 0.2),
     'L1_attn_ln1_b': (0.0, 0.337),
     'L1_attn_ln2_g': (1.0, 0.2),
     'L1_attn_ln2_b': (0.0, 0.1),
     'L1_ffn_bias': (0.0, 0.1),
     'L2_attn_ln1_g': (1.0, 0.6),
     'L2_attn_ln1_b': (0.0, 0.8),
     'L2_attn_conv_b': (0.0, 0.8),
     'L2_attn_dt_proj_b': (0.0, 0.8),
     'L2_attn_D_skip': (1.0, 0.6),
     'L2_attn_ln2_g': (1.0, 0.6),
     'L2_attn_ln2_b': (0.0, 0.8),
     'L2_attn_ln3_g': (1.0, 0.6),
     'L2_attn_ln3_b': (0.0, 0.8),
     'L2_ffn_b_proj': (0.0, 0.1),
     'L2_ffn_b1': (0.0, 0.1),
     'L2_ffn_ln1_g': (1.0, 0.2),
     'L2_ffn_ln1_b': (0.0, 0.1),
     'L2_ffn_b2': (0.0, 0.1),
     'L2_ffn_ln_g': (1.0, 0.2),
     'L2_ffn_ln_b': (0.0, 0.1),
     'L3_attn_in_proj_b': (0.0, 0.337),
     'L3_attn_conv_b': (0.0, 0.1),
     'L3_attn_D': (1.0, 0.537),
     'L3_attn_out_proj_b': (0.0, 0.1)}
    factors = {'L0_ffn_fast_b': 8.0,
     'L0_ffn_u': 8.0,
     'L0_ffn_v': 8.0,
     'L2_attn_in_proj_w': 8.0,
     'L2_attn_conv_w': 8.0,
     'L2_attn_x_proj_w': 8.0,
     'L2_attn_dt_proj_w': 8.0,
     'L2_attn_A_log': 8.0,
     'L2_attn_out_proj_w': 8.0,
     'L2_attn_q_w': 8.0,
     'L2_attn_k_w': 8.0,
     'L2_attn_v_w': 8.0,
     'L2_attn_o_w': 8.0,
     'L2_attn_w1': 8.0,
     'L2_attn_w2': 8.0,
     'L2_attn_w3': 8.0,
     'L3_attn_A_log': 8.0,
     'L3_attn_x_proj_w': 8.0,
     'L3_attn_dt_proj_w': 8.0,
     'L3_attn_dt_proj_b': 8.0}
    for name, (base, spread) in spreads.items():
        noise = np.random.default_rng([zlib.crc32(name.encode()), seed]).standard_normal(out[name].shape)
        drawn = base * np.exp(spread * noise) if base else spread * noise
        out[name] = jnp.asarray(drawn.astype(out[name].dtype))
    for name, factor in factors.items():
        out[name] = (out[name] * factor).astype(out[name].dtype)
    return out
```

```python
from contextlib import ExitStack, contextmanager

import concourse.bass as bass
from concourse import mybir

F32 = mybir.dt.float32
BF16 = mybir.dt.bfloat16
ALU = mybir.AluOpType
ACT = mybir.ActivationFunctionType
AX = mybir.AxisListType.X

P = 128
B, T = 32, 256
N = B * T
TILE = 512
NT = N // TILE
U = 4
EPS = 1e-5


@contextmanager
def phase(nc, names):
    stage = nc.next_id()
    sems = [nc.alloc_semaphore(f"{n}_{stage}") for n in names.split()]
    with nc.Block() as block:
        yield (block, *sems)
    nc.clear_and_free_semaphores(sems)
    nc.all_engine_barrier()


class Chain:

    def __init__(self, eng, sem, start=0):
        self.eng, self.sem, self.start, self.n = eng, sem, start, 0

    def then(self, ins):
        ins.then_inc(self.sem, 1)
        self.n += 1
        self.eng.wait_ge(self.sem, self.start + self.n)


def tile(i):
    return bass.ds(i * TILE, TILE)

def layernorm(nc, tag, src, dst, const, gain=None, shift=None, rms=None):
    with ExitStack() as ctx:
        cen = ctx.enter_context(nc.psum_tensor(tag + "_cen", [P, U, TILE], F32))
        var = ctx.enter_context(nc.psum_tensor(tag + "_var", [P, 2, TILE], F32))
        sq = ctx.enter_context(nc.sbuf_tensor(tag + "_sq", [P, 2, TILE], F32))
        lg = ctx.enter_context(nc.sbuf_tensor(tag + "_lg", [P, 2, TILE], F32))
        ri = ctx.enter_context(nc.sbuf_tensor(tag + "_ri", [P, 2, TILE], F32))
        block, centred, squared, var_ready, log_ready, ri_ready, chain, normed = ctx.enter_context(
            phase(nc, "centred squared var_ready log_ready ri_ready chain normed"))

        @block.tensor
        def _(pe):
            with pe.Fori(0, NT // U) as i:
                for g in range(0, U, 2):
                    for j in (g, g + 1):
                        pe.wait_ge(normed, i * U + j + 1)
                        nc.tensor.matmul(cen[:, j], const["centre"], src[:, tile(i * U + j)],
                                         start=True, stop=True).then_inc(centred, 1)
                    for j in (g, g + 1):
                        pe.wait_ge(squared, i * U + j + 1)
                        pe.wait_ge(log_ready, i * U + j + 1)
                        nc.tensor.matmul(var[:, j % 2], const["mean"], sq[:, j % 2],
                                         start=True, stop=True).then_inc(var_ready, 1)

        @block.scalar
        def _(act):
            act.sem_inc(log_ready, 2)
            with act.Fori(0, NT // U) as i:
                for g in range(0, U, 2):
                    for j in (g, g + 1):
                        act.wait_ge(centred, i * U + j + 1)
                        act.wait_ge(log_ready, i * U + j + 1)
                        nc.scalar.activation(sq[:, j % 2], cen[:, j], ACT.Square).then_inc(squared, 1)
                    for j in (g, g + 1):
                        act.wait_ge(var_ready, i * U + j + 1)
                        nc.scalar.activation(lg[:, j % 2], var[:, j % 2], ACT.Ln,
                                             bias=const["eps_col"]).then_inc(log_ready, 1)
                    for j in (g, g + 1):
                        act.wait_ge(log_ready, i * U + j + 3)
                        act.wait_ge(normed, i * U + j + U - 1)
                        nc.scalar.activation(ri[:, j % 2], lg[:, j % 2], ACT.Exp, scale=-0.5).then_inc(ri_ready, 1)

        @block.vector
        def _(dve):
            dve.sem_inc(normed, U)
            with dve.Fori(0, NT // U) as i:
                ch = Chain(dve, chain, i * U)
                for j in range(U):
                    dve.wait_ge(ri_ready, i * U + j + 1)
                    out = dst(i * U + j) if callable(dst) else dst[:, tile(i * U + j)]
                    two = (lambda ap: ap.rearrange("p (r t) -> p r t", t=T)) if callable(dst) else (lambda ap: ap)
                    last = nc.vector.tensor_tensor(out, two(cen[:, j]), two(ri[:, j % 2]), ALU.mult)
                    if gain is not None:
                        ch.then(last)
                        last = nc.vector.tensor_scalar(out, out, gain, shift, ALU.mult, ALU.add)
                    last.then_inc(normed, 1)


def load(nc, name, pairs):
    with phase(nc, name) as (block, loaded):
        @block.sync
        def _(sp):
            for dst, src in pairs:
                sp.dma_start(dst, src).then_inc(loaded, 16)
            sp.wait_ge(loaded, 16 * len(pairs))


@contextmanager
def weights(nc, groups, name, w):
    src, cols = groups[name]
    with nc.sbuf_tensor(f"w_{name}_{nc.next_id()}", [P, src.shape[1]], F32) as sb:
        load(nc, name + "_loaded", [(sb[:], src)])
        yield {**w, **{k: sb[:, a:b] for k, (a, b) in cols.items()}}



H0, D0 = 16, 8
HL = 4
STEPS = TILE // B
HD = HL * D0
ST = HL * D0 * D0
NS = 4


def delta_rule(nc, w, xn, s):
    with ExitStack() as ctx:
        def sb(name, shape):
            return ctx.enter_context(nc.sbuf_tensor(name, shape, F32))

        proj = ctx.enter_context(nc.psum_tensor("proj", [P, 4, TILE], F32))
        oproj = ctx.enter_context(nc.psum_tensor("oproj", [P, TILE], F32))
        fm = sb("fm", [P, 4, TILE])
        tm = sb("tm", [P, 4, TILE])
        q, k, v, beta = (tm[:, n].rearrange("p (t h d) -> p t h d", h=HL, d=D0) for n in range(4))
        beta = tm[:, 3].rearrange("p (t c) -> p t c", c=HD)[:, :, 0:HL]
        sqk = sb("sqk", [P, STEPS * HL, D0])
        nrm = sb("nrm", [P, STEPS * HL])
        kb = sb("kb", [P, STEPS, HL, D0])
        vb = sb("vb", [P, STEPS, HL, D0])
        state = sb("state", [P, NS, HL, D0, D0])
        prod = sb("prod", [P, HL * D0, D0])
        outer = sb("outer", [P, HL, D0, D0])
        pred = sb("pred", [P, HL * D0])
        upd = sb("upd", [P, HL, D0])
        sq_q = sb("sq_q", [P, STEPS, HL * D0, D0])
        o_tm = sb("o_tm", [P, TILE])
        o_fm = sb("o_fm", [P, TILE])
        (block, projected, evacuated, turned, norm2, norm1, prepared, chain, state_ready, sq_ready, o_ready,
         o_projected, s_ready) = ctx.enter_context(phase(
             nc, "projected evacuated turned norm2 norm1 prepared chain state_ready sq_ready o_ready "
             "o_projected s_ready"))

        @block.tensor
        def _(pe):
            with pe.Fori(0, NT) as i:
                for n, name in enumerate(("Wq", "Wk", "Wv", "Wbeta")):
                    pe.wait_ge(evacuated, i * 4 + n + 1)
                    nc.tensor.matmul(proj[:, n], w[name], xn[:, tile(i)], start=True, stop=True).then_inc(projected, 1)
                pe.wait_ge(o_ready, i + 1)
                pe.wait_ge(s_ready, i + 1)
                nc.tensor.matmul(oproj[:], w["Wo"], o_fm[:], start=True, stop=True).then_inc(o_projected, 1)

        @block.scalar
        def _(act):
            act.sem_inc(evacuated, 4)
            act.sem_inc(s_ready, 1)
            with act.Fori(0, NT) as i:
                act.wait_ge(turned, i + 1)
                for n, name in enumerate(("bq", "bk", "bv", "bbeta")):
                    act.wait_ge(projected, i * 4 + n + 1)
                    nc.scalar.activation(fm[:, n], proj[:, n], ACT.Identity if n < 3 else ACT.Sigmoid,
                                         bias=w[name]).then_inc(evacuated, 1)
                act.wait_ge(norm2, i + 1)
                nc.scalar.activation(nrm[:], nrm[:], ACT.Sqrt).then_inc(norm1, 1)
                act.wait_ge(o_projected, i + 1)
                nc.scalar.activation(s[:, tile(i)], oproj[:], ACT.Identity, bias=w["bo"]).then_inc(s_ready, 1)

        @block.gpsimd
        def _(pool):
            pool.sem_inc(sq_ready, NS)
            with pool.Fori(0, NT) as i:
                pool.wait_ge(o_ready, i)
                for t in range(STEPS):
                    pool.wait_ge(state_ready, i * STEPS + t + 2)
                    nc.gpsimd.tensor_tensor(
                        sq_q[:, t].rearrange("p (h d) e -> p h d e", h=HL), state[:, (t + 1) % NS],
                        q[:, t].unsqueeze(2).broadcast_to([P, HL, D0, D0]), ALU.mult).then_inc(sq_ready, 1)

        @block.vector
        def _(dve):
            dve.sem_inc(turned, 1)
            nc.vector.memset(state[:, 0], 0.0).then_inc(state_ready, 1)
            dve.wait_ge(state_ready, 1)
            links = 6 + 4 * STEPS + 1
            with dve.Fori(0, NT) as i:
                ch = Chain(dve, chain, i * links)
                dve.wait_ge(evacuated, i * 4 + 8)
                dve.wait_ge(sq_ready, i * STEPS + NS)
                ins = nc.vector.transpose(tm[:].rearrange("p n c -> p (n c)"), fm[:].rearrange("p n c -> p (n c)"))
                ins.then_inc(turned, 1)
                dve.wait_ge(turned, i + 2)
                kk = k.rearrange("p t h d -> p (t h) d")
                ch.then(nc.vector.tensor_tensor(sqk[:], kk, kk, ALU.mult))
                nc.vector.tensor_reduce(nrm[:], sqk[:], AX, ALU.add).then_inc(norm2, 1)
                nc.vector.tensor_tensor(vb[:], v, beta.unsqueeze(3).broadcast_to([P, STEPS, HL, D0]),
                                        ALU.mult).then_inc(prepared, 1)
                dve.wait_ge(norm1, i + 1)
                ch.then(nc.vector.tensor_scalar_add(nrm[:], nrm[:], 1e-6))
                ch.then(nc.vector.reciprocal(nrm[:], nrm[:]))
                ch.then(nc.vector.tensor_tensor(kk, kk, nrm[:].unsqueeze(2).broadcast_to([P, STEPS * HL, D0]),
                                                ALU.mult))
                ch.then(nc.vector.tensor_tensor(kb[:], k, beta.unsqueeze(3).broadcast_to([P, STEPS, HL, D0]),
                                                ALU.mult))
                dve.wait_ge(prepared, i + 1)
                for t in range(STEPS):
                    old, new = state[:, t % NS], state[:, (t + 1) % NS]
                    ch.then(nc.vector.tensor_tensor(
                        prod[:].rearrange("p (h d) e -> p h d e", h=HL), old,
                        kb[:, t].unsqueeze(2).broadcast_to([P, HL, D0, D0]), ALU.mult))
                    ch.then(nc.vector.tensor_reduce(pred[:], prod[:], AX, ALU.add))
                    ch.then(nc.vector.tensor_tensor(upd[:].rearrange("p h d -> p (h d)"),
                                                    vb[:, t].rearrange("p h d -> p (h d)"), pred[:], ALU.subtract))
                    ch.then(nc.vector.tensor_tensor(
                        outer[:], upd[:].unsqueeze(3).broadcast_to([P, HL, D0, D0]),
                        k[:, t].unsqueeze(2).broadcast_to([P, HL, D0, D0]), ALU.mult))
                    dve.wait_ge(sq_ready, i * STEPS + t + 1)
                    nc.vector.tensor_tensor(new, old, outer[:], ALU.add).then_inc(state_ready, 1)
                    dve.wait_ge(state_ready, i * STEPS + t + 2)
                dve.wait_ge(sq_ready, (i + 1) * STEPS + NS)
                ch.then(nc.vector.tensor_reduce(o_tm[:], sq_q[:].rearrange("p t h e -> p (t h) e"), AX, ALU.add))
                dve.wait_ge(o_projected, i)
                ch.then(nc.vector.transpose(o_fm[:], o_tm[:]))
                dve.sem_inc(o_ready, 1)


def ternary_weights(nc, w, wfc_t, wproj_t):
    with ExitStack() as ctx:
        def sb(name, shape):
            return ctx.enter_context(nc.sbuf_tensor(name, shape, F32))

        fcs = w["w_fc"].rearrange("p (m c) -> p m c", m=4)
        neg = sb("tw_neg", [P, 4, P])
        pos = sb("tw_pos", [P, 4, P])
        sc = sb("tw_sc", [P, 3, 4])
        fbv = sb("tw_fbv", [16, P])
        pst = ctx.enter_context(nc.psum_tensor("tw_pst", [P, 4, P], F32))
        psl = ctx.enter_context(nc.psum_tensor("tw_psl", [P, TILE], F32))
        block, chain, fc_ready, fc_turned, low1, low1s, low2, fc_done, proj_ready, proj_turned = ctx.enter_context(
            phase(nc, "chain fc_ready fc_turned low1 low1s low2 fc_done proj_ready proj_turned"))

        @block.vector
        def _(dve):
            ch = Chain(dve, chain)
            dve.wait_ge(low1, 1)
            nc.vector.tensor_copy(fbv[:], psl[0:16, 0:P]).then_inc(low1s, 1)

            def rows(src, blocks, cols):
                p, n = (x[:].rearrange("p m c -> p (m c)").rearrange("p (m c) -> p m c", m=blocks)
                           for x in (pos, neg))
                mean, half, nhalf = (sc[:, n, 0:blocks] for n in range(3))
                ch.then(nc.vector.tensor_reduce(mean, src, AX, ALU.add, apply_absolute_value=True))
                ch.then(nc.vector.tensor_scalar(mean, mean, 1.0 / cols, EPS, ALU.mult, ALU.max))
                ch.then(nc.vector.tensor_scalar(half, mean, 0.5, None, ALU.mult))
                ch.then(nc.vector.tensor_scalar(nhalf, mean, -0.5, None, ALU.mult))
                for m in range(blocks):
                    ch.then(nc.vector.tensor_scalar(p[:, m], src[:, m], sc[:, 1, m:m + 1], sc[:, 0, m:m + 1],
                                                    ALU.is_gt, ALU.mult))
                    ch.then(nc.vector.tensor_scalar(n[:, m], src[:, m], sc[:, 2, m:m + 1], sc[:, 0, m:m + 1],
                                                    ALU.is_lt, ALU.mult))
                ch.then(nc.vector.tensor_tensor(p, p, n, ALU.subtract))

            rows(fcs, 4, P)
            dve.sem_inc(fc_ready, 1)
            dve.wait_ge(fc_turned, 1)
            ch.then(nc.vector.tensor_copy(wfc_t, pst[:].rearrange("p m c -> p (m c)")))
            dve.wait_ge(low2, 1)
            ch.then(nc.vector.scalar_tensor_tensor(out=wfc_t, in0=psl[:], scalar=w["gate"], in1=wfc_t,
                                                   op0=ALU.mult, op1=ALU.add))
            rows(w["w_proj"].rearrange("p (m c) -> p m c", m=1), 1, 512)
            dve.sem_inc(proj_ready, 1)
            dve.wait_ge(proj_turned, 1)
            ch.then(nc.vector.tensor_copy(wproj_t, pst[:]))

        @block.tensor
        def _(pe):
            nc.tensor.matmul(psl[0:16, 0:P], w["fast_bT"][0:16], w["v"][0:16], start=True, stop=True).then_inc(low1, 1)
            pe.wait_ge(low1s, 1)
            nc.tensor.matmul(psl[:], fbv[:], w["uT"][0:16], start=True, stop=True).then_inc(low2, 1)
            for ready, turned in ((fc_ready, fc_turned), (proj_ready, proj_turned)):
                pe.wait_ge(ready, 1)
                for m in range(4):
                    last = nc.tensor.transpose(pst[:, m], pos[:, m], w["eye"])
                last.then_inc(turned, 1)


LAG = 3


def ffn0(nc, w, wfc_t, wproj_t, xn, s, x, x_out):
    M = 4
    with ExitStack() as ctx:
        def sb(name, shape):
            return ctx.enter_context(nc.sbuf_tensor(name, shape, F32))

        up = ctx.enter_context(nc.psum_tensor("f0_up", [P, 4, TILE], F32))
        down = ctx.enter_context(nc.psum_tensor("f0_down", [P, 2, TILE], F32))
        r = sb("f0_r", [P, 4, TILE])
        r2 = sb("f0_r2", [P, 4, TILE])
        g = sb("f0_g", [P, 2, TILE])
        block, h_ready, relu_ready, r2_ready, y_ready, g_ready, chain, done = ctx.enter_context(
            phase(nc, "h_ready relu_ready r2_ready y_ready g_ready chain done"))
        K = U * M

        @block.tensor
        def _(pe):
            with pe.Fori(0, NT // U) as i:
                for n in range(K + LAG):
                    if n < K:
                        pe.wait_ge(relu_ready, i * K + n + 1)
                        nc.tensor.matmul(up[:, n % 4], wfc_t[:, (n % M) * P:(n % M + 1) * P], xn[:, tile(i * U + n // M)],
                                         start=True, stop=True).then_inc(h_ready, 1)
                    m = n - LAG
                    if m >= 0:
                        pe.wait_ge(r2_ready, i * K + m + 5)
                        if m % M == 0:
                            pe.wait_ge(g_ready, i * U + m // M + 1)
                        mm = nc.tensor.matmul(down[:, m // M % 2], wproj_t[:, m % M], r2[:, m % 4],
                                              start=m % M == 0, stop=m % M == M - 1)
                        mm.then_inc(y_ready, 1)

        @block.scalar
        def _(act):
            act.sem_inc(relu_ready, 4)
            act.sem_inc(g_ready, 2)
            with act.Fori(0, NT // U) as i:
                for n in range(K + M + 1):
                    if n < K:
                        act.wait_ge(h_ready, i * K + n + 1)
                        act.wait_ge(r2_ready, i * K + n + 1)
                        nc.scalar.activation(r[:, n % 4], up[:, n % 4], ACT.Relu).then_inc(relu_ready, 1)
                    if n > M and n % M == 0 or n == K + M:
                        j = n // M - 2 if n < K + M else U - 1
                        if n == K:
                            j = U - 2
                        act.wait_ge(y_ready, (i * U + j + 1) * M)
                        act.wait_ge(done, i * U + j + 1)
                        nc.scalar.activation(g[:, j % 2], down[:, j % 2], ACT.Silu).then_inc(g_ready, 1)

        @block.vector
        def _(dve):
            dve.sem_inc(r2_ready, 4)
            dve.sem_inc(done, 2)
            with dve.Fori(0, NT // U) as i:
                for n in range(K + M + 1):
                    if n < K:
                        dve.wait_ge(relu_ready, i * K + n + 5)
                        dve.wait_ge(y_ready, i * K + n - 3) if n >= 4 else dve.wait_ge(y_ready, i * K)
                        nc.vector.tensor_tensor(r2[:, n % 4], r[:, n % 4], r[:, n % 4], ALU.mult).then_inc(r2_ready, 1)
                    if n > M and n % M == 0 or n == K + M:
                        j = n // M - 2 if n < K + M else U - 1
                        ch = Chain(dve, chain, i * U + j)
                        dve.wait_ge(g_ready, i * U + j + 3)
                        at = tile(i * U + j)
                        ch.then(nc.vector.tensor_tensor(g[:, j % 2], g[:, j % 2], s[:, at], ALU.mult))
                        nc.vector.tensor_tensor(
                            x_out.rearrange("p (b t) -> p t b", b=B)[:, bass.ds((i * U + j) * STEPS, STEPS), :],
                            g[:, j % 2].rearrange("p (t b) -> p t b", b=B),
                            x[:, at].rearrange("p (t b) -> p t b", b=B), ALU.add).then_inc(done, 1)


def layer0(nc, w0, groups, x, xn, s, x_out):
    layernorm(nc, "ln0", x, xn, w0)
    with weights(nc, groups, "l0", w0) as w:
        delta_rule(nc, w, xn, s)
        with ExitStack() as ctx:
            wfc_t = ctx.enter_context(nc.sbuf_tensor("wfc_t", [P, 512], F32))
            wproj_t = ctx.enter_context(nc.sbuf_tensor("wproj_t", [P, 4, P], F32))
            ternary_weights(nc, w, wfc_t[:], wproj_t[:])
            ffn0(nc, w, wfc_t[:], wproj_t[:], xn, s, x, x_out)


class Marks:

    def __init__(self, eng, sem, start=0):
        self.eng, self.sem, self.start, self.n, self.at = eng, sem, start, 0, {}

    def mark(self, name, ins):
        ins.then_inc(self.sem, 1)
        self.n += 1
        self.at[name] = self.n

    def need(self, name):
        self.eng.wait_ge(self.sem, self.start + self.at[name])



CH = 64
KEIG = 64
TWO_PI_HI, TWO_PI_LO = 6.28125, 0.0019353071795864769
ROUND = 1.5 * 2 ** 23


def eigen_tables(nc, w, cos_t, sin_t, decay, wa, wb):
    with ExitStack() as ctx:
        def sb(name, shape):
            return ctx.enter_context(nc.sbuf_tensor(name, shape, F32))

        ph, tn, hs = sb("et_ph", [P, CH]), sb("et_tn", [P, CH]), sb("et_hs", [P, CH])
        mag = sb("et_mag", [P, 1])
        ps = ctx.enter_context(nc.psum_tensor("et_ps", [P, 2, P], F32))
        block, chain, folded, phase_ready, half_ready, mag_ready = ctx.enter_context(
            phase(nc, "chain folded phase_ready half_ready mag_ready"))

        @block.tensor
        def _(pe):
            nc.tensor.matmul(ps[:, 0], w["couple"], w["w_outT"], start=True, stop=True).then_inc(folded, 1)
            nc.tensor.matmul(ps[:, 1], w["couple_sw"], w["w_outT"], start=True, stop=True).then_inc(folded, 1)

        @block.vector
        def _(dve):
            ch = Chain(dve, chain)
            dve.wait_ge(folded, 2)
            ch.then(nc.vector.tensor_copy(wa, ps[:, 0]))
            ch.then(nc.vector.tensor_copy(wb, ps[:, 1]))
            ch.then(nc.vector.tensor_scalar(ph[:], w["steps"], w["frequency"], None, ALU.mult))
            ch.then(nc.vector.tensor_scalar(tn[:], ph[:], 0.15915494309189535, ROUND, ALU.mult, ALU.add))
            ch.then(nc.vector.tensor_scalar(tn[:], tn[:], ROUND, None, ALU.subtract))
            ch.then(nc.vector.scalar_tensor_tensor(out=ph[:], in0=tn[:], scalar=-TWO_PI_HI, in1=ph[:],
                                                   op0=ALU.mult, op1=ALU.add))
            ch.then(nc.vector.scalar_tensor_tensor(out=ph[:], in0=tn[:], scalar=-TWO_PI_LO, in1=ph[:],
                                                   op0=ALU.mult, op1=ALU.add))
            ch.then(nc.vector.tensor_scalar(ph[:], ph[:], 3.1415925, -3.1415925, ALU.min, ALU.max))
            dve.sem_inc(phase_ready, 1)
            dve.wait_ge(half_ready, 2)
            ch.then(nc.vector.tensor_tensor(tn[:], hs[:], hs[:], ALU.mult))
            ch.then(nc.vector.tensor_scalar(cos_t, tn[:], -2.0, 1.0, ALU.mult, ALU.add))
            ch.then(nc.vector.tensor_scalar(sin_t, sin_t, w["sign"], None, ALU.mult))
            dve.wait_ge(mag_ready, 1)
            ch.then(nc.vector.tensor_scalar(decay, w["inner"], mag[:], None, ALU.mult))

        @block.scalar
        def _(act):
            nc.scalar.activation(mag[:], w["log_decay"], ACT.Sigmoid).then_inc(mag_ready, 1)
            act.wait_ge(phase_ready, 1)
            nc.scalar.activation(sin_t, ph[:], ACT.Sin).then_inc(half_ready, 1)
            nc.scalar.activation(hs[:], ph[:], ACT.Sin, scale=0.5).then_inc(half_ready, 1)


def eigen_mixer(nc, w, xnn, xn, x1, cos_t, sin_t, decay, wa, wb):
    G = 2
    with ExitStack() as ctx:
        def sb(name, shape):
            return ctx.enter_context(nc.sbuf_tensor(name, shape, F32))

        ps_in = ctx.enter_context(nc.psum_tensor("em_in", [P, G, 3, TILE], F32))
        ps_h = ctx.enter_context(nc.psum_tensor("em_h", [P, G, TILE], F32))
        ta, tb = sb("em_ta", [P, G, TILE]), sb("em_tb", [P, G, TILE])
        z = sb("em_z", [P, G, TILE])
        zc, zs = sb("em_zc", [P, G, TILE]), sb("em_zs", [P, G, TILE])
        gate = sb("em_gate", [P, G, TILE])
        block, in_ready, beta_used, gate_ready, z_ready, h_ready, chain, done = ctx.enter_context(
            phase(nc, "in_ready beta_used gate_ready z_ready h_ready chain done"))
        cosb = cos_t.unsqueeze(1).broadcast_to([P, TILE // CH, CH])
        sinb = sin_t.unsqueeze(1).broadcast_to([P, TILE // CH, CH])

        def chunks(ap):
            return ap.rearrange("p (c j) -> p c j", j=CH)

        @block.tensor
        def _(pe):
            with pe.Fori(0, NT // G) as i:
                for j in range(G):
                    pe.wait_ge(beta_used, i * G + j + 1)
                    pe.wait_ge(gate_ready, i * G + j + 1)
                    for n, name in enumerate(("w_inT", "w_inT_sw", "w_gateT")):
                        nc.tensor.matmul(ps_in[:, j, n], w[name], xnn[:, tile(i * G + j)],
                                         start=True, stop=True).then_inc(in_ready, 1)
                for j in range(G):
                    pe.wait_ge(z_ready, i * G + j + 1)
                    pe.wait_ge(done, i * G + j + 1)
                    nc.tensor.matmul(ps_h[:, j], wa, zc[:, j], start=True, stop=False)
                    nc.tensor.matmul(ps_h[:, j], wb, zs[:, j], start=False, stop=True).then_inc(h_ready, 1)

        @block.scalar
        def _(act):
            act.sem_inc(gate_ready, G)
            with act.Fori(0, NT // G) as i:
                for j in range(G):
                    act.wait_ge(in_ready, (i * G + j + 1) * 3)
                    act.wait_ge(done, i * G + j + 1)
                    nc.scalar.activation(gate[:, j], ps_in[:, j, 2], ACT.Sigmoid, bias=w["b_gate"]).then_inc(gate_ready, 1)

        @block.vector
        def _(dve):
            dve.sem_inc(beta_used, G)
            dve.sem_inc(done, G)
            with dve.Fori(0, NT // G) as i:
                m = Marks(dve, chain, i * (G * 7))
                for j in range(G):
                    dve.wait_ge(in_ready, (i * G + j) * 3 + 2)
                    m.mark(("a", j), nc.vector.tensor_tensor(chunks(ta[:, j]), chunks(ps_in[:, j, 0]), cosb, ALU.mult))
                    m.mark(("b", j), nc.vector.tensor_tensor(chunks(tb[:, j]), chunks(ps_in[:, j, 1]), sinb, ALU.mult))
                for j in range(G):
                    m.need(("b", j))
                    m.mark(("r", j), nc.vector.tensor_tensor(ta[:, j], ta[:, j], tb[:, j], ALU.add))
                for j in range(G):
                    m.need(("r", j))
                    m.mark(("z", j), nc.vector.tensor_tensor_scan(z[:, j, ::-1], decay, ta[:, j, ::-1], 0.0,
                                                                  ALU.mult, ALU.add))
                for j in range(G):
                    m.need(("z", j))
                    zv = z[:, j].rearrange("p (r c j) -> p r c j", r=TILE // T, j=CH)
                    bv = ps_in[:, j, 0].rearrange("p (r c j) -> p r c j", r=TILE // T, j=CH)
                    m.mark(("y", j), nc.vector.tensor_tensor(zv[:, :, 1:, 0], zv[:, :, 1:, 0], bv[:, :, :-1, CH - 1],
                                                             ALU.add))
                for j in range(G):
                    m.need(("y", j))
                    dve.sem_inc(beta_used, 1)
                    m.mark(("c", j), nc.vector.tensor_tensor(chunks(zc[:, j]), chunks(z[:, j]), cosb, ALU.mult))
                    nc.vector.tensor_tensor(chunks(zs[:, j]), chunks(z[:, j]), sinb, ALU.mult).then_inc(z_ready, 1)
                for j in range(G):
                    dve.wait_ge(h_ready, i * G + j + 1)
                    dve.wait_ge(gate_ready, i * G + j + G + 1)
                    m.mark(("g", j), nc.vector.tensor_tensor(gate[:, j], gate[:, j], ps_h[:, j], ALU.mult))
                for j in range(G):
                    m.need(("g", j))
                    at = tile(i * G + j)
                    nc.vector.tensor_tensor(x1[:, at], gate[:, j], xn[:, at], ALU.add).then_inc(done, 1)


def silu_mlp(nc, tag, w_up, b_up, w_down, b_down, x_in, x1):
    M = 4
    K = U * M
    with ExitStack() as ctx:
        up = ctx.enter_context(nc.psum_tensor(tag + "_up", [P, 4, TILE], F32))
        down = ctx.enter_context(nc.psum_tensor(tag + "_down", [P, 2, TILE], F32))
        h = ctx.enter_context(nc.sbuf_tensor(tag + "_h", [P, 4, TILE], F32))
        block, up_ready, h_ready, down_ready, done = ctx.enter_context(
            phase(nc, "up_ready h_ready down_ready done"))

        @block.tensor
        def _(pe):
            with pe.Fori(0, NT // U) as i:
                for n in range(K + LAG):
                    if n < K:
                        pe.wait_ge(h_ready, i * K + n + 1)
                        nc.tensor.matmul(up[:, n % 4], w_up[:, (n % M) * P:(n % M + 1) * P], x_in[:, tile(i * U + n // M)],
                                         start=True, stop=True).then_inc(up_ready, 1)
                    m = n - LAG
                    if m >= 0:
                        pe.wait_ge(h_ready, i * K + m + 5)
                        if m % M == 0:
                            pe.wait_ge(done, i * U + m // M + 1)
                        nc.tensor.matmul(down[:, m // M % 2], w_down[:, m % M], h[:, m % 4],
                                         start=m % M == 0, stop=m % M == M - 1).then_inc(down_ready, 1)

        @block.scalar
        def _(act):
            act.sem_inc(h_ready, 4)
            act.sem_inc(down_ready, 4)
            with act.Fori(0, NT // U) as i:
                for n in range(K):
                    act.wait_ge(up_ready, i * K + n + 1)
                    act.wait_ge(down_ready, i * K + n + 1)
                    nc.scalar.activation(h[:, n % 4], up[:, n % 4], ACT.Silu,
                                         bias=b_up[:, n % M:n % M + 1]).then_inc(h_ready, 1)

        @block.vector
        def _(dve):
            dve.sem_inc(done, 2)
            with dve.Fori(0, NT // U) as i:
                for j in range(U):
                    dve.wait_ge(down_ready, (i * U + j + 1) * M + 4)
                    at = tile(i * U + j)
                    nc.vector.scalar_tensor_tensor(out=x1[:, at], in0=down[:, j % 2], scalar=b_down, in1=x1[:, at],
                                                   op0=ALU.add, op1=ALU.add).then_inc(done, 1)


E8 = 8
NBLK = N // P


def route(nc, tag, w, router, x_in, topk, capacity, wt3):
    with ExitStack() as ctx:
        def sb(name, shape, dt=F32):
            return ctx.enter_context(nc.sbuf_tensor(tag + name, shape, dt))

        ps_l = ctx.enter_context(nc.psum_tensor(tag + "_psl", [P, NBLK, E8], F32))
        ps_c = ctx.enter_context(nc.psum_tensor(tag + "_psc", [P, NBLK, E8], F32))
        ps_t = ctx.enter_context(nc.psum_tensor(tag + "_pst", [P, NBLK, E8], F32))
        ps_w = ctx.enter_context(nc.psum_tensor(tag + "_psw", [3 * E8, 2, 8, P], BF16))
        sc = sb("sc", [P, NBLK, E8])
        t1 = sb("t1", [P, NBLK, E8])
        mask = sb("mask", [P, NBLK, E8])
        run = sb("run", [P, NBLK, E8])
        tot = sb("tot", [P, NBLK, E8])
        acc = sb("acc", [P, NBLK, E8])
        mx = sb("mx", [P, NBLK])
        ix = sb("ix", [P, NBLK])
        parts = sb("parts", [P, NBLK, 3 * E8], BF16)
        eyeb = sb("eyeb", [P, P], BF16)
        block, logits, chain, exp_in, exp_done, mask_ready, counted, split, turned, stored = ctx.enter_context(
            phase(nc, "logits chain exp_in exp_done mask_ready counted split turned stored"))

        def over_e(ap):
            return ap.unsqueeze(2).broadcast_to([P, NBLK, E8])

        iota = w["iota8"].unsqueeze(1).broadcast_to([P, NBLK, E8])

        @block.tensor
        def _(pe):
            for b in range(NBLK):
                last = nc.tensor.matmul(ps_l[:, b], x_in[:, b * P:(b + 1) * P], router, start=True, stop=True)
            last.then_inc(logits, 1)
            for k in range(topk):
                pe.wait_ge(mask_ready, k + 1)
                flat = mask[:].rearrange("p b e -> p (b e)")
                nc.tensor.matmul(ps_c[:].rearrange("p b e -> p (b e)"), w["tri"], flat, start=True, stop=True)
                nc.tensor.matmul(ps_t[:].rearrange("p b e -> p (b e)"), w["ones"], flat, start=True, stop=True)\
                    .then_inc(counted, 1)
            pe.wait_ge(split, 1)
            for b in range(NBLK):
                if b % 8 == 0 and b >= 16:
                    pe.wait_ge(stored, b // 8 - 1)
                last = nc.tensor.transpose(ps_w[:, b // 8 % 2, b % 8], parts[:, b], eyeb[:])
                if b % 8 == 7:
                    last.then_inc(turned, 1)

        @block.scalar
        def _(act):
            act.wait_ge(exp_in, 1)
            nc.scalar.activation(sc[:], t1[:], ACT.Exp).then_inc(exp_done, 1)

        @block.vector
        def _(dve):
            ch = Chain(dve, chain)
            V = nc.vector
            ch.then(V.tensor_copy(eyeb[:], w["eye"]))
            dve.wait_ge(logits, 1)
            ch.then(V.tensor_reduce(mx[:], ps_l[:], AX, ALU.max))
            ch.then(V.tensor_tensor(t1[:], ps_l[:], over_e(mx[:]), ALU.subtract))
            dve.sem_inc(exp_in, 1)
            dve.wait_ge(exp_done, 1)
            ch.then(V.tensor_reduce(mx[:], sc[:], AX, ALU.add))
            ch.then(V.reciprocal(mx[:], mx[:]))
            ch.then(V.tensor_tensor(sc[:], sc[:], over_e(mx[:]), ALU.mult))
            for k in range(topk):
                ch.then(V.tensor_reduce(mx[:], sc[:], AX, ALU.max))
                ch.then(V.tensor_tensor(t1[:], sc[:], over_e(mx[:]), ALU.is_equal))
                ch.then(V.tensor_tensor(t1[:], t1[:], iota, ALU.mult))
                ch.then(V.tensor_reduce(ix[:], t1[:], AX, ALU.min))
                ch.then(V.tensor_tensor(mask[:], iota, over_e(ix[:]), ALU.is_equal))
                dve.sem_inc(mask_ready, 1)
                dve.wait_ge(counted, k + 1)
                ch.then(V.tensor_copy(tot[:], ps_t[:]))
                for e in range(E8):
                    ch.then(V.tensor_tensor_scan(run[:, :, e], w["ones"][:, 0:NBLK], tot[:, :, e], 0.0,
                                                 ALU.mult, ALU.add))
                ch.then(V.tensor_tensor(run[:], run[:], tot[:], ALU.subtract))
                ch.then(V.tensor_tensor(run[:], run[:], ps_c[:], ALU.add))
                if topk > 1:
                    ch.then(V.tensor_tensor(t1[:], mask[:], over_e(mx[:]), ALU.mult))
                    wk = t1
                else:
                    wk = mask
                out = acc if k == 0 else t1
                ch.then(V.scalar_tensor_tensor(out=out[:].rearrange("p b e -> p (b e)"),
                                               in0=run[:].rearrange("p b e -> p (b e)"), scalar=float(capacity),
                                               in1=wk[:].rearrange("p b e -> p (b e)"), op0=ALU.is_le, op1=ALU.mult))
                if k:
                    ch.then(V.tensor_tensor(acc[:], acc[:], t1[:], ALU.add))
                if k + 1 < topk:
                    ch.then(V.scalar_tensor_tensor(out=sc[:].rearrange("p b e -> p (b e)"),
                                                   in0=mask[:].rearrange("p b e -> p (b e)"), scalar=-2.0,
                                                   in1=sc[:].rearrange("p b e -> p (b e)"), op0=ALU.mult, op1=ALU.add))
            for n in range(3):
                part = parts[:, :, n * E8:(n + 1) * E8]
                ch.then(V.tensor_copy(part, acc[:]))
                if n < 2:
                    ch.then(V.tensor_tensor(acc[:], acc[:], part, ALU.subtract))
            dve.sem_inc(split, 1)
            for g in range(NBLK // 8):
                dve.wait_ge(turned, g + 1)
                V.tensor_copy(wt3[:, g * 1024:(g + 1) * 1024], ps_w[:, g % 2].rearrange("p b c -> p (b c)"))\
                    .then_inc(stored, 1)


def experts_gelu(nc, w, w1, w2, wt3, x_in, s, x):
    M = 4
    K = E8 * M
    with ExitStack() as ctx:
        def sb(name, shape, dt=F32):
            return ctx.enter_context(nc.sbuf_tensor("xg_" + name, shape, dt))

        up = ctx.enter_context(nc.psum_tensor("xg_up", [P, 4, TILE], F32))
        wbc = ctx.enter_context(nc.psum_tensor("xg_wbc", [P, 2, TILE], F32))
        down = ctx.enter_context(nc.psum_tensor("xg_down", [P, 2, TILE], F32))
        h = sb("h", [P, 4, TILE])
        hw = sb("hw", [P, 4, TILE])
        g = sb("g", [P, TILE])
        sel = sb("sel", [3 * E8, E8, P], BF16)
        (block, sel_ready, up_ready, wbc_ready, gelu_ready, hw_ready, down_ready, g_ready, chain, done) = \
            ctx.enter_context(phase(
                nc, "sel_ready up_ready wbc_ready gelu_ready hw_ready down_ready g_ready chain done"))

        @block.tensor
        def _(pe):
            pe.wait_ge(sel_ready, 1)
            with pe.Fori(0, NT // 2) as ii:
                for half in range(2):
                    i = ii * 2 + half
                    for n in range(K + LAG):
                        if n < K:
                            if n % M == 0:
                                pe.wait_ge(hw_ready, i * K + (max(n // M, 1) - 1) * M + 4)
                            pe.wait_ge(gelu_ready, i * K + n + 1)
                            nc.tensor.matmul(up[:, n % 4], w1[:, n * P:(n + 1) * P], x_in[:, tile(i)],
                                             start=True, stop=True).then_inc(up_ready, 1)
                        if n < K and n % M == 0:
                            e = n // M
                            nc.tensor.matmul(wbc[:, e % 2], sel[:, e], wt3[:, tile(i)], start=True, stop=True)\
                                .then_inc(wbc_ready, 1)
                        m = n - LAG
                        if m >= 0:
                            pe.wait_ge(hw_ready, i * K + m + 5)
                            if m == 0:
                                pe.wait_ge(g_ready, i + 1)
                            nc.tensor.matmul(down[:, half], w2[:, m], hw[:, m % 4],
                                             start=m == 0, stop=m == K - 1).then_inc(down_ready, 1)

        @block.scalar
        def _(act):
            act.sem_inc(gelu_ready, 4)
            act.sem_inc(g_ready, 2)
            with act.Fori(0, NT // 2) as ii:
                for half in range(2):
                    i = ii * 2 + half
                    for n in range(K):
                        act.wait_ge(up_ready, i * K + n + 1)
                        act.wait_ge(hw_ready, i * K + n + 1)
                        nc.scalar.activation(h[:, n % 4], up[:, n % 4], ACT.Gelu_apprx_tanh).then_inc(gelu_ready, 1)
                    act.wait_ge(down_ready, (i + 1) * K + 4)
                    act.wait_ge(done, i + 1)
                    nc.scalar.activation(g[:], down[:, half], ACT.Silu, bias=w["moe_bias"]).then_inc(g_ready, 1)

        @block.vector
        def _(dve):
            nc.vector.tensor_copy(sel[:].rearrange("p e c -> p (e c)"), w["sel3"][0:3 * E8]).then_inc(sel_ready, 1)
            dve.sem_inc(hw_ready, 4)
            dve.sem_inc(down_ready, 4)
            dve.sem_inc(done, 1)
            with dve.Fori(0, NT // 2) as ii:
                for half in range(2):
                    i = ii * 2 + half
                    for n in range(K):
                        dve.wait_ge(gelu_ready, i * K + n + 5)
                        dve.wait_ge(down_ready, i * K + n + 1)
                        if n % M == 0:
                            dve.wait_ge(wbc_ready, i * E8 + n // M + 1)
                        nc.vector.tensor_tensor(hw[:, n % 4], h[:, n % 4], wbc[:, n // M % 2], ALU.mult)\
                            .then_inc(hw_ready, 1)
                    ch = Chain(dve, chain, i)
                    dve.wait_ge(g_ready, i + 3)
                    ch.then(nc.vector.tensor_tensor(g[:], g[:], s[:, tile(i)], ALU.mult))
                    nc.vector.tensor_tensor(x[:, tile(i)], x[:, tile(i)], g[:], ALU.add).then_inc(done, 1)


def layer1(nc, w0, groups, x, xn, s):
    layernorm(nc, "ln1", x, xn, w0)
    with ExitStack() as ctx:
        w = ctx.enter_context(weights(nc, groups, "l1", w0))

        def sb(name, shape, dt=F32):
            return ctx.enter_context(nc.sbuf_tensor("l1_" + name, shape, dt))

        xnn = sb("xnn", [P, N])
        cos_t, sin_t, decay = sb("cos", [P, CH]), sb("sin", [P, CH]), sb("decay", [P, TILE])
        wa, wb = sb("wa", [P, P]), sb("wb", [P, P])
        eigen_tables(nc, w, cos_t[:], sin_t[:], decay[:], wa[:], wb[:])
        layernorm(nc, "ln1a", xn, xnn, w, w["ln1_g"], w["ln1_b"])
        eigen_mixer(nc, w, xnn, xn, s, cos_t[:], sin_t[:], decay[:], wa[:], wb[:])
        layernorm(nc, "ln1b", s, xnn, w, w["ln2_g"], w["ln2_b"])
        silu_mlp(nc, "m1", w["w_mlp1T"], w["b_mlp1"], w["w_mlp2T"].rearrange("p (m c) -> p m c", m=4), w["b_mlp2"],
                 xnn, s)
    with ExitStack() as ctx:
        w = ctx.enter_context(weights(nc, groups, "route", w0))
        w = ctx.enter_context(weights(nc, groups, "experts1", w))
        wt3 = ctx.enter_context(nc.sbuf_tensor("l1_wt3", [3 * E8, N], BF16))
        w2 = w["w2"].rearrange("p (m c) -> p m c", c=P)
        route(nc, "r1", w, w["router"], xn, 2, N // E8, wt3)
        experts_gelu(nc, w, w["w1"], w2, wt3, xn, s, x)



DI = 2 * P
NSTATE = 16
TAPS = 4
PAD = TAPS - 1
TP = T + PAD
RT = TILE // T
SG = 2
GROUPS = NSTATE // SG
RING = 4
UNITS = 2 * GROUPS


def padded(ap):
    return ap[:, 0:B * TP].rearrange("p (b t) -> p b t", t=TP)


def padded_tile(ap, shift=PAD):
    return lambda i: padded(ap)[:, bass.ds(i * RT, RT), shift:shift + T]


def rows(ap):
    return ap.rearrange("p (r t) -> p r t", t=T)


def mamba_weights(nc, w, once, l3, hp, wconv, a_neg, diag_y, diag_d, sel, conv_bias, corr):
    with ExitStack() as ctx:
        raw = ctx.enter_context(nc.sbuf_tensor(f"mw{3 if l3 else 2}_raw", [P, TAPS * DI + 2 * NSTATE * P], F32))
        block, chain, a_exp, ready, raw_ready = ctx.enter_context(phase(nc, "chain a_exp ready raw_ready"))
        safe = ctx.enter_context(nc.sbuf_tensor(f"mw{3 if l3 else 2}_safe", [P, 2, 2 * NSTATE], F32))
        tmp = ctx.enter_context(nc.sbuf_tensor(f"mw{3 if l3 else 2}_tmp", [P, 2 * TAPS], F32))

        @block.sync
        def _(sp):
            sp.dma_start(raw[:], once).then_inc(raw_ready, 16)

        @block.gpsimd
        def _(pool):
            nc.gpsimd.memset(padded(hp)[:, :, 0:PAD], 0.0).then_inc(ready, 1)
            pool.wait_ge(ready, 1)

        @block.scalar
        def _(act):
            nc.scalar.activation(a_neg, w["A_log"], ACT.Exp).then_inc(a_exp, 1)

        @block.vector
        def _(dve):
            V = nc.vector
            ch = Chain(dve, chain)
            dve.wait_ge(raw_ready, 16)
            ch.then(V.tensor_copy(sel.rearrange("p s c -> p (s c)"), raw[:, TAPS * DI:]))
            for k in range(TAPS):
                ch.then(V.tensor_tensor(wconv[:, k], w["in_w"][:, 0:DI], raw[:, k * DI:(k + 1) * DI], ALU.mult))
            for h in range(2):
                ch.then(V.tensor_scalar(diag_d[:, h], w["eye"], w["D"][:, h:h + 1], None, ALU.mult))
            dve.wait_ge(a_exp, 1)
            ch.then(V.tensor_scalar(a_neg, a_neg, -1.0, None, ALU.mult))
            if l3:
                small, inv = safe[:, 0], safe[:, 1]
                ch.then(V.tensor_scalar(small, a_neg, -1e-6, None, ALU.is_gt))
                ch.then(V.tensor_scalar(inv, small, -1.0, 1.0, ALU.mult, ALU.add))
                ch.then(V.tensor_tensor(inv, inv, a_neg, ALU.mult))
                ch.then(V.tensor_tensor(inv, inv, small, ALU.add))
                ch.then(V.reciprocal(inv, inv))
                for n in range(2 * NSTATE):
                    ch.then(V.tensor_scalar(diag_y[:, n], w["eye"], inv[:, n:n + 1], None, ALU.mult))
                for h in range(2):
                    bw = tmp[:, h * TAPS:(h + 1) * TAPS]
                    ch.then(V.tensor_scalar(bw, w["conv_cols"][:, h * TAPS:(h + 1) * TAPS], w["in_b"][:, h:h + 1], None,
                                            ALU.mult))
                    for k in range(1, TAPS):
                        ch.then(V.tensor_tensor(bw[:, k:k + 1], bw[:, k:k + 1], bw[:, k - 1:k], ALU.add))
                    ch.then(V.tensor_tensor(conv_bias[:, h:h + 1], w["conv_b"][:, h:h + 1], bw[:, TAPS - 1:TAPS], ALU.add))
                    for t in range(PAD):
                        ch.then(V.tensor_scalar(corr[:, h, t:t + 1], bw[:, PAD - 1 - t:PAD - t], -1.0, None, ALU.mult))
            else:
                ch.then(V.tensor_copy(conv_bias, w["conv_b"]))


def mamba(nc, w, once, l3, hp, res, out):
    with ExitStack() as ctx:
        def sb(name, shape, dt=F32):
            return ctx.enter_context(nc.sbuf_tensor(("m3_" if l3 else "m2_") + name, shape, dt))

        wconv = sb("wconv", [P, TAPS, DI])
        a_neg = sb("a_neg", [P, 2 * NSTATE])
        diag_y = sb("diag_y", [P, 2 * NSTATE, P]) if l3 else None
        diag_d = sb("diag_d", [P, 2, P])
        sel = sb("sel", [P, 2 * NSTATE, P], BF16)
        conv_bias = sb("conv_bias", [P, 2])
        corr = sb("corr", [P, 2, PAD])
        mamba_weights(nc, w, once, l3, hp, wconv[:], a_neg[:], diag_y, diag_d, sel[:], conv_bias[:], corr)

        ps_b = ctx.enter_context(nc.psum_tensor(f"mb{3 if l3 else 2}_b", [P, SG, TILE], F32))
        ps_c = ctx.enter_context(nc.psum_tensor(f"mb{3 if l3 else 2}_c", [P, SG, TILE], F32))
        ps_y = ctx.enter_context(nc.psum_tensor(f"mb{3 if l3 else 2}_y", [P, 2, TILE], F32))
        ps_w = ctx.enter_context(nc.psum_tensor(f"mb{3 if l3 else 2}_w", [P, 2, TILE], F32))
        xs = sb("xs", [P, 2, 2, TILE])
        sg = sb("sg", [P, 2, 2, TILE])
        dt = sb("dt", [P, 2, 2, TILE])
        dtx = xs if l3 else sb("dtx", [P, 2, 2, TILE])
        bct = sb("bct", [P, 2, TILE], BF16)
        rest = sb("rest", [P, TILE])
        bcf = sb("bcf", [P, TILE])
        low = sb("low", [64, TILE]) if l3 else bcf
        sp = sb("sp", [P, 2, TILE])
        lin = sb("lin", [P, TILE])
        bsb = sb("bsb", [P, 2, SG, TILE])
        csb = sb("csb", [P, 2, SG, TILE])
        da = sb("da", [P, RING, SG, TILE])
        u = sb("u", [P, RING, SG, TILE])
        hs = sb("hs", [P, 2, SG, TILE])
        hc = sb("hc", [P, 2, SG, TILE])
        yg = sb("yg", [P, 2, TILE])
        (block, xs_in, xs_fixed, xs_ready, gate_in, sg_ready, bc_in, bc_split, low_in, bcf_ready, low_ready, dt_in, sp_step,
         sp_ready, dt_ready, dtx_ready, b_ready, c_ready, bsb_ready, csb_ready, da_ready, reset_ready, u_ready, h_ready,
         hc_ready, y_used, made, yg_ready, out_ready, x_done, chain) = ctx.enter_context(phase(
             nc, "xs_in xs_fixed xs_ready gate_in sg_ready bc_in bc_split low_in bcf_ready low_ready dt_in sp_step sp_ready "
             "dt_ready dtx_ready b_ready c_ready bsb_ready csb_ready da_ready reset_ready u_ready h_ready hc_ready y_used "
             "made yg_ready out_ready x_done chain"))
        out_bank = 0 if l3 else 1

        @block.tensor
        def _(pe):
            def stage_a(a, first):
                def conv(h):
                    def run():
                        if not first:
                            if (h == 0) == (not l3):
                                pe.wait_ge(dt_ready, 2 * a)
                            else:
                                pe.wait_ge(x_done, a - 1)
                        for k in range(TAPS):
                            mm = nc.tensor.matmul(ps_w[:, h], wconv[:, k, h * P:(h + 1) * P], padded_tile(hp, k)(a),
                                                  start=k == 0, stop=k == TAPS - 1)
                        mm.then_inc(xs_in, 1)
                    return run

                def gate(h):
                    def run():
                        pe.wait_ge(xs_ready, 2 * a + 1 + h)
                        nc.tensor.matmul(ps_w[:, h], w["in_w"][:, DI + h * P:DI + (h + 1) * P], padded_tile(hp)(a),
                                         start=True, stop=True).then_inc(gate_in, 1)
                    return run

                def project(bank, name, rows_out, sem, par):
                    def run():
                        pe.wait_ge(sg_ready, 2 * a + 1 + bank)
                        for h in range(2):
                            mm = nc.tensor.matmul(ps_w[0:rows_out, bank], w[name][:, h * rows_out:(h + 1) * rows_out],
                                                  xs[:, par, h], start=h == 0, stop=h == 1)
                        mm.then_inc(sem, 1)
                    return run

                def step_size(h):
                    bank = h if l3 else 1 - h
                    K = 64 if l3 else NSTATE

                    def run():
                        pe.wait_ge(low_ready, a + 1)
                        if bank == 1 and not l3:
                            pe.wait_ge(sg_ready, 2 * a + 2)
                        nc.tensor.matmul(ps_w[:, bank], w["dt_w"][0:K, h * P:(h + 1) * P], low[0:K],
                                         start=True, stop=True).then_inc(dt_in, 1)
                    return run
                return conv, gate, project, step_size

            def pieces(a, par, first=False):
                conv, gate, project, step_size = stage_a(a, first)
                third = [project(0, "xp_bc", P, bc_in, par)] + ([project(1, "xp_low", 64, low_in, par)] if l3 else [])
                return {1: [conv(0), conv(1)], 2: [gate(0), gate(1)], 3: third, 5: [step_size(0), step_size(1)]}

            def spread_b(i, par, g):
                pe.wait_ge(bc_split, i + 1)
                pe.wait_ge(bsb_ready, i * GROUPS + g)
                for s in range(SG):
                    mm = nc.tensor.matmul(ps_b[:, s], sel[:, g * SG + s], bct[:, par], start=True, stop=True)
                mm.then_inc(b_ready, 1)

            def spread_c(i, par, g):
                pe.wait_ge(csb_ready, i * GROUPS + g)
                for s in range(SG):
                    mm = nc.tensor.matmul(ps_c[:, s], sel[:, NSTATE + g * SG + s], bct[:, par], start=True, stop=True)
                mm.then_inc(c_ready, 1)

            def spread(i, par, g):
                spread_b(i, par, g)
                spread_c(i, par, g)

            def sum_states(i, par, g, h):
                pe.wait_ge(hc_ready, i * UNITS + g * 2 + h + 5)
                for s in range(SG):
                    weight = diag_y[:, h * NSTATE + g * SG + s] if l3 else w["eye"]
                    mm = nc.tensor.matmul(ps_y[:, h], weight, hc[:, h, s], start=False, stop=g == GROUPS - 1 and s == SG - 1)
                mm.then_inc(y_used, 1)

            def project_out(i, before_next):
                pe.wait_ge(yg_ready, 2 * i + 2)
                if before_next:
                    pe.wait_ge(dt_ready, 2 * i + 3)
                else:
                    pe.wait_ge(x_done, i)
                for h in range(2):
                    mm = nc.tensor.matmul(ps_w[:, out_bank], w["out_w"][:, h * P:(h + 1) * P], yg[:, h],
                                          start=h == 0, stop=h == 1)
                mm.then_inc(out_ready, 1)

            def step(i, par, first, more):
                ahead = pieces(i + 1, 1 - par) if more else {}
                for g in range(GROUPS):
                    if g + 2 < GROUPS:
                        spread(i, par, g + 2)
                    elif more:
                        spread(i + 1, 1 - par, g + 2 - GROUPS)
                    if g == 0:
                        if not first:
                            project_out(i - 1, True)
                        for h in range(2):
                            nc.tensor.matmul(ps_y[:, h], diag_d[:, h], xs[:, par, h], start=True, stop=False)
                    sum_states(i, par, g, 0)
                    sum_states(i, par, g, 1)
                    for piece in ahead.get(g, []):
                        piece()

            for group in pieces(0, 0, True).values():
                for piece in group:
                    piece()
            spread(0, 0, 0)
            spread(0, 0, 1)
            step(0, 0, True, True)
            with pe.Fori(0, NT // 2 - 1) as ii:
                step(ii * 2 + 1, 1, False, True)
                step(ii * 2 + 2, 0, False, True)
            step(NT - 1, 1, False, False)
            project_out(NT - 1, False)

        @block.scalar
        def _(act):
            def pieces(a, par):
                def silu_xs(h):
                    def run():
                        act.wait_ge(x_done, a - 1) if not isinstance(a, int) or a > 1 else None
                        act.wait_ge(xs_fixed if l3 else xs_in, 2 * a + 1 + h)
                        nc.scalar.activation(xs[:, par, h], ps_w[:, h], ACT.Silu, bias=conv_bias[:, h:h + 1])\
                            .then_inc(xs_ready, 1)
                    return run

                def silu_gate(h):
                    def run():
                        act.wait_ge(gate_in, 2 * a + 1 + h)
                        nc.scalar.activation(sg[:, par, h], ps_w[:, h], ACT.Silu,
                                             bias=w["in_b"][:, 2 + h:3 + h] if l3 else 0.0).then_inc(sg_ready, 1)
                    return run

                def copy_low():
                    act.wait_ge(bc_split, a)
                    act.wait_ge(dt_in, 2 * a)
                    act.wait_ge(bc_in, a + 1)
                    ins = nc.scalar.copy(bcf[:], ps_w[:, 0])
                    if l3:
                        act.wait_ge(low_in, a + 1)
                        ins.then_inc(bcf_ready, 1)
                        ins = nc.scalar.copy(low[:], ps_w[0:64, 1])
                    ins.then_inc(low_ready, 1)

                def soft():
                    m = Marks(act, sp_step, a * 4)
                    for h in range(2):
                        bank = h if l3 else 1 - h
                        act.wait_ge(dt_in, 2 * a + 1 + h)
                        act.wait_ge(dt_ready, 2 * a)
                        m.mark(("abs", h), nc.scalar.activation(sp[:, h], ps_w[:, bank], ACT.Abs, bias=w["dt_b"][:, h:h + 1]))
                    for h in range(2):
                        m.need(("abs", h))
                        m.mark(("exp", h), nc.scalar.activation(sp[:, h], sp[:, h], ACT.Exp, scale=-1.0))
                    for h in range(2):
                        m.need(("exp", h))
                        nc.scalar.activation(sp[:, h], sp[:, h], ACT.Ln, bias=1.0).then_inc(sp_ready, 1)
                return {2: [silu_xs(0), silu_xs(1)], 3: [silu_gate(0), silu_gate(1)], 4: [copy_low],
                        6: [soft]}

            def copy_b(i, g):
                act.wait_ge(b_ready, i * GROUPS + g + 1)
                act.wait_ge(u_ready, (i * GROUPS + g) * 2)
                nc.scalar.copy(bsb[:, g % 2], ps_b[:]).then_inc(bsb_ready, 1)

            def copy_c(i, g):
                act.wait_ge(c_ready, i * GROUPS + g + 1)
                act.wait_ge(hc_ready, (i * GROUPS + g) * 2 + 2)
                nc.scalar.copy(csb[:, g % 2], ps_c[:]).then_inc(csb_ready, 1)

            def decay(i, par, g, h):
                act.wait_ge(h_ready, i * UNITS + g * 2 + h + 1)
                slot = (g * 2 + h) % RING
                for s in range(SG):
                    n = h * NSTATE + g * SG + s
                    ins = nc.scalar.activation(da[:, slot, s], dt[:, par, h], ACT.Exp, scale=a_neg[:, n:n + 1])
                ins.then_inc(da_ready, 1)

            def step(i, par, more):
                ahead = pieces(i + 1, 1 - par) if more else {}
                act.wait_ge(dt_ready, 2 * i + 2)
                for g in range(GROUPS):
                    decay(i, par, g, 0)
                    if g + 1 < GROUPS:
                        copy_b(i, g + 1)
                    elif more:
                        copy_b(i + 1, 0)
                    copy_c(i, g)
                    decay(i, par, g, 1)
                    for piece in ahead.get(g, []):
                        piece()

            for group in pieces(0, 0).values():
                for piece in group:
                    piece()
            copy_b(0, 0)
            step(0, 0, True)
            with act.Fori(0, NT // 2 - 1) as ii:
                step(ii * 2 + 1, 1, True)
                step(ii * 2 + 2, 0, True)
            step(NT - 1, 1, False)

        @block.gpsimd
        def _(pool):
            pool.sem_inc(u_ready, 2)

            def step(i, par):
                pool.wait_ge(dtx_ready, i + 1)
                for g in range(GROUPS):
                    pool.wait_ge(bsb_ready, i * GROUPS + g + 1)
                    for h in range(2):
                        pool.wait_ge(h_ready, i * UNITS + g * 2 + h + 1)
                        if not l3:
                            pool.wait_ge(da_ready, i * UNITS + g * 2 + h + 1)
                        slot = (g * 2 + h) % RING
                        nc.gpsimd.tensor_tensor(u[:, slot], bsb[:, g % 2],
                                                dtx[:, par, h].unsqueeze(1).broadcast_to([P, SG, TILE]),
                                                ALU.mult).then_inc(u_ready, 1)
                        if not l3:
                            nc.gpsimd.memset(da[:, slot].rearrange("p s (r t) -> p (s r) t", t=T)[:, :, 0:1], 0.0)\
                                .then_inc(reset_ready, 1)

            with pool.Fori(0, NT // 2) as ii:
                step(ii * 2, 0)
                step(ii * 2 + 1, 1)

        @block.vector
        def _(dve):
            V = nc.vector
            dve.sem_inc(h_ready, RING)
            dve.sem_inc(y_used, 2)
            dve.sem_inc(hc_ready, 4)

            def pieces(a, par, m):
                def fix(h):
                    def run():
                        dve.wait_ge(xs_in, 2 * a + 1 + h)
                        at = rows(ps_w[:, h])[:, :, 0:PAD]
                        V.tensor_tensor(at, at, corr[:, h].unsqueeze(1).broadcast_to([P, RT, PAD]), ALU.add)\
                            .then_inc(xs_fixed, 1)
                    return run

                def split():
                    if not isinstance(a, int) or a > 1:
                        dve.wait_ge(x_done, a - 1)
                    dve.wait_ge(bcf_ready if l3 else low_ready, a + 1)
                    m.mark("hi", V.tensor_copy(bct[:, par], bcf[:]))
                    m.need("hi")
                    m.mark("r1", V.tensor_tensor(rest[64:], bcf[64:], bct[64:, par], ALU.subtract))
                    m.need("r1")
                    m.mark("mid", V.tensor_copy(bct[64:, par], rest[64:]))
                    m.need("mid")
                    m.mark("r2", V.tensor_tensor(rest[96:], rest[96:], bct[96:, par], ALU.subtract))
                    m.need("r2")
                    V.tensor_copy(bct[96:, par], rest[96:]).then_inc(bc_split, 1)

                def step_size(h):
                    bank = h if l3 else 1 - h

                    def run():
                        dve.wait_ge(sp_ready, 2 * a + 1 + h)
                        m.mark(("lin", h), V.tensor_scalar(lin[:], ps_w[:, bank], w["dt_b"][:, h:h + 1], 0.0,
                                                           ALU.add, ALU.max))
                        m.need(("lin", h))
                        V.tensor_tensor(dt[:, par, h], lin[:], sp[:, h], ALU.add).then_inc(dt_ready, 1)
                        dve.wait_ge(dt_ready, 2 * a + 1 + h)
                    return run

                def times_x():
                    if l3:
                        dve.sem_inc(dtx_ready, 1)
                        return
                    dve.wait_ge(xs_ready, 2 * a + 2)
                    V.tensor_tensor(dtx[:, par], dt[:, par], xs[:, par], ALU.mult).then_inc(dtx_ready, 1)
                return {1: [fix(0), fix(1)] if l3 else [], 4: [split], 6: [step_size(0), step_size(1), times_x]}

            def flat(ap):
                return ap.rearrange("p s t -> p (s t)")

            def make(i, n):
                q = i * UNITS + n
                dve.wait_ge(da_ready, q + 1)
                dve.wait_ge(u_ready, q + 3)
                V.scalar_tensor_tensor(out=flat(u[:, n % RING]), in0=flat(da[:, n % RING]), scalar=-1.0,
                                       in1=flat(u[:, n % RING]), op0=ALU.add, op1=ALU.mult).then_inc(made, 1)
                dve.wait_ge(made, 2 * q + 1)
                V.memset(da[:, n % RING].rearrange("p s (r t) -> p (s r) t", t=T)[:, :, 0:1], 0.0).then_inc(made, 1)

            def scan(i, n):
                q = i * UNITS + n
                if l3:
                    dve.wait_ge(made, 2 * q + 2)
                else:
                    dve.wait_ge(u_ready, q + 3)
                    dve.wait_ge(reset_ready, q + 1)
                dve.wait_ge(hc_ready, q + 3)
                V.tensor_tensor_scan(flat(hs[:, n % 2]), flat(da[:, n % RING]), flat(u[:, n % RING]), 0.0,
                                     ALU.mult, ALU.add).then_inc(h_ready, 1)

            def times_c(i, n):
                q = i * UNITS + n
                dve.wait_ge(h_ready, q + RING + 1)
                dve.wait_ge(csb_ready, i * GROUPS + n // 2 + 1)
                dve.wait_ge(y_used, q + 1)
                V.tensor_tensor(hc[:, n % 2], hs[:, n % 2], csb[:, n // 2 % 2], ALU.mult).then_inc(hc_ready, 1)

            def gated(i, par):
                dve.wait_ge(out_ready, i)
                dve.wait_ge(y_used, (i + 1) * UNITS + 2)
                for h in range(2):
                    V.tensor_tensor(yg[:, h], ps_y[:, h], sg[:, par, h], ALU.mult).then_inc(yg_ready, 1)

            def finish(i):
                dve.wait_ge(out_ready, i + 1)
                if l3:
                    V.tensor_scalar(out[:, tile(i)], ps_w[:, out_bank], w["out_b"], None, ALU.add).then_inc(x_done, 1)
                else:
                    V.tensor_tensor(out[:, tile(i)], ps_w[:, out_bank], res[:, tile(i)], ALU.add).then_inc(x_done, 1)

            def step(i, par, first, more):
                ahead = pieces(i + 1, 1 - par, Marks(dve, chain, i * 6 + 6)) if more else {}
                for n in range(UNITS):
                    if l3 and n + 1 < UNITS:
                        make(i, n + 1)
                    elif l3 and more:
                        make(i + 1, 0)
                    scan(i, n)
                    if n:
                        times_c(i, n - 1)
                    elif not first:
                        times_c(i - 1, UNITS - 1)
                    if n == 1 and not first:
                        gated(i - 1, 1 - par)
                    if n == 4 and not first:
                        finish(i - 1)
                    if n % 2 == 0 and n:
                        for piece in ahead.get(n // 2 - 1, []):
                            piece()

            for group in pieces(0, 0, Marks(dve, chain, 0)).values():
                for piece in group:
                    piece()
            if l3:
                make(0, 0)
            step(0, 0, True, True)
            with dve.Fori(0, NT // 2 - 1) as ii:
                step(ii * 2 + 1, 1, False, True)
                step(ii * 2 + 2, 0, False, True)
            step(NT - 1, 1, False, False)
            times_c(NT - 1, UNITS - 1)
            gated(NT - 1, 1)
            finish(NT - 1)



NH, NKV, DH = 16, 4, 8
QPK = NH // NKV


def attention_inputs(nc, w, h, q, v_all):
    with ExitStack() as ctx:
        def sb(name, shape):
            return ctx.enter_context(nc.sbuf_tensor("ai_" + name, shape, F32))

        ps = ctx.enter_context(nc.psum_tensor("ai_ps", [P, 4, TILE], F32))
        ps_v = ctx.enter_context(nc.psum_tensor("ai_v", [P, TILE], F32))
        ps_t = ctx.enter_context(nc.psum_tensor("ai_t", [P, 4, P], F32))
        prod = sb("prod", [P, 4, TILE])
        vt = sb("vt", [P, TILE])
        block, in_ready, rotated, added, v_in, v_copied, v_turned, v_done = ctx.enter_context(
            phase(nc, "in_ready rotated added v_in v_copied v_turned v_done"))

        @block.tensor
        def _(pe):
            with pe.Fori(0, NT) as i:
                for n, name in enumerate(("q_w", "q_w_rot", "k_w", "k_w_rot")):
                    pe.wait_ge(rotated, i * 4 + n + 1)
                    nc.tensor.matmul(ps[:, n], w[name], h[:, tile(i)], start=True, stop=True).then_inc(in_ready, 1)
                pe.wait_ge(v_copied, i)
                nc.tensor.matmul(ps_v[:], w["v_w"], h[:, tile(i)], start=True, stop=True).then_inc(v_in, 1)
                pe.wait_ge(v_copied, i + 1)
                pe.wait_ge(v_done, i)
                for b in range(4):
                    mm = nc.tensor.transpose(ps_t[:, b], vt[:, b * P:(b + 1) * P], w["eye"])
                mm.then_inc(v_turned, 1)

        @block.scalar
        def _(act):
            with act.Fori(0, NT) as i:
                act.wait_ge(v_in, i + 1)
                nc.scalar.copy(vt[:], ps_v[:]).then_inc(v_copied, 1)
                act.wait_ge(v_turned, i + 1)
                nc.scalar.copy(v_all[:, bass.ds(i * 4, 4)], ps_t[:, :, 0:NKV * DH]).then_inc(v_done, 1)

        @block.vector
        def _(dve):
            dve.sem_inc(rotated, 4)
            with dve.Fori(0, NT) as i:
                dve.wait_ge(added, i * 2)
                for n, name in enumerate(("q_cos", "q_sin", "k_cos", "k_sin")):
                    dve.wait_ge(in_ready, i * 4 + n + 1)
                    nc.vector.tensor_tensor(rows(prod[:, n]), rows(ps[:, n]),
                                            w[name].unsqueeze(1).broadcast_to([P, RT, T]), ALU.mult).then_inc(rotated, 1)

        @block.gpsimd
        def _(pool):
            with pool.Fori(0, NT) as i:
                pool.wait_ge(rotated, i * 4 + 6)
                nc.gpsimd.tensor_tensor(q[:, tile(i)], prod[:, 0], prod[:, 1], ALU.add).then_inc(added, 1)
                pool.wait_ge(rotated, i * 4 + 8)
                pool.wait_ge(v_in, i + 1)
                nc.gpsimd.tensor_tensor(h[:, tile(i)], prod[:, 2], prod[:, 3], ALU.add).then_inc(added, 1)


def attention(nc, w, q, k, v_all, x):
    G = 4
    BLK = G * RT * 2
    HALVES = NKV * 2
    CU = [(n, g, kb) for n in range(BLK) for g in range(NKV) for kb in range(n % 2 + 1)]
    NU = len(CU)
    first = [min(u for u in range(NU) if CU[u][0] == n) for n in range(BLK)]
    last = [max(u for u in range(NU) if CU[u][0] == n) for n in range(BLK)]
    LAG = 2
    max_at = {}
    for n in range(1, BLK):
        steps = [0, 0, 0, 1, 1, 1, 2, 2] if n % 2 else [0, 1, 2, 3, 3, 4, 4, 5]
        for i, s in enumerate(steps):
            max_at.setdefault(first[n - 1] + s, []).append(n * HALVES + i)
    turn_at = {last[n - 1]: n for n in range(1, BLK)}
    copy_at = {last[n] + LAG: n for n in range(BLK)}
    sums_at = {last[n] + LAG + 1: n for n in range(BLK)}
    out_at = {last[n] + LAG + 6: n // 4 for n in range(3, BLK, 4)}
    spread_at = {first[j * 4 - 2] + c: (j, c) for j in range(1, G) for c in range(QPK)}
    STEPS = max(out_at) + 1
    divide_at = {sums_at_u + c: (n, c) for sums_at_u, n in sums_at.items() for c in range(QPK)}
    with ExitStack() as ctx:
        def sb(name, shape, dt=F32):
            return ctx.enter_context(nc.sbuf_tensor("at_" + name, shape, dt))

        ps_s = ctx.enter_context(nc.psum_tensor("at_ps_s", [P, 2, 2, T], F32))
        ps_t = ctx.enter_context(nc.psum_tensor("at_ps_t", [P, QPK, P], F32))
        ps_c = ctx.enter_context(nc.psum_tensor("at_ps_c", [P, 2, QPK, P], F32))
        ps_v = ctx.enter_context(nc.psum_tensor("at_ps_v", [P, QPK, P], F32))
        ps_x = ctx.enter_context(nc.psum_tensor("at_ps_x", [P, QPK, P], F32))
        ps_w = ctx.enter_context(nc.psum_tensor("at_ps_w", [P, TILE], F32))
        qm = sb("qm", [P, 2, QPK, TILE])
        kt = sb("kt", [P, 2, TILE])
        vt = sb("vt", [P, 2, 4, NKV, P])
        pt = sb("pt", [P, 4, QPK, P])
        mx = sb("mx", [P, QPK, P])
        ov = sb("ov", [P, QPK, P])
        rc = sb("rc", [P, QPK, P])
        on = sb("on", [P, QPK, TILE])
        maskb = sb("maskb", [P, 2, T], BF16)
        eyeb = sb("eyeb", [P, QPK, P], BF16)
        (block, consts, filled, spread_in, qm_ready, kv_ready, s_ready, max_ready, turned, less_max, c_ready, exp_ready, v_ready,
         ov_ready, sums_in, rc_ready, on_ready, out_ready, x_done) = ctx.enter_context(phase(
             nc, "consts filled spread_in qm_ready kv_ready s_ready max_ready turned less_max c_ready exp_ready v_ready "
             "ov_ready sums_in rc_ready on_ready out_ready x_done"))

        def flat(bank):
            return bank.rearrange("p a b -> p (a b)")

        def place(n):
            return n // 4 % 2, n % 4 * P, n % 4 // 2 * T

        @block.tensor
        def _(pe):
            pe.wait_ge(consts, 3)

            def spread(ii, j, c, bank):
                pe.wait_ge(qm_ready, (ii * G + j) * QPK + c)
                nc.tensor.matmul(bank, w["spread"][:, c * P:(c + 1) * P], q[:, tile(ii * G + j)], start=True, stop=True)\
                    .then_inc(spread_in, 1)

            def scores(ii, h):
                n, g, cp = h // HALVES, h % HALVES // 2, h % 2
                slot, col, row = place(n)
                if h % (4 * HALVES) == 0:
                    pe.wait_ge(qm_ready, (ii * G + n // 4 + 1) * QPK)
                    pe.wait_ge(kv_ready, ii * G + n // 4 + 1)
                pe.wait_ge(max_ready, ii * BLK * HALVES + h + 1)
                at, keys = slice(32 * g, 32 * g + 32), (n % 2 + 1) * P
                nc.tensor.matmul(ps_s[:, h % 2, :, 0:keys], eyeb[:, 0], maskb[:, :, T - keys:T], start=True, stop=False)
                for c in range(2):
                    mm = nc.tensor.matmul(ps_s[:, h % 2, c, 0:keys], qm[at, slot, cp * 2 + c, col:col + P],
                                          kt[at, slot, row:row + keys], start=False, stop=c == 1)
                mm.then_inc(s_ready, 1)

            def turn(ii, n):
                pe.wait_ge(max_ready, (ii * BLK + n + 1) * HALVES + 2)
                pe.wait_ge(less_max, ii * BLK + n)
                for c in range(QPK):
                    mm = nc.tensor.transpose(ps_t[:, c], mx[:, c], w["eye"])
                mm.then_inc(turned, 1)

            def scores_t(ii, u):
                n, g, kb = CU[u]
                slot, col, row = place(n)
                if u == first[n]:
                    pe.wait_ge(less_max, ii * BLK + n + 1)
                pe.wait_ge(exp_ready, ii * NU + u + 1)
                at, diagonal = slice(32 * g, 32 * g + 32), kb == n % 2
                mm = nc.tensor.matmul(ps_c[:, u % 2], kt[at, slot, row + kb * P:row + (kb + 1) * P],
                                      qm[at, slot, :, col:col + P], start=True, stop=not diagonal)
                if diagonal:
                    mm = nc.tensor.matmul(ps_c[:, u % 2], maskb[:, 0, P:T], eyeb[:], start=False, stop=True)
                mm.then_inc(c_ready, 1)

            def values(ii, u):
                n, g, kb = CU[u]
                pe.wait_ge(exp_ready, ii * NU + u + 3)
                if u == first[n]:
                    pe.wait_ge(ov_ready, ii * BLK + n + 4)
                nc.tensor.matmul(ps_v[:], vt[:, place(n)[0], n % 4 // 2 * 2 + kb, g], pt[:, u % 4],
                                 start=u == first[n], stop=u == last[n]).then_inc(v_ready, 1)

            def sums(ii, n):
                pe.wait_ge(ov_ready, ii * BLK + n + 5)
                pe.wait_ge(on_ready, ii * BLK + n)
                nc.tensor.matmul(ps_x[:], w["sum_rows"], ov[:], start=True, stop=True).then_inc(sums_in, 1)

            def project(ii, j):
                pe.wait_ge(on_ready, (ii * G + j + 1) * 4)
                pe.wait_ge(x_done, ii * G + j)
                pe.wait_ge(qm_ready, (ii * G + min(j + 2, G)) * QPK)
                for c in range(QPK):
                    mm = nc.tensor.matmul(ps_w[:], w["o_w"][:, c * P:(c + 1) * P], on[:, c],
                                          start=c == 0, stop=c == QPK - 1)
                mm.then_inc(out_ready, 1)

            with pe.Fori(0, NT // G) as ii:
                pe.wait_ge(on_ready, ii * BLK)
                for c, bank in enumerate((flat(ps_c[:, 0]), flat(ps_c[:, 1]), flat(ps_t[:]), flat(ps_x[:]))):
                    spread(ii, 0, c, bank)
                for h in range(HALVES):
                    scores(ii, h)
                turn(ii, 0)
                for u in range(STEPS):
                    if u < NU:
                        scores_t(ii, u)
                    for h in max_at.get(u, ()):
                        scores(ii, h)
                    if u in turn_at:
                        turn(ii, turn_at[u])
                    if LAG <= u < NU + LAG:
                        values(ii, u - LAG)
                    if u in sums_at:
                        sums(ii, sums_at[u])
                    if u in spread_at:
                        j, c = spread_at[u]
                        pe.wait_ge(x_done, ii * G + j - 1) if j > 1 else pe.wait_ge(x_done, ii * G)
                        spread(ii, j, c, ps_w[:])
                    if u in out_at:
                        project(ii, out_at[u])

        @block.scalar
        def _(act):
            act.sem_inc(ov_ready, 4)

            def copy_q(ii, j, c, bank):
                act.wait_ge(spread_in, (ii * G + j) * QPK + c + 1)
                nc.scalar.copy(qm[:, j % 2, c], bank).then_inc(qm_ready, 1)

            with act.Fori(0, NT // G) as ii:
                for c, bank in enumerate((flat(ps_c[:, 0]), flat(ps_c[:, 1]), flat(ps_t[:]), flat(ps_x[:]))):
                    copy_q(ii, 0, c, bank)
                for u in range(STEPS):
                    if u < NU:
                        act.wait_ge(c_ready, ii * NU + u + 1)
                        act.wait_ge(v_ready, ii * NU + u + 1)
                        nc.scalar.activation(pt[:, u % 4], ps_c[:, u % 2], ACT.Exp).then_inc(exp_ready, 1)
                    if u in copy_at:
                        n = copy_at[u]
                        act.wait_ge(v_ready, ii * NU + last[n] + 5)
                        act.wait_ge(on_ready, ii * BLK + n)
                        nc.scalar.copy(ov[:], ps_v[:]).then_inc(ov_ready, 1)
                    if u in spread_at:
                        copy_q(ii, *spread_at[u], ps_w[:])

        @block.gpsimd
        def _(pool):
            pool.wait_ge(consts, 3)
            with pool.Fori(0, NT // G) as ii:
                for j in range(G):
                    i = ii * G + j
                    pool.wait_ge(ov_ready, i * 4)
                    nc.gpsimd.tensor_tensor(kt[:, j % 2], k[:, tile(i)], w["ones_rows"].broadcast_to([P, TILE]), ALU.add)
                    for g in range(NKV):
                        ins = nc.gpsimd.tensor_copy(vt[:, j % 2, :, g, 32 * g + 1:32 * g + 1 + DH],
                                                    v_all[:, bass.ds(i * 4, 4), g * DH:(g + 1) * DH])
                    ins.then_inc(kv_ready, 1)

        @block.vector
        def _(dve):
            V = nc.vector
            V.memset(vt[:].rearrange("p j b g c -> p (j b g c)"), 0.0).then_inc(filled, 1)
            V.memset(mx[:].rearrange("p c q -> p (c q)"), 0.0).then_inc(filled, 1)
            V.memset(maskb[:, :, 0:P], 0.0)
            V.tensor_copy(maskb[:, :, P:T], w["causal"].unsqueeze(1).broadcast_to([P, 2, P])).then_inc(consts, 1)
            V.tensor_copy(eyeb[:], w["eye"].unsqueeze(1).broadcast_to([P, QPK, P])).then_inc(consts, 1)
            dve.wait_ge(filled, 2)
            for g in range(NKV):
                for j in range(2):
                    ins = V.memset(vt[:, j, :, g, 32 * g:32 * g + 1], 1.0)
            ins.then_inc(consts, 1)
            dve.sem_inc(max_ready, 2)
            dve.sem_inc(exp_ready, 2)
            dve.sem_inc(v_ready, 4)

            def biggest(ii, h):
                n, g, cp = h // HALVES, h % HALVES // 2, h % 2
                dve.wait_ge(s_ready, ii * BLK * HALVES + h + 1)
                V.tensor_reduce(mx[:, cp * 2:cp * 2 + 2, 32 * g], ps_s[:, h % 2, :, 0:(n % 2 + 1) * P], AX, ALU.max)\
                    .then_inc(max_ready, 1)

            def subtract(ii, n):
                slot, col, _row = place(n)
                dve.wait_ge(turned, ii * BLK + n + 1)
                V.tensor_tensor(qm[:, slot, :, col:col + P], qm[:, slot, :, col:col + P], ps_t[:], ALU.subtract)\
                    .then_inc(less_max, 1)

            def divide(ii, n, c):
                if c == 0:
                    dve.wait_ge(sums_in, ii * BLK + n + 1)
                    if n % 4 == 0:
                        dve.wait_ge(out_ready, ii * G + n // 4)
                V.reciprocal(rc[:, c], ps_x[:, c]).then_inc(rc_ready, 1)
                dve.wait_ge(rc_ready, (ii * BLK + n) * QPK + c + 1)
                ins = V.tensor_tensor(on[:, c, n % 4 * P:(n % 4 + 1) * P], ov[:, c], rc[:, c], ALU.mult)
                if c == QPK - 1:
                    ins.then_inc(on_ready, 1)

            with dve.Fori(0, NT // G) as ii:
                for h in range(HALVES):
                    biggest(ii, h)
                subtract(ii, 0)
                for u in range(STEPS):
                    for h in max_at.get(u, ()):
                        biggest(ii, h)
                    if u in turn_at:
                        subtract(ii, turn_at[u])
                    if u in divide_at:
                        divide(ii, *divide_at[u])
                    if u in out_at:
                        j = out_at[u]
                        dve.wait_ge(out_ready, ii * G + j + 1)
                        at = tile(ii * G + j)
                        V.tensor_tensor(x[:, at], ps_w[:], x[:, at], ALU.add).then_inc(x_done, 1)


def gated_mlp(nc, w, h, x):
    M = 4
    K = U * M
    with ExitStack() as ctx:
        up = ctx.enter_context(nc.psum_tensor("gm_up", [P, 2, 2, TILE], F32))
        down = ctx.enter_context(nc.psum_tensor("gm_down", [P, 2, TILE], F32))
        s = ctx.enter_context(nc.sbuf_tensor("gm_s", [P, 4, TILE], F32))
        hg = ctx.enter_context(nc.sbuf_tensor("gm_hg", [P, 4, TILE], F32))
        block, up_ready, silu_ready, gated, down_ready, done = ctx.enter_context(
            phase(nc, "up_ready silu_ready gated down_ready done"))
        lag = 2
        w2 = w["gm_w2"].rearrange("p (m c) -> p m c", m=M)

        @block.tensor
        def _(pe):
            with pe.Fori(0, NT // U) as i:
                for n in range(K + lag):
                    if n < K:
                        pe.wait_ge(gated, i * K + n + 1)
                        for a, name in enumerate(("gm_w1", "gm_w3")):
                            mm = nc.tensor.matmul(up[:, n % 2, a], w[name][:, (n % M) * P:(n % M + 1) * P],
                                                  h[:, tile(i * U + n // M)], start=True, stop=True)
                        mm.then_inc(up_ready, 1)
                    m = n - lag
                    if m >= 0:
                        pe.wait_ge(gated, i * K + m + 3)
                        if m % M == 0:
                            pe.wait_ge(done, i * U + m // M + 1)
                        nc.tensor.matmul(down[:, m // M % 2], w2[:, m % M], hg[:, m % 4],
                                         start=m % M == 0, stop=m % M == M - 1).then_inc(down_ready, 1)

        @block.scalar
        def _(act):
            act.sem_inc(down_ready, 4)
            with act.Fori(0, NT // U) as i:
                for n in range(K):
                    act.wait_ge(up_ready, i * K + n + 1)
                    if n >= 2:
                        act.wait_ge(gated, i * K + n - 1)
                    else:
                        act.wait_ge(gated, i * K + 1)
                    nc.scalar.activation(s[:, n % 4], up[:, n % 2, 0], ACT.Silu).then_inc(silu_ready, 1)

        @block.vector
        def _(dve):
            dve.sem_inc(gated, 2)
            dve.sem_inc(done, 2)
            with dve.Fori(0, NT // U) as i:
                for n in range(K + lag + 1):
                    if n < K:
                        dve.wait_ge(silu_ready, i * K + n + 1)
                        dve.wait_ge(down_ready, i * K + n + 1)
                        nc.vector.tensor_tensor(hg[:, n % 4], s[:, n % 4], up[:, n % 2, 1], ALU.mult).then_inc(gated, 1)
                    m = n - lag
                    if m > 0 and m % M == 0:
                        j = m // M - 1
                        dve.wait_ge(down_ready, (i * U + j + 1) * M + 4) if m < K else None
                        at = tile(i * U + j)
                        nc.vector.tensor_tensor(x[:, at], down[:, j % 2], x[:, at], ALU.add).then_inc(done, 1) \
                            if m < K else None
                dve.wait_ge(down_ready, (i * U + U) * M + 4)
                at = tile(i * U + U - 1)
                nc.vector.tensor_tensor(x[:, at], down[:, (U - 1) % 2], x[:, at], ALU.add).then_inc(done, 1)


def project_tokens(nc, w, xn, xf):
    with ExitStack() as ctx:
        ps = ctx.enter_context(nc.psum_tensor("pt_ps", [P, U, TILE], F32))
        block, ready, done = ctx.enter_context(phase(nc, "ready done"))

        @block.tensor
        def _(pe):
            with pe.Fori(0, NT // U) as i:
                for j in range(U):
                    pe.wait_ge(done, i * U + j + 1)
                    nc.tensor.matmul(ps[:, j], w["W_proj"], xn[:, tile(i * U + j)], start=True, stop=True).then_inc(ready, 1)

        @block.scalar
        def _(act):
            act.sem_inc(done, U)
            with act.Fori(0, NT // U) as i:
                for j in range(U):
                    act.wait_ge(ready, i * U + j + 1)
                    nc.scalar.activation(xf[:, tile(i * U + j)], ps[:, j], ACT.Identity, bias=w["b_proj"]).then_inc(done, 1)


def centre_experts(nc, w, w1, b1c):
    with ExitStack() as ctx:
        ps = ctx.enter_context(nc.psum_tensor("ce_ps", [P, E8, 4], F32))
        mean = ctx.enter_context(nc.sbuf_tensor("ce_mean", [P, E8], F32))
        block, chain, ready = ctx.enter_context(phase(nc, "chain ready"))

        @block.tensor
        def _(pe):
            nc.tensor.matmul(ps[:].rearrange("p e m -> p (e m)"), w["mean"], w["b1"], start=True, stop=True).then_inc(ready, 1)

        @block.vector
        def _(dve):
            V = nc.vector
            ch = Chain(dve, chain)
            wv = w1.rearrange("p (e f) -> p e f", e=E8)
            ch.then(V.tensor_reduce(mean[:], wv, AX, ALU.add))
            ch.then(V.tensor_scalar(mean[:], mean[:], 1.0 / 512, None, ALU.mult))
            ch.then(V.tensor_tensor(wv, wv, mean[:].unsqueeze(2).broadcast_to([P, E8, 512]), ALU.subtract))
            dve.wait_ge(ready, 1)
            ch.then(V.tensor_reduce(mean[:], ps[:], AX, ALU.add))
            ch.then(V.tensor_scalar(mean[:], mean[:], 0.25, None, ALU.mult))
            ch.then(V.tensor_tensor(b1c[:].rearrange("p (e m) -> p e m", m=4), w["b1"].rearrange("p (e m) -> p e m", m=4),
                                    mean[:].unsqueeze(2).broadcast_to([P, E8, 4]), ALU.subtract))


def experts_norm(nc, w, w1, b1c, w2, wt3, xf, y):
    M = 4
    with ExitStack() as ctx:
        def sb(name, shape, dt=F32):
            return ctx.enter_context(nc.sbuf_tensor("xl_" + name, shape, dt))

        up = ctx.enter_context(nc.psum_tensor("xl_up", [P, M, TILE], F32))
        var = ctx.enter_context(nc.psum_tensor("xl_var", [P, TILE], F32))
        wbc = ctx.enter_context(nc.psum_tensor("xl_wbc", [P, TILE], F32))
        down = ctx.enter_context(nc.psum_tensor("xl_down", [P, 2, TILE], F32))
        sq = sb("sq", [P, M, TILE])
        lg = sb("lg", [P, TILE])
        ri = sb("ri", [P, TILE])
        hn = sb("hn", [P, M, TILE])
        hg = sb("hg", [P, M, TILE])
        ws = sb("ws", [P, 2, TILE])
        t = sb("t", [P, 2, TILE])
        sel = sb("sel", [3 * E8, E8, P], BF16)
        (block, sel_ready, up_ready, sq_ready, var_ready, wbc_ready, lg_ready, ri_ready, ws_ready, hn_ready, hg_ready,
         down_ready, t_ready, y_ready) = ctx.enter_context(phase(
             nc, "sel_ready up_ready sq_ready var_ready wbc_ready lg_ready ri_ready ws_ready hn_ready hg_ready "
             "down_ready t_ready y_ready"))

        @block.tensor
        def _(pe):
            pe.wait_ge(sel_ready, 1)

            def product(i, e):
                v = i * E8 + e
                for m in range(M):
                    pe.wait_ge(hg_ready, v * M + m + 5)
                    if m == 0:
                        pe.wait_ge(t_ready, v + 1)
                    nc.tensor.matmul(down[:, e % 2], w2[:, e * M + m], hg[:, m], start=m == 0, stop=m == M - 1)\
                        .then_inc(down_ready, 1)

            with pe.Fori(0, NT) as i:
                for e in range(E8):
                    v = i * E8 + e
                    pe.wait_ge(ws_ready, v)
                    for m in range(M):
                        pe.wait_ge(hn_ready, v * M + m + 1)
                        nc.tensor.matmul(up[:, m], w1[:, (e * M + m) * P:(e * M + m + 1) * P], xf[:, tile(i)],
                                         start=True, stop=True).then_inc(up_ready, 1)
                    nc.tensor.matmul(wbc[:], sel[:, e], wt3[:, tile(i)], start=True, stop=True).then_inc(wbc_ready, 1)
                    if e:
                        product(i, e - 1)
                    for m in range(M):
                        pe.wait_ge(sq_ready, v * M + m + 1)
                        if m == 0:
                            pe.wait_ge(lg_ready, v)
                        mm = nc.tensor.matmul(var[:], w["mean"], sq[:, m], start=m == 0, stop=m == M - 1)
                    mm.then_inc(var_ready, 1)
                product(i, E8 - 1)

        @block.scalar
        def _(act):
            act.sem_inc(hg_ready, 4)
            act.sem_inc(down_ready, 4)
            with act.Fori(0, NT) as i:
                for e in range(E8):
                    v = i * E8 + e
                    act.wait_ge(var_ready, v)
                    for m in range(M):
                        n = e * M + m
                        act.wait_ge(up_ready, v * M + m + 1)
                        nc.scalar.activation(sq[:, m], up[:, m], ACT.Square, bias=b1c[:, n:n + 1]).then_inc(sq_ready, 1)
                    act.wait_ge(wbc_ready, v + 1)
                    act.wait_ge(t_ready, v + 1)
                    nc.scalar.copy(ws[:, e % 2], wbc[:]).then_inc(ws_ready, 1)
                    act.wait_ge(var_ready, v + 1)
                    nc.scalar.activation(lg[:], var[:], ACT.Ln, scale=0.25, bias=w["eps_col"]).then_inc(lg_ready, 1)
                    act.wait_ge(lg_ready, v + 1)
                    act.wait_ge(hn_ready, v * M + 4)
                    nc.scalar.activation(ri[:], lg[:], ACT.Exp, scale=-0.5).then_inc(ri_ready, 1)
                    for m in range(M):
                        n = e * M + m
                        act.wait_ge(hn_ready, v * M + m + 5)
                        act.wait_ge(down_ready, v * M + m + 1)
                        nc.scalar.activation(hg[:, m], hn[:, m], ACT.Gelu, scale=w["eg"][:, n:n + 1],
                                             bias=w["eb"][:, n:n + 1]).then_inc(hg_ready, 1)

        @block.vector
        def _(dve):
            V = nc.vector
            V.tensor_copy(sel[:].rearrange("p e c -> p (e c)"), w["sel3"][0:3 * E8]).then_inc(sel_ready, 1)
            dve.sem_inc(hn_ready, 4)
            dve.sem_inc(t_ready, 2)

            def combine(i, e):
                v = i * E8 + e
                dve.wait_ge(down_ready, (v + 1) * M + 4)
                dve.wait_ge(ws_ready, v + 1)
                out = y[:, tile(i)] if e == 0 else t[:, e % 2]
                V.scalar_tensor_tensor(out=out, in0=down[:, e % 2], scalar=w["eb2"][:, e:e + 1], in1=ws[:, e % 2],
                                       op0=ALU.add, op1=ALU.mult).then_inc(t_ready, 1)
                if e:
                    dve.wait_ge(t_ready, v + 3)
                    V.tensor_tensor(y[:, tile(i)], y[:, tile(i)], t[:, e % 2], ALU.add).then_inc(y_ready, 1)
                    dve.wait_ge(y_ready, i * (E8 - 1) + e)

            with dve.Fori(0, NT) as i:
                for e in range(E8):
                    v = i * E8 + e
                    dve.wait_ge(ri_ready, v + 1)
                    for m in range(M):
                        n = e * M + m
                        dve.wait_ge(hg_ready, v * M + m + 1)
                        V.scalar_tensor_tensor(out=hn[:, m], in0=up[:, m], scalar=b1c[:, n:n + 1], in1=ri[:],
                                               op0=ALU.add, op1=ALU.mult).then_inc(hn_ready, 1)
                    if e:
                        combine(i, e - 1)
                combine(i, E8 - 1)


def gate_with(nc, tag, x_old, s, g_old, x):
    with ExitStack() as ctx:
        xo = ctx.enter_context(nc.sbuf_tensor(tag + "_xo", [P, U, TILE], F32))
        go = ctx.enter_context(nc.sbuf_tensor(tag + "_go", [P, U, TILE], F32))
        names = " ".join(f"{k}{j}" for j in range(U) for k in ("x_in", "g_in"))
        block, silu_ready, chain, done, *ins = ctx.enter_context(phase(nc, "silu_ready chain done " + names))

        @block.sync
        def _(sp):
            with sp.Fori(0, NT // U) as i:
                for j in range(U):
                    sp.wait_ge(done, i * U + j + 1)
                    sp.dma_start(xo[:, j], x_old[:, tile(i * U + j)]).then_inc(ins[2 * j], 16)
                    sp.dma_start(go[:, j], g_old[:, tile(i * U + j)]).then_inc(ins[2 * j + 1], 16)

        @block.scalar
        def _(act):
            with act.Fori(0, NT // U) as i:
                for j in range(U):
                    act.wait_ge(ins[2 * j + 1], i * 16 + 16)
                    nc.scalar.activation(go[:, j], go[:, j], ACT.Silu).then_inc(silu_ready, 1)

        @block.vector
        def _(dve):
            dve.sem_inc(done, U)
            with dve.Fori(0, NT // U) as i:
                for j in range(U):
                    ch = Chain(dve, chain, i * U + j)
                    dve.wait_ge(silu_ready, i * U + j + 1)
                    ch.then(nc.vector.tensor_tensor(go[:, j], go[:, j], s[:, tile(i * U + j)], ALU.mult))
                    dve.wait_ge(ins[2 * j], i * 16 + 16)
                    nc.vector.tensor_tensor(x[:, tile(i * U + j)], go[:, j], xo[:, j], ALU.add).then_inc(done, 1)


def layer2(nc, w0, groups, r0, r1, x_d, g_d):
    x, xn = r0[:, 0:N], r1[:, 0:N]
    layernorm(nc, "ln2", x, xn, w0)
    load(nc, "x_kept", [(x_d, x)])
    with ExitStack() as ctx:
        w = ctx.enter_context(weights(nc, groups, "route", w0))
        w = ctx.enter_context(weights(nc, groups, "experts2", w))
        b1c = ctx.enter_context(nc.sbuf_tensor("l2_b1c", [P, E8 * 4], F32))
        wt3 = ctx.enter_context(nc.sbuf_tensor("l2_wt3", [3 * E8, N], BF16))
        y = ctx.enter_context(nc.sbuf_tensor("l2_y", [P, N], F32))
        w2 = w["w2"].rearrange("p (m c) -> p m c", c=P)
        centre_experts(nc, w, w["w1"], b1c)
        project_tokens(nc, w, xn, x)
        route(nc, "r2", w, w["W_gate"], x, 1, 2 * N // E8, wt3)
        experts_norm(nc, w, w["w1"], b1c, w2, wt3, x, y)
        layernorm(nc, "ln2m", y, y, w, w["moe_g"], w["moe_b"])
        load(nc, "g_kept", [(g_d, y[:])])
    with weights(nc, groups, "mamba2", w0) as w:
        layernorm(nc, "ln2a", xn, padded_tile(r0), w, w["ln1_g"], w["ln1_b"])
        mamba(nc, w, groups["once2"][0], False, r0, xn, xn)
    h = r0[:, 0:N]
    with weights(nc, groups, "attention2", w0) as w:
        layernorm(nc, "ln2b", xn, h, w, w["ln2_g"], w["ln2_b"])
        with ExitStack() as ctx:
            q = ctx.enter_context(nc.sbuf_tensor("l2_q", [P, N], F32))
            v_all = ctx.enter_context(nc.sbuf_tensor("l2_v", [P, NBLK, NKV * DH], F32))
            attention_inputs(nc, w, h, q, v_all)
            attention(nc, w, q, h, v_all, xn)
        layernorm(nc, "ln2c", xn, h, w, w["ln3_g"], w["ln3_b"])
        gated_mlp(nc, w, h, xn)
    gate_with(nc, "gw2", x_d, xn, g_d, x)



def ternary(nc, tag, w, pairs):
    with ExitStack() as ctx:
        ab = ctx.enter_context(nc.sbuf_tensor(tag + "_ab", [P, len(pairs)], F32))
        th = ctx.enter_context(nc.sbuf_tensor(tag + "_th", [P, 2, len(pairs)], F32))
        neg = ctx.enter_context(nc.sbuf_tensor(tag + "_neg", [P, 512], F32))
        ps = ctx.enter_context(nc.psum_tensor(tag + "_ps", [P, len(pairs)], F32))
        block, chain, summed, averaged = ctx.enter_context(phase(nc, "chain summed averaged"))

        @block.tensor
        def _(pe):
            pe.wait_ge(summed, 1)
            nc.tensor.matmul(ps[:], w["mean"], ab[:], start=True, stop=True).then_inc(averaged, 1)

        @block.vector
        def _(dve):
            V = nc.vector
            ch = Chain(dve, chain)
            for n, (src, dst) in enumerate(pairs):
                ch.then(V.tensor_reduce(ab[:, n:n + 1], src, AX, ALU.add, apply_absolute_value=True))
            dve.sem_inc(summed, 1)
            dve.wait_ge(averaged, 1)
            ch.then(V.tensor_scalar(th[:, 0], ps[:], 0.5 / 512, None, ALU.mult))
            ch.then(V.tensor_scalar(th[:, 1], ps[:], -0.5 / 512, None, ALU.mult))
            for n, (src, dst) in enumerate(pairs):
                ch.then(V.tensor_scalar(neg[:], src, th[:, 1, n:n + 1], None, ALU.is_lt))
                ch.then(V.scalar_tensor_tensor(out=dst, in0=src, scalar=th[:, 0, n:n + 1], in1=neg[:],
                                               op0=ALU.is_gt, op1=ALU.subtract))


def ffn3(nc, w, w_up, w_down, xn, g):
    M = 4
    with ExitStack() as ctx:
        def sb(name, shape):
            return ctx.enter_context(nc.sbuf_tensor("f3_" + name, shape, F32))

        up = ctx.enter_context(nc.psum_tensor("f3_up", [P, 2, TILE], F32))
        ms = ctx.enter_context(nc.psum_tensor("f3_ms", [P, 2, TILE], F32))
        down = ctx.enter_context(nc.psum_tensor("f3_down", [P, 2, TILE], F32))
        sqx = sb("sqx", [P, TILE])
        rms = sb("rms", [P, 2, TILE])
        rin = sb("rin", [P, 2, TILE])
        hs = sb("hs", [P, M, TILE])
        h = sb("h", [P, M, TILE])
        sqh = sb("sqh", [P, M, TILE])
        (block, sqx_ready, msx_ready, rms_ready, eps_ready, rin_ready, up_ready, hs_ready, h_ready, sqh_ready, down_ready,
         msh_ready, done) = ctx.enter_context(phase(
             nc, "sqx_ready msx_ready rms_ready eps_ready rin_ready up_ready hs_ready h_ready sqh_ready down_ready "
             "msh_ready done"))

        @block.tensor
        def _(pe):
            with pe.Fori(0, NT // 2) as ii:
                for j in range(2):
                    i = ii * 2 + j
                    pe.wait_ge(sqx_ready, i + 1)
                    pe.wait_ge(rms_ready, i * 2)
                    nc.tensor.matmul(ms[:, 0], w["mean"], sqx[:], start=True, stop=True).then_inc(msx_ready, 1)
                    for m in range(M):
                        pe.wait_ge(hs_ready, i * M + m + 1)
                        nc.tensor.matmul(up[:, (j * M + m) % 2], w_up[:, m * P:(m + 1) * P],
                                         xn[:, tile(i)], start=True, stop=True).then_inc(up_ready, 1)
                    for m in range(M):
                        pe.wait_ge(h_ready, i * M + m + 1)
                        if m == 0:
                            pe.wait_ge(done, i + 1)
                        nc.tensor.matmul(down[:, j], w_down[:, m], h[:, m], start=m == 0, stop=m == M - 1)\
                            .then_inc(down_ready, 1)
                    for m in range(M):
                        pe.wait_ge(sqh_ready, i * M + m + 1)
                        mm = nc.tensor.matmul(ms[:, 1], w["mean"], sqh[:, m], start=m == 0, stop=m == M - 1)
                    mm.then_inc(msh_ready, 1)

        @block.scalar
        def _(act):
            with act.Fori(0, NT) as i:
                act.wait_ge(msx_ready, i)
                nc.scalar.activation(sqx[:], xn[:, tile(i)], ACT.Square).then_inc(sqx_ready, 1)
                act.wait_ge(msx_ready, i + 1)
                act.wait_ge(eps_ready, i * 2)
                nc.scalar.activation(rms[:, 0], ms[:, 0], ACT.Sqrt).then_inc(rms_ready, 1)
                for m in range(M):
                    act.wait_ge(hs_ready, i * M + m + 3)
                    act.wait_ge(down_ready, i * M)
                    act.wait_ge(msh_ready, i)
                    nc.scalar.activation(h[:, m], hs[:, m], ACT.Gelu).then_inc(h_ready, 1)
                for m in range(M):
                    act.wait_ge(h_ready, i * M + m + 1)
                    nc.scalar.activation(sqh[:, m], h[:, m], ACT.Square).then_inc(sqh_ready, 1)
                act.wait_ge(msh_ready, i + 1)
                act.wait_ge(eps_ready, i * 2 + 1)
                nc.scalar.activation(rms[:, 1], ms[:, 1], ACT.Sqrt, scale=0.25).then_inc(rms_ready, 1)

        @block.vector
        def _(dve):
            V = nc.vector
            dve.sem_inc(hs_ready, 2)
            dve.sem_inc(done, 2)
            with dve.Fori(0, NT // 2) as ii:
                for j in range(2):
                    i = ii * 2 + j

                    def inverse(n):
                        dve.wait_ge(rms_ready, i * 2 + n + 1)
                        V.tensor_scalar(rms[:, n], rms[:, n], 1e-8, None, ALU.add).then_inc(eps_ready, 1)
                        dve.wait_ge(eps_ready, i * 2 + n + 1)
                        V.reciprocal(rin[:, n], rms[:, n]).then_inc(rin_ready, 1)
                        dve.wait_ge(rin_ready, i * 2 + n + 1)

                    inverse(0)
                    for m in range(M):
                        dve.wait_ge(up_ready, i * M + m + 1)
                        dve.wait_ge(h_ready, i * M)
                        V.tensor_tensor(hs[:, m], up[:, (j * M + m) % 2], rin[:, 0], ALU.mult).then_inc(hs_ready, 1)
                    inverse(1)
                    dve.wait_ge(down_ready, (i + 1) * M)
                    V.tensor_tensor(g[:, tile(i)], down[:, j], rin[:, 1], ALU.mult).then_inc(done, 1)


def copy_padded(nc, src, dst):
    with phase(nc, "copied") as (block, copied):
        @block.vector
        def _(dve):
            for i in range(4):
                at = slice(i * B // 4, (i + 1) * B // 4)
                nc.vector.tensor_copy(padded(dst)[:, at, PAD:], src.rearrange("p (b t) -> p b t", t=T)[:, at])\
                    .then_inc(copied, 1)
            dve.wait_ge(copied, 4)


def layer3(nc, w0, groups, r0, r1, x_d, g_d):
    x, xn = r0[:, 0:N], r1[:, 0:N]
    layernorm(nc, "ln3", x, xn, w0)
    load(nc, "x_kept", [(x_d, x)])
    with ExitStack() as ctx:
        w = ctx.enter_context(weights(nc, groups, "ffn3", w0))
        w_up = ctx.enter_context(nc.sbuf_tensor("l3_up", [P, 512], F32))
        w_down = ctx.enter_context(nc.sbuf_tensor("l3_down", [P, 4, P], F32))
        ternary(nc, "t3", w, [(w["w_upT"], w_up[:]), (w["w_downT"], w_down[:].rearrange("p m c -> p (m c)"))])
        ffn3(nc, w, w_up, w_down, xn, x)
        load(nc, "g_kept", [(g_d, x)])
    copy_padded(nc, xn, r0)
    with weights(nc, groups, "mamba3", w0) as w:
        mamba(nc, w, groups["once3"][0], True, r0, None, xn)
    gate_with(nc, "gw3", x_d, xn, g_d, x)



def common_pieces(np):
    return {
        "eye": np.eye(P, dtype=np.float32),
        "centre": (np.eye(P) - 1.0 / P).astype(np.float32),
        "mean": np.full((P, P), 1.0 / P, np.float32),
        "eps_col": np.full((P, 1), EPS, np.float32),
    }


def layer0_pieces(np, a):
    def padded_heads(m):
        out = np.zeros((m.shape[0], 4, 32), np.float32)
        out[:, :, 0:HL] = m.reshape(m.shape[0], 4, HL)
        return out.reshape(m.shape[0], P)

    return {
        "Wq": a["L0_attn_Wq"], "Wk": a["L0_attn_Wk"], "Wv": a["L0_attn_Wv"],
        "Wbeta": padded_heads(a["L0_attn_Wbeta"]), "Wo": a["L0_attn_Wo"],
        "bq": a["L0_attn_bq"][:, None], "bk": a["L0_attn_bk"][:, None], "bv": a["L0_attn_bv"][:, None],
        "bbeta": padded_heads(a["L0_attn_bbeta"][None]).T, "bo": a["L0_attn_bo"][:, None],
        "w_fc": a["L0_ffn_w_fc"].reshape(4, P, P).transpose(1, 0, 2).reshape(P, 512),
        "w_proj": a["L0_ffn_w_proj"], "uT": a["L0_ffn_u"].T, "v": a["L0_ffn_v"],
        "fast_bT": a["L0_ffn_fast_b"].T, "gate": np.full((P, 1), a["L0_ffn_gate"], np.float32),
    }


def routing_pieces(np):
    sel = np.zeros((3 * E8, E8, P), np.float32)
    for n in range(3):
        sel[n * E8 + np.arange(E8), np.arange(E8)] = 1.0
    return {
        "tri": np.triu(np.ones((P, P), np.float32)),
        "ones": np.ones((P, P), np.float32),
        "iota8": np.tile(np.arange(-E8, 0, dtype=np.float32), (P, 1)),
        "sel3": sel.reshape(3 * E8, E8 * P),
    }


def layer1_pieces(np, a):
    K2 = 2 * KEIG
    swap = np.r_[KEIG:K2, 0:KEIG]
    couple = np.zeros((2, 4, 16, 2, 4, 16), np.float32)
    for r in range(2):
        for h in range(4):
            couple[r, h, :, r, h, :] = a["L1_attn_coupling"][h]
    couple = couple.reshape(K2, K2)
    inner = np.ones((P, TILE), np.float32)
    inner[:, 0::CH] = 0.0
    w_in = a["L1_attn_w_in"].T
    col = lambda v: v.reshape(-1, P).T
    return {
        "w_inT": w_in, "w_inT_sw": w_in[:, swap], "w_gateT": a["L1_attn_w_gate"].T, "b_gate": col(a["L1_attn_b_gate"]),
        "w_outT": a["L1_attn_w_out"].T, "couple": couple, "couple_sw": couple[:, swap],
        "frequency": np.tile(a["L1_attn_frequency"], 2)[:, None], "log_decay": np.tile(a["L1_attn_log_decay"], 2)[:, None],
        "steps": np.tile(np.arange(CH, dtype=np.float32), (P, 1)), "inner": inner,
        "sign": np.repeat(np.array([-1.0, 1.0], np.float32), KEIG)[:, None],
        "ln1_g": col(a["L1_attn_ln1_g"]), "ln1_b": col(a["L1_attn_ln1_b"]),
        "ln2_g": col(a["L1_attn_ln2_g"]), "ln2_b": col(a["L1_attn_ln2_b"]),
        "w_mlp1T": a["L1_attn_w_mlp1"].T, "b_mlp1": col(a["L1_attn_b_mlp1"]),
        "w_mlp2T": a["L1_attn_w_mlp2"].T.reshape(4, P, P).transpose(1, 0, 2).reshape(P, 512),
        "b_mlp2": col(a["L1_attn_b_mlp2"]),
    }


def expert_pieces(w1, w2):
    return {"w1": w1.transpose(1, 0, 2).reshape(P, E8 * 512),
            "w2": w2.reshape(E8, 4, P, P).transpose(2, 0, 1, 3).reshape(P, E8 * 512)}


def mamba_pieces(np, a, tag, l3):
    halves = lambda m: m.reshape(2, P, -1).transpose(1, 0, 2).reshape(P, -1)
    get = lambda name: a[f"{tag}_{name}"]
    conv = get("conv_w").reshape(DI, TAPS)
    if l3:
        in_w, xp, dt_w, out_w, a_log, d = (get("in_proj_w").T, get("x_proj_w").T, get("dt_proj_w").T,
                                           get("out_proj_w").T, get("A_log").T, get("D"))
        low, bc = xp[:, 0:64], xp[:, 64:]
    else:
        in_w, bc, dt_w, out_w, a_log, d = (get("in_proj_w"), get("x_proj_w"), get("dt_proj_w"), get("out_proj_w"),
                                           get("A_log"), get("D_skip"))
    spread = np.zeros((DI, 4, 2 * NSTATE), np.float32)
    spread[:, [0, 2, 3]] = bc[:, None]
    sel = np.zeros((P, 2 * NSTATE, P), np.float32)
    for first in (0, 64, 96):
        sel[first + np.arange(2 * NSTATE), np.arange(2 * NSTATE)] = 1.0
    out = {
        "in_w": in_w, "conv_b": halves(get("conv_b")),
        "xp_bc": halves(spread.reshape(DI, P)), "dt_w": dt_w, "dt_b": halves(get("dt_proj_b")),
        "A_log": halves(a_log), "D": halves(d), "out_w": halves(out_w),
    }
    once = {"conv_rows": np.tile(conv.T.reshape(1, TAPS * DI), (P, 1)), "sel_bc": sel.reshape(P, 2 * NSTATE * P)}
    if l3:
        out.update({"xp_low": halves(low), "in_b": get("in_proj_b").reshape(4, P).T, "conv_cols": halves(conv),
                    "out_b": get("out_proj_b")[:, None]})
    return out, once


def layer2_pieces(np, a):
    get = lambda name: a["L2_attn_" + name]
    inv = 1.0 / 10000.0 ** (np.arange(0, DH, 2, dtype=np.float32) / DH)
    emb = np.arange(T, dtype=np.float32)[:, None] * np.concatenate([inv, inv])[None].astype(np.float32)
    sign = np.where(np.arange(DH) < DH // 2, -1.0, 1.0)
    cos, sin = np.cos(emb).T, np.sin(emb).T * sign[:, None]
    heads = lambda m: np.tile(m, (NH, 1)).astype(np.float32)
    rot = np.arange(P).reshape(-1, 2, DH // 2)[:, ::-1].reshape(P)
    rows = np.arange(NKV)[:, None] * 32 + 1 + np.arange(DH)[None]
    swap = np.concatenate([np.arange(DH // 2, DH), np.arange(DH // 2)])

    def at_rows(m, axis=1):
        out = np.zeros((m.shape[0], P) if axis else (P, m.shape[1]), np.float32)
        out[(slice(None), rows.reshape(-1)) if axis else (rows.reshape(-1),)] = m
        return out

    k_w = get("k_w")
    k_rot = k_w.reshape(P, NKV, DH)[:, :, swap].reshape(P, NKV * DH)
    of_head = lambda c: ((np.arange(NKV)[:, None] * QPK + c) * DH + np.arange(DH)[None]).reshape(-1)
    eye = np.eye(P, dtype=np.float32)
    key_heads = lambda m: at_rows(np.tile(m, (NKV, 1)).astype(np.float32), 0)
    col = lambda v: v.reshape(-1, P).T
    scale = 1.0 / np.sqrt(np.float32(DH))
    return {
        "ln2_g": col(get("ln2_g")), "ln2_b": col(get("ln2_b")), "ln3_g": col(get("ln3_g")), "ln3_b": col(get("ln3_b")),
        "q_w": get("q_w"), "q_w_rot": get("q_w")[:, rot], "k_w": at_rows(k_w), "k_w_rot": at_rows(k_rot), "v_w": np.pad(get("v_w"), ((0, 0), (0, P - NKV * DH))),
        "o_w": np.concatenate([at_rows(get("o_w")[of_head(c)], 0) for c in range(QPK)], axis=1),
        "spread": np.concatenate([at_rows(eye[:, of_head(c)]) for c in range(QPK)], axis=1),
        "sum_rows": np.repeat(eye[:, 0:P:32], 32, axis=1), "ones_rows": eye[:, 0:P:32].sum(axis=1, keepdims=True),
        "q_cos": heads(cos * scale), "q_sin": heads(sin * scale), "k_cos": key_heads(cos), "k_sin": key_heads(sin),
        "causal": np.where(np.tril(np.ones((P, P), bool)), 0.0, -1e9).astype(np.float32),
        "gm_w1": get("w1"), "gm_w3": get("w3"), "gm_w2": get("w2").reshape(4, P, P).transpose(1, 0, 2).reshape(P, 512),
    }


def experts2_pieces(np, a):
    moe = lambda name: a["L2_ffn_" + name]
    col = lambda v: v.reshape(-1, P).T
    experts = lambda m: m.reshape(E8 * 4, P).T
    return {
        "W_proj": moe("W_proj"), "b_proj": col(moe("b_proj")), "W_gate": moe("W_gate"), "b1": experts(moe("b1")),
        "eg": experts(moe("ln1_g")), "eb": experts(moe("ln1_b")), "eb2": moe("b2").T,
        "moe_g": col(moe("ln_g")), "moe_b": col(moe("ln_b")),
    }


def layer3_pieces(np, a):
    return {"w_upT": a["L3_ffn_w_up"].T,
            "w_downT": a["L3_ffn_w_down"].T.reshape(4, P, P).transpose(1, 0, 2).reshape(P, 512)}


def pack(np, pieces):
    cols, at, n = {}, [], 0
    for name, piece in pieces.items():
        cols[name] = (n, n + piece.shape[1])
        n += piece.shape[1]
        full = np.zeros((P, piece.shape[1]), np.float32)
        full[0:piece.shape[0]] = piece
        at.append(full)
    return np.ascontiguousarray(np.concatenate(at, axis=1)), cols


def groups_of(np, a):
    col = lambda v: v.reshape(-1, P).T
    mamba2, once2 = mamba_pieces(np, a, "L2_attn", False)
    mamba3, once3 = mamba_pieces(np, a, "L3_attn", True)
    mamba2.update({"ln1_g": col(a["L2_attn_ln1_g"]), "ln1_b": col(a["L2_attn_ln1_b"])})
    experts1 = {"router": a["L1_ffn_router_w"], "moe_bias": a["L1_ffn_bias"].reshape(P, 1),
                **expert_pieces(a["L1_ffn_w1"], a["L1_ffn_w2"])}
    experts2 = {**experts2_pieces(np, a), **expert_pieces(a["L2_ffn_W1"], a["L2_ffn_W2"])}
    return {"common": common_pieces(np), "l0": layer0_pieces(np, a), "l1": layer1_pieces(np, a),
            "route": routing_pieces(np), "experts1": experts1, "experts2": experts2, "mamba2": mamba2, "once2": once2,
            "attention2": layer2_pieces(np, a), "mamba3": mamba3, "once3": once3, "ffn3": layer3_pieces(np, a)}


def build(nc, groups, x_in, x_out, x_d, g_d, layers=(0, 1, 2, 3)):
    with ExitStack() as ctx:
        r0 = ctx.enter_context(nc.sbuf_tensor("r0", [P, B * TP], F32))
        r1 = ctx.enter_context(nc.sbuf_tensor("r1", [P, B * TP], F32))
        w0 = ctx.enter_context(weights(nc, groups, "common", {}))
        if 0 in layers:
            with nc.sbuf_tensor("x0", [P, N], F32) as x0, nc.sbuf_tensor("s0", [P, N], F32) as s0:
                load(nc, "x_loaded", [(x0[:], x_in)])
                layer0(nc, w0, groups, x0[:], r1[:, 0:N], s0[:], r0[:, 0:N])
        else:
            load(nc, "x_loaded", [(r0[:, 0:N], x_in)])
        if 1 in layers:
            with nc.sbuf_tensor("s1", [P, N], F32) as s1:
                layer1(nc, w0, groups, r0[:, 0:N], r1[:, 0:N], s1[:])
        if 2 in layers:
            layer2(nc, w0, groups, r0, r1, x_d, g_d)
        if 3 in layers:
            layer3(nc, w0, groups, r0, r1, x_d, g_d)
        load(nc, "x_stored", [(x_out, r0[:, 0:N])])


def kernel(**inputs):
    import numpy as np
    import concourse.bacc as bacc
    from concourse.bass_utils import run_bass_kernel_spmd

    a = {k: np.asarray(v) for k, v in inputs.items()}
    nc = bacc.Bacc("TRN2", target_bir_lowering=False, num_devices=1)
    arrays, groups = {}, {}
    for name, pieces in groups_of(np, a).items():
        arrays["in_" + name], cols = pack(np, pieces)
        groups[name] = (nc.dram_tensor("in_" + name, arrays["in_" + name].shape, F32, kind="ExternalInput").ap(), cols)
    arrays["in_x"] = np.ascontiguousarray(a["L0_attn_x"].transpose(2, 1, 0).reshape(P, N))
    x_in = nc.dram_tensor("in_x", (P, N), F32, kind="ExternalInput").ap()
    x_out = nc.dram_tensor("out_x", (P, N), F32, kind="ExternalOutput").ap()
    x_d = nc.dram_tensor("kept_x", (P, N), F32).ap()
    g_d = nc.dram_tensor("kept_g", (P, N), F32).ap()
    build(nc, groups, x_in, x_out, x_d, g_d)
    r = run_bass_kernel_spmd(nc, [arrays], core_ids=[0])
    return np.ascontiguousarray(r.results[0]["out_x"].reshape(P, B, T).transpose(1, 2, 0))
```

```python
from contextlib import ExitStack, contextmanager

import concourse.bass as bass
from concourse import mybir

F32 = mybir.dt.float32
BF16 = mybir.dt.bfloat16
ALU = mybir.AluOpType
ACT = mybir.ActivationFunctionType
AX = mybir.AxisListType.X

P = 128
B, T = 32, 256
N = B * T
TILE = 512
NT = N // TILE
U = 4
EPS = 1e-5


@contextmanager
def phase(nc, names):
    stage = nc.next_id()
    sems = [nc.alloc_semaphore(f"{n}_{stage}") for n in names.split()]
    with nc.Block() as block:
        yield (block, *sems)
    nc.clear_and_free_semaphores(sems)
    nc.all_engine_barrier()


class Chain:

    def __init__(self, eng, sem, start=0):
        self.eng, self.sem, self.start, self.n = eng, sem, start, 0

    def then(self, ins):
        ins.then_inc(self.sem, 1)
        self.n += 1
        self.eng.wait_ge(self.sem, self.start + self.n)


def tile(i):
    return bass.ds(i * TILE, TILE)

def layernorm(nc, tag, src, dst, const, gain=None, shift=None, keep=None):
    with ExitStack() as ctx:
        cen = ctx.enter_context(nc.psum_tensor(tag + "_cen", [P, U, TILE], F32))
        var = ctx.enter_context(nc.psum_tensor(tag + "_var", [P, 2, TILE], F32))
        sq = ctx.enter_context(nc.sbuf_tensor(tag + "_sq", [P, 2, TILE], F32))
        lg = ctx.enter_context(nc.sbuf_tensor(tag + "_lg", [P, 2, TILE], F32))
        ri = ctx.enter_context(nc.sbuf_tensor(tag + "_ri", [P, 2, TILE], F32))
        block, centred, squared, var_ready, log_ready, ri_ready, chain, normed, kept = ctx.enter_context(
            phase(nc, "centred squared var_ready log_ready ri_ready chain normed kept"))

        if keep is not None:
            @block.sync
            def _(sp):
                sp.dma_start(keep, src).then_inc(kept, 16)
                sp.wait_ge(kept, 16)

        @block.tensor
        def _(pe):
            with pe.Fori(0, NT // U) as i:
                for g in range(0, U, 2):
                    for j in (g, g + 1):
                        pe.wait_ge(normed, i * U + j + 1)
                        nc.tensor.matmul(cen[:, j], const["centre"], src[:, tile(i * U + j)],
                                         start=True, stop=True).then_inc(centred, 1)
                    for j in (g, g + 1):
                        pe.wait_ge(squared, i * U + j + 1)
                        pe.wait_ge(log_ready, i * U + j + 1)
                        nc.tensor.matmul(var[:, j % 2], const["mean"], sq[:, j % 2],
                                         start=True, stop=True).then_inc(var_ready, 1)

        @block.scalar
        def _(act):
            act.sem_inc(log_ready, 2)
            with act.Fori(0, NT // U) as i:
                for g in range(0, U, 2):
                    for j in (g, g + 1):
                        act.wait_ge(centred, i * U + j + 1)
                        act.wait_ge(log_ready, i * U + j + 1)
                        nc.scalar.activation(sq[:, j % 2], cen[:, j], ACT.Square).then_inc(squared, 1)
                    for j in (g, g + 1):
                        act.wait_ge(var_ready, i * U + j + 1)
                        nc.scalar.activation(lg[:, j % 2], var[:, j % 2], ACT.Ln,
                                             bias=const["eps_col"]).then_inc(log_ready, 1)
                    for j in (g, g + 1):
                        act.wait_ge(log_ready, i * U + j + 3)
                        act.wait_ge(normed, i * U + j + U - 1)
                        nc.scalar.activation(ri[:, j % 2], lg[:, j % 2], ACT.Exp, scale=-0.5).then_inc(ri_ready, 1)

        @block.vector
        def _(dve):
            dve.sem_inc(normed, U)
            with dve.Fori(0, NT // U) as i:
                ch = Chain(dve, chain, i * U)
                for j in range(U):
                    dve.wait_ge(ri_ready, i * U + j + 1)
                    out = dst(i * U + j) if callable(dst) else dst[:, tile(i * U + j)]
                    two = (lambda ap: ap.rearrange("p (r t) -> p r t", t=T)) if callable(dst) else (lambda ap: ap)
                    last = nc.vector.tensor_tensor(out, two(cen[:, j]), two(ri[:, j % 2]), ALU.mult)
                    if gain is not None:
                        ch.then(last)
                        last = nc.vector.tensor_scalar(out, out, gain, shift, ALU.mult, ALU.add)
                    last.then_inc(normed, 1)


def load(nc, name, pairs):
    with phase(nc, name) as (block, loaded):
        @block.sync
        def _(sp):
            for dst, src in pairs:
                sp.dma_start(dst, src).then_inc(loaded, 16)
            sp.wait_ge(loaded, 16 * len(pairs))


@contextmanager
def weights(nc, groups, name, w):
    src, cols = groups[name]
    with nc.sbuf_tensor(f"w_{name}_{nc.next_id()}", [P, src.shape[1]], F32) as sb:
        load(nc, name + "_loaded", [(sb[:], src)])
        yield {**w, **{k: sb[:, a:b] for k, (a, b) in cols.items()}}



H0, D0 = 16, 8
HL = 4
STEPS = TILE // B
HD = HL * D0
ST = HL * D0 * D0
NS = 4


def delta_rule(nc, w, xn, s):
    HH = HL // 2
    with ExitStack() as ctx:
        def sb(name, shape):
            return ctx.enter_context(nc.sbuf_tensor(name, shape, F32))

        proj = ctx.enter_context(nc.psum_tensor("proj", [P, 4, TILE], F32))
        oproj = ctx.enter_context(nc.psum_tensor("oproj", [P, TILE], F32))
        fm = sb("fm", [P, 4, TILE])
        tm = sb("tm", [P, 4, TILE])
        q, k, v, beta = (tm[:, n].rearrange("p (t h d) -> p t h d", h=HL, d=D0) for n in range(4))
        beta = tm[:, 3].rearrange("p (t c) -> p t c", c=HD)[:, :, 0:HL]
        sqk = sb("sqk", [P, STEPS * HL, D0])
        nrm = sb("nrm", [P, STEPS * HL])
        kb = sb("kb", [P, STEPS, HL, D0])
        vb = sb("vb", [P, STEPS, HL, D0])
        state = sb("state", [P, NS, HL, D0, D0])
        prod = sb("prod", [P, HL, D0, D0])
        outer = sb("outer", [P, HL, D0, D0])
        pred = sb("pred", [P, HL, D0])
        upd = sb("upd", [P, HL, D0])
        sq_q = sb("sq_q", [P, STEPS, HL * D0, D0])
        o_tm = sb("o_tm", [P, TILE])
        o_fm = sb("o_fm", [P, TILE])
        (block, projected, evacuated, turned, norm2, norm1, prepared, chain, stepped, state_ready, sq_ready, o_ready,
         o_projected, s_ready) = ctx.enter_context(phase(
             nc, "projected evacuated turned norm2 norm1 prepared chain stepped state_ready sq_ready o_ready "
             "o_projected s_ready"))

        @block.tensor
        def _(pe):
            with pe.Fori(0, NT) as i:
                for n, name in enumerate(("Wq", "Wk", "Wv", "Wbeta")):
                    pe.wait_ge(evacuated, i * 4 + n + 1)
                    nc.tensor.matmul(proj[:, n], w[name], xn[:, tile(i)], start=True, stop=True).then_inc(projected, 1)
                pe.wait_ge(o_ready, i + 1)
                pe.wait_ge(s_ready, i + 1)
                nc.tensor.matmul(oproj[:], w["Wo"], o_fm[:], start=True, stop=True).then_inc(o_projected, 1)

        @block.scalar
        def _(act):
            act.sem_inc(evacuated, 4)
            act.sem_inc(s_ready, 1)
            with act.Fori(0, NT) as i:
                act.wait_ge(turned, i + 1)
                for n, name in enumerate(("bq", "bk", "bv", "bbeta")):
                    act.wait_ge(projected, i * 4 + n + 1)
                    nc.scalar.activation(fm[:, n], proj[:, n], ACT.Identity if n < 3 else ACT.Sigmoid,
                                         bias=w[name]).then_inc(evacuated, 1)
                act.wait_ge(norm2, i + 1)
                nc.scalar.activation(nrm[:], nrm[:], ACT.Sqrt).then_inc(norm1, 1)
                act.wait_ge(o_projected, i + 1)
                nc.scalar.activation(s[:, tile(i)], oproj[:], ACT.Identity, bias=w["bo"]).then_inc(s_ready, 1)

        @block.gpsimd
        def _(pool):
            pool.sem_inc(sq_ready, NS)
            with pool.Fori(0, NT) as i:
                pool.wait_ge(o_ready, i)
                for t in range(STEPS):
                    pool.wait_ge(state_ready, (i * STEPS + t + 2) * 2)
                    nc.gpsimd.tensor_tensor(
                        sq_q[:, t].rearrange("p (h d) e -> p h d e", h=HL), state[:, (t + 1) % NS],
                        q[:, t].unsqueeze(2).broadcast_to([P, HL, D0, D0]), ALU.mult).then_inc(sq_ready, 1)

        @block.vector
        def _(dve):
            dve.sem_inc(turned, 1)
            nc.vector.memset(state[:, 0], 0.0).then_inc(state_ready, 2)
            dve.wait_ge(state_ready, 2)
            links = 7
            with dve.Fori(0, NT) as i:
                ch = Chain(dve, chain, i * links)
                dve.wait_ge(evacuated, i * 4 + 8)
                dve.wait_ge(sq_ready, i * STEPS + NS)
                ins = nc.vector.transpose(tm[:].rearrange("p n c -> p (n c)"), fm[:].rearrange("p n c -> p (n c)"))
                ins.then_inc(turned, 1)
                dve.wait_ge(turned, i + 2)
                kk = k.rearrange("p t h d -> p (t h) d")
                ch.then(nc.vector.tensor_tensor(sqk[:], kk, kk, ALU.mult))
                nc.vector.tensor_reduce(nrm[:], sqk[:], AX, ALU.add).then_inc(norm2, 1)
                nc.vector.tensor_tensor(vb[:], v, beta.unsqueeze(3).broadcast_to([P, STEPS, HL, D0]),
                                        ALU.mult).then_inc(prepared, 1)
                dve.wait_ge(norm1, i + 1)
                ch.then(nc.vector.tensor_scalar_add(nrm[:], nrm[:], 1e-6))
                ch.then(nc.vector.reciprocal(nrm[:], nrm[:]))
                ch.then(nc.vector.tensor_tensor(kk, kk, nrm[:].unsqueeze(2).broadcast_to([P, STEPS * HL, D0]),
                                                ALU.mult))
                ch.then(nc.vector.tensor_tensor(kb[:], k, beta.unsqueeze(3).broadcast_to([P, STEPS, HL, D0]),
                                                ALU.mult))
                dve.wait_ge(prepared, i + 1)
                for t in range(STEPS):
                    old, new = state[:, t % NS], state[:, (t + 1) % NS]
                    n = i * STEPS + t
                    for f in range(2):
                        at = slice(f * HH, (f + 1) * HH)
                        dve.wait_ge(state_ready, n * 2 + f + 1)
                        nc.vector.tensor_tensor(prod[:, at], old[:, at],
                                                kb[:, t, at].unsqueeze(2).broadcast_to([P, HH, D0, D0]),
                                                ALU.mult).then_inc(stepped, 1)
                    for f in range(2):
                        at = slice(f * HH, (f + 1) * HH)
                        dve.wait_ge(stepped, n * 8 + f + 1)
                        nc.vector.tensor_reduce(pred[:, at], prod[:, at], AX, ALU.add).then_inc(stepped, 1)
                    for f in range(2):
                        at = slice(f * HH, (f + 1) * HH)
                        dve.wait_ge(stepped, n * 8 + 2 + f + 1)
                        nc.vector.tensor_tensor(upd[:, at], vb[:, t, at], pred[:, at], ALU.subtract).then_inc(stepped, 1)
                    for f in range(2):
                        at = slice(f * HH, (f + 1) * HH)
                        dve.wait_ge(stepped, n * 8 + 4 + f + 1)
                        nc.vector.tensor_tensor(outer[:, at], upd[:, at].unsqueeze(3).broadcast_to([P, HH, D0, D0]),
                                                k[:, t, at].unsqueeze(2).broadcast_to([P, HH, D0, D0]),
                                                ALU.mult).then_inc(stepped, 1)
                    dve.wait_ge(sq_ready, n + 1)
                    for f in range(2):
                        at = slice(f * HH, (f + 1) * HH)
                        dve.wait_ge(stepped, n * 8 + 6 + f + 1)
                        nc.vector.tensor_tensor(new[:, at], old[:, at], outer[:, at], ALU.add).then_inc(state_ready, 1)
                dve.wait_ge(sq_ready, (i + 1) * STEPS + NS)
                ch.then(nc.vector.tensor_reduce(o_tm[:], sq_q[:].rearrange("p t h e -> p (t h) e"), AX, ALU.add))
                dve.wait_ge(o_projected, i)
                ch.then(nc.vector.transpose(o_fm[:], o_tm[:]))
                dve.sem_inc(o_ready, 1)


def ternary_weights(nc, w, wfc_t, wproj_t):
    with ExitStack() as ctx:
        def sb(name, shape):
            return ctx.enter_context(nc.sbuf_tensor(name, shape, F32))

        fcs = w["w_fc"].rearrange("p (m c) -> p m c", m=4)
        neg = sb("tw_neg", [P, 4, P])
        pos = sb("tw_pos", [P, 4, P])
        sc = sb("tw_sc", [P, 3, 4])
        fbv = sb("tw_fbv", [16, P])
        pst = ctx.enter_context(nc.psum_tensor("tw_pst", [P, 4, P], F32))
        psl = ctx.enter_context(nc.psum_tensor("tw_psl", [P, TILE], F32))
        block, chain, fc_ready, fc_turned, low1, low1s, low2, fc_done, proj_ready, proj_turned = ctx.enter_context(
            phase(nc, "chain fc_ready fc_turned low1 low1s low2 fc_done proj_ready proj_turned"))

        @block.vector
        def _(dve):
            ch = Chain(dve, chain)
            dve.wait_ge(low1, 1)
            nc.vector.tensor_copy(fbv[:], psl[0:16, 0:P]).then_inc(low1s, 1)

            def rows(src, blocks, cols):
                p, n = (x[:].rearrange("p m c -> p (m c)").rearrange("p (m c) -> p m c", m=blocks)
                           for x in (pos, neg))
                mean, half, nhalf = (sc[:, n, 0:blocks] for n in range(3))
                ch.then(nc.vector.tensor_reduce(mean, src, AX, ALU.add, apply_absolute_value=True))
                ch.then(nc.vector.tensor_scalar(mean, mean, 1.0 / cols, EPS, ALU.mult, ALU.max))
                ch.then(nc.vector.tensor_scalar(half, mean, 0.5, None, ALU.mult))
                ch.then(nc.vector.tensor_scalar(nhalf, mean, -0.5, None, ALU.mult))
                for m in range(blocks):
                    ch.then(nc.vector.tensor_scalar(p[:, m], src[:, m], sc[:, 1, m:m + 1], sc[:, 0, m:m + 1],
                                                    ALU.is_gt, ALU.mult))
                    ch.then(nc.vector.tensor_scalar(n[:, m], src[:, m], sc[:, 2, m:m + 1], sc[:, 0, m:m + 1],
                                                    ALU.is_lt, ALU.mult))
                ch.then(nc.vector.tensor_tensor(p, p, n, ALU.subtract))

            rows(fcs, 4, P)
            dve.sem_inc(fc_ready, 1)
            dve.wait_ge(fc_turned, 1)
            ch.then(nc.vector.tensor_copy(wfc_t, pst[:].rearrange("p m c -> p (m c)")))
            dve.wait_ge(low2, 1)
            ch.then(nc.vector.scalar_tensor_tensor(out=wfc_t, in0=psl[:], scalar=w["gate"], in1=wfc_t,
                                                   op0=ALU.mult, op1=ALU.add))
            rows(w["w_proj"].rearrange("p (m c) -> p m c", m=1), 1, 512)
            dve.sem_inc(proj_ready, 1)
            dve.wait_ge(proj_turned, 1)
            ch.then(nc.vector.tensor_copy(wproj_t, pst[:]))

        @block.tensor
        def _(pe):
            nc.tensor.matmul(psl[0:16, 0:P], w["fast_bT"][0:16], w["v"][0:16], start=True, stop=True).then_inc(low1, 1)
            pe.wait_ge(low1s, 1)
            nc.tensor.matmul(psl[:], fbv[:], w["uT"][0:16], start=True, stop=True).then_inc(low2, 1)
            for ready, turned in ((fc_ready, fc_turned), (proj_ready, proj_turned)):
                pe.wait_ge(ready, 1)
                for m in range(4):
                    last = nc.tensor.transpose(pst[:, m], pos[:, m], w["eye"])
                last.then_inc(turned, 1)


LAG = 3


def ffn0(nc, w, wfc_t, wproj_t, xn, s, x, x_out):
    M = 4
    with ExitStack() as ctx:
        def sb(name, shape):
            return ctx.enter_context(nc.sbuf_tensor(name, shape, F32))

        up = ctx.enter_context(nc.psum_tensor("f0_up", [P, 4, TILE], F32))
        down = ctx.enter_context(nc.psum_tensor("f0_down", [P, 2, TILE], F32))
        r = sb("f0_r", [P, 4, TILE])
        r2 = sb("f0_r2", [P, 4, TILE])
        g = sb("f0_g", [P, 2, TILE])
        block, h_ready, relu_ready, r2_ready, y_ready, g_ready, chain, done = ctx.enter_context(
            phase(nc, "h_ready relu_ready r2_ready y_ready g_ready chain done"))
        K = U * M

        @block.tensor
        def _(pe):
            with pe.Fori(0, NT // U) as i:
                for n in range(K + LAG):
                    if n < K:
                        pe.wait_ge(relu_ready, i * K + n + 1)
                        nc.tensor.matmul(up[:, n % 4], wfc_t[:, (n % M) * P:(n % M + 1) * P], xn[:, tile(i * U + n // M)],
                                         start=True, stop=True).then_inc(h_ready, 1)
                    m = n - LAG
                    if m >= 0:
                        pe.wait_ge(r2_ready, i * K + m + 5)
                        if m % M == 0:
                            pe.wait_ge(g_ready, i * U + m // M + 1)
                        mm = nc.tensor.matmul(down[:, m // M % 2], wproj_t[:, m % M], r2[:, m % 4],
                                              start=m % M == 0, stop=m % M == M - 1)
                        mm.then_inc(y_ready, 1)

        @block.scalar
        def _(act):
            act.sem_inc(relu_ready, 4)
            act.sem_inc(g_ready, 2)
            with act.Fori(0, NT // U) as i:
                for n in range(K + M + 1):
                    if n < K:
                        act.wait_ge(h_ready, i * K + n + 1)
                        act.wait_ge(r2_ready, i * K + n + 1)
                        nc.scalar.activation(r[:, n % 4], up[:, n % 4], ACT.Relu).then_inc(relu_ready, 1)
                    if n > M and n % M == 0 or n == K + M:
                        j = n // M - 2 if n < K + M else U - 1
                        if n == K:
                            j = U - 2
                        act.wait_ge(y_ready, (i * U + j + 1) * M)
                        act.wait_ge(done, i * U + j + 1)
                        nc.scalar.activation(g[:, j % 2], down[:, j % 2], ACT.Silu).then_inc(g_ready, 1)

        @block.vector
        def _(dve):
            dve.sem_inc(r2_ready, 4)
            dve.sem_inc(done, 2)
            with dve.Fori(0, NT // U) as i:
                for n in range(K + M + 1):
                    if n < K:
                        dve.wait_ge(relu_ready, i * K + n + 5)
                        dve.wait_ge(y_ready, i * K + n - 3) if n >= 4 else dve.wait_ge(y_ready, i * K)
                        nc.vector.tensor_tensor(r2[:, n % 4], r[:, n % 4], r[:, n % 4], ALU.mult).then_inc(r2_ready, 1)
                    if n > M and n % M == 0 or n == K + M:
                        j = n // M - 2 if n < K + M else U - 1
                        ch = Chain(dve, chain, i * U + j)
                        dve.wait_ge(g_ready, i * U + j + 3)
                        at = tile(i * U + j)
                        ch.then(nc.vector.tensor_tensor(g[:, j % 2], g[:, j % 2], s[:, at], ALU.mult))
                        nc.vector.tensor_tensor(
                            x_out.rearrange("p (b t) -> p t b", b=B)[:, bass.ds((i * U + j) * STEPS, STEPS), :],
                            g[:, j % 2].rearrange("p (t b) -> p t b", b=B),
                            x[:, at].rearrange("p (t b) -> p t b", b=B), ALU.add).then_inc(done, 1)


def layer0(nc, w0, groups, x, xn, s, x_out):
    layernorm(nc, "ln0", x, xn, w0)
    with weights(nc, groups, "l0", w0) as w:
        delta_rule(nc, w, xn, s)
        with ExitStack() as ctx:
            wfc_t = ctx.enter_context(nc.sbuf_tensor("wfc_t", [P, 512], F32))
            wproj_t = ctx.enter_context(nc.sbuf_tensor("wproj_t", [P, 4, P], F32))
            ternary_weights(nc, w, wfc_t[:], wproj_t[:])
            ffn0(nc, w, wfc_t[:], wproj_t[:], xn, s, x, x_out)


class Marks:

    def __init__(self, eng, sem, start=0):
        self.eng, self.sem, self.start, self.n, self.at = eng, sem, start, 0, {}

    def mark(self, name, ins):
        ins.then_inc(self.sem, 1)
        self.n += 1
        self.at[name] = self.n

    def need(self, name):
        self.eng.wait_ge(self.sem, self.start + self.at[name])



CH = 64
KEIG = 64
TWO_PI_HI, TWO_PI_LO = 6.28125, 0.0019353071795864769
ROUND = 1.5 * 2 ** 23


def eigen_tables(nc, w, cos_t, sin_t, decay, wa, wb):
    with ExitStack() as ctx:
        def sb(name, shape):
            return ctx.enter_context(nc.sbuf_tensor(name, shape, F32))

        ph, tn, hs = sb("et_ph", [P, CH]), sb("et_tn", [P, CH]), sb("et_hs", [P, CH])
        mag = sb("et_mag", [P, 1])
        ps = ctx.enter_context(nc.psum_tensor("et_ps", [P, 2, P], F32))
        block, chain, folded, phase_ready, half_ready, mag_ready = ctx.enter_context(
            phase(nc, "chain folded phase_ready half_ready mag_ready"))

        @block.tensor
        def _(pe):
            nc.tensor.matmul(ps[:, 0], w["couple"], w["w_outT"], start=True, stop=True).then_inc(folded, 1)
            nc.tensor.matmul(ps[:, 1], w["couple_sw"], w["w_outT"], start=True, stop=True).then_inc(folded, 1)

        @block.vector
        def _(dve):
            ch = Chain(dve, chain)
            dve.wait_ge(folded, 2)
            ch.then(nc.vector.tensor_copy(wa, ps[:, 0]))
            ch.then(nc.vector.tensor_copy(wb, ps[:, 1]))
            ch.then(nc.vector.tensor_scalar(ph[:], w["steps"], w["frequency"], None, ALU.mult))
            ch.then(nc.vector.tensor_scalar(tn[:], ph[:], 0.15915494309189535, ROUND, ALU.mult, ALU.add))
            ch.then(nc.vector.tensor_scalar(tn[:], tn[:], ROUND, None, ALU.subtract))
            ch.then(nc.vector.scalar_tensor_tensor(out=ph[:], in0=tn[:], scalar=-TWO_PI_HI, in1=ph[:],
                                                   op0=ALU.mult, op1=ALU.add))
            ch.then(nc.vector.scalar_tensor_tensor(out=ph[:], in0=tn[:], scalar=-TWO_PI_LO, in1=ph[:],
                                                   op0=ALU.mult, op1=ALU.add))
            ch.then(nc.vector.tensor_scalar(ph[:], ph[:], 3.1415925, -3.1415925, ALU.min, ALU.max))
            dve.sem_inc(phase_ready, 1)
            dve.wait_ge(half_ready, 2)
            ch.then(nc.vector.tensor_tensor(tn[:], hs[:], hs[:], ALU.mult))
            ch.then(nc.vector.tensor_scalar(cos_t, tn[:], -2.0, 1.0, ALU.mult, ALU.add))
            ch.then(nc.vector.tensor_scalar(sin_t, sin_t, w["sign"], None, ALU.mult))
            dve.wait_ge(mag_ready, 1)
            ch.then(nc.vector.tensor_scalar(decay, w["inner"], mag[:], None, ALU.mult))

        @block.scalar
        def _(act):
            nc.scalar.activation(mag[:], w["log_decay"], ACT.Sigmoid).then_inc(mag_ready, 1)
            act.wait_ge(phase_ready, 1)
            nc.scalar.activation(sin_t, ph[:], ACT.Sin).then_inc(half_ready, 1)
            nc.scalar.activation(hs[:], ph[:], ACT.Sin, scale=0.5).then_inc(half_ready, 1)


def eigen_mixer(nc, w, xnn, xn, x1, cos_t, sin_t, decay, wa, wb):
    G = 2
    with ExitStack() as ctx:
        def sb(name, shape):
            return ctx.enter_context(nc.sbuf_tensor(name, shape, F32))

        ps_in = ctx.enter_context(nc.psum_tensor("em_in", [P, G, 3, TILE], F32))
        ps_h = ctx.enter_context(nc.psum_tensor("em_h", [P, G, TILE], F32))
        ta, tb = sb("em_ta", [P, G, TILE]), sb("em_tb", [P, G, TILE])
        z = sb("em_z", [P, G, TILE])
        zc, zs = sb("em_zc", [P, G, TILE]), sb("em_zs", [P, G, TILE])
        gate = sb("em_gate", [P, G, TILE])
        block, in_ready, beta_used, gate_ready, z_ready, h_ready, chain, done = ctx.enter_context(
            phase(nc, "in_ready beta_used gate_ready z_ready h_ready chain done"))
        cosb = cos_t.unsqueeze(1).broadcast_to([P, TILE // CH, CH])
        sinb = sin_t.unsqueeze(1).broadcast_to([P, TILE // CH, CH])

        def chunks(ap):
            return ap.rearrange("p (c j) -> p c j", j=CH)

        @block.tensor
        def _(pe):
            with pe.Fori(0, NT // G) as i:
                for j in range(G):
                    pe.wait_ge(beta_used, i * G + j + 1)
                    pe.wait_ge(gate_ready, i * G + j + 1)
                    for n, name in enumerate(("w_inT", "w_inT_sw", "w_gateT")):
                        nc.tensor.matmul(ps_in[:, j, n], w[name], xnn[:, tile(i * G + j)],
                                         start=True, stop=True).then_inc(in_ready, 1)
                for j in range(G):
                    pe.wait_ge(z_ready, i * G + j + 1)
                    pe.wait_ge(done, i * G + j + 1)
                    nc.tensor.matmul(ps_h[:, j], wa, zc[:, j], start=True, stop=False)
                    nc.tensor.matmul(ps_h[:, j], wb, zs[:, j], start=False, stop=True).then_inc(h_ready, 1)

        @block.scalar
        def _(act):
            act.sem_inc(gate_ready, G)
            with act.Fori(0, NT // G) as i:
                for j in range(G):
                    act.wait_ge(in_ready, (i * G + j + 1) * 3)
                    act.wait_ge(done, i * G + j + 1)
                    nc.scalar.activation(gate[:, j], ps_in[:, j, 2], ACT.Sigmoid, bias=w["b_gate"]).then_inc(gate_ready, 1)

        @block.vector
        def _(dve):
            dve.sem_inc(beta_used, G)
            dve.sem_inc(done, G)
            with dve.Fori(0, NT // G) as i:
                m = Marks(dve, chain, i * (G * 7))
                for j in range(G):
                    dve.wait_ge(in_ready, (i * G + j) * 3 + 2)
                    m.mark(("a", j), nc.vector.tensor_tensor(chunks(ta[:, j]), chunks(ps_in[:, j, 0]), cosb, ALU.mult))
                    m.mark(("b", j), nc.vector.tensor_tensor(chunks(tb[:, j]), chunks(ps_in[:, j, 1]), sinb, ALU.mult))
                for j in range(G):
                    m.need(("b", j))
                    m.mark(("r", j), nc.vector.tensor_tensor(ta[:, j], ta[:, j], tb[:, j], ALU.add))
                for j in range(G):
                    m.need(("r", j))
                    m.mark(("z", j), nc.vector.tensor_tensor_scan(z[:, j, ::-1], decay, ta[:, j, ::-1], 0.0,
                                                                  ALU.mult, ALU.add))
                for j in range(G):
                    m.need(("z", j))
                    zv = z[:, j].rearrange("p (r c j) -> p r c j", r=TILE // T, j=CH)
                    bv = ps_in[:, j, 0].rearrange("p (r c j) -> p r c j", r=TILE // T, j=CH)
                    m.mark(("y", j), nc.vector.tensor_tensor(zv[:, :, 1:, 0], zv[:, :, 1:, 0], bv[:, :, :-1, CH - 1],
                                                             ALU.add))
                for j in range(G):
                    m.need(("y", j))
                    dve.sem_inc(beta_used, 1)
                    m.mark(("c", j), nc.vector.tensor_tensor(chunks(zc[:, j]), chunks(z[:, j]), cosb, ALU.mult))
                    nc.vector.tensor_tensor(chunks(zs[:, j]), chunks(z[:, j]), sinb, ALU.mult).then_inc(z_ready, 1)
                for j in range(G):
                    dve.wait_ge(h_ready, i * G + j + 1)
                    dve.wait_ge(gate_ready, i * G + j + G + 1)
                    m.mark(("g", j), nc.vector.tensor_tensor(gate[:, j], gate[:, j], ps_h[:, j], ALU.mult))
                for j in range(G):
                    m.need(("g", j))
                    at = tile(i * G + j)
                    nc.vector.tensor_tensor(x1[:, at], gate[:, j], xn[:, at], ALU.add).then_inc(done, 1)


def silu_mlp(nc, tag, w_up, b_up, w_down, b_down, x_in, x1):
    M = 4
    K = U * M
    with ExitStack() as ctx:
        up = ctx.enter_context(nc.psum_tensor(tag + "_up", [P, 4, TILE], F32))
        down = ctx.enter_context(nc.psum_tensor(tag + "_down", [P, 2, TILE], F32))
        h = ctx.enter_context(nc.sbuf_tensor(tag + "_h", [P, 4, TILE], F32))
        block, up_ready, h_ready, down_ready, done = ctx.enter_context(
            phase(nc, "up_ready h_ready down_ready done"))

        @block.tensor
        def _(pe):
            with pe.Fori(0, NT // U) as i:
                for n in range(K + LAG):
                    if n < K:
                        pe.wait_ge(h_ready, i * K + n + 1)
                        nc.tensor.matmul(up[:, n % 4], w_up[:, (n % M) * P:(n % M + 1) * P], x_in[:, tile(i * U + n // M)],
                                         start=True, stop=True).then_inc(up_ready, 1)
                    m = n - LAG
                    if m >= 0:
                        pe.wait_ge(h_ready, i * K + m + 5)
                        if m % M == 0:
                            pe.wait_ge(done, i * U + m // M + 1)
                        nc.tensor.matmul(down[:, m // M % 2], w_down[:, m % M], h[:, m % 4],
                                         start=m % M == 0, stop=m % M == M - 1).then_inc(down_ready, 1)

        @block.scalar
        def _(act):
            act.sem_inc(h_ready, 4)
            act.sem_inc(down_ready, 4)
            with act.Fori(0, NT // U) as i:
                for n in range(K):
                    act.wait_ge(up_ready, i * K + n + 1)
                    act.wait_ge(down_ready, i * K + n + 1)
                    nc.scalar.activation(h[:, n % 4], up[:, n % 4], ACT.Silu,
                                         bias=b_up[:, n % M:n % M + 1]).then_inc(h_ready, 1)

        @block.vector
        def _(dve):
            dve.sem_inc(done, 2)
            with dve.Fori(0, NT // U) as i:
                for j in range(U):
                    dve.wait_ge(down_ready, (i * U + j + 1) * M + 4)
                    at = tile(i * U + j)
                    nc.vector.scalar_tensor_tensor(out=x1[:, at], in0=down[:, j % 2], scalar=b_down, in1=x1[:, at],
                                                   op0=ALU.add, op1=ALU.add).then_inc(done, 1)


E8 = 8
NBLK = N // P


def route(nc, tag, w, router, x_in, topk, capacity, slots, x_slots, weight=None):
    with ExitStack() as ctx:
        def sb(name, shape, dt=F32):
            return ctx.enter_context(nc.sbuf_tensor(tag + name, shape, dt))

        ps_l = ctx.enter_context(nc.psum_tensor(tag + "_psl", [P, NBLK, E8], F32))
        ps_c = ctx.enter_context(nc.psum_tensor(tag + "_psc", [P, NBLK, E8], F32))
        ps_t = ctx.enter_context(nc.psum_tensor(tag + "_pst", [P, NBLK, E8], F32))
        sc = sb("sc", [P, NBLK, E8])
        t1 = sb("t1", [P, NBLK, E8])
        mask = sb("mask", [P, NBLK, E8])
        run = sb("run", [P, NBLK, E8])
        tot = sb("tot", [P, NBLK, E8])
        mx = sb("mx", [P, NBLK])
        ix = sb("ix", [P, NBLK])
        block, logits, chain, exp_in, exp_done, mask_ready, counted, zeroed, filled = ctx.enter_context(
            phase(nc, "logits chain exp_in exp_done mask_ready counted zeroed filled"))
        n_slots = E8 * topk * capacity

        def over_e(ap):
            return ap.unsqueeze(2).broadcast_to([P, NBLK, E8])

        iota = w["iota8"].unsqueeze(1).broadcast_to([P, NBLK, E8])

        @block.tensor
        def _(pe):
            for b in range(NBLK):
                last = nc.tensor.matmul(ps_l[:, b], x_in[:, b * P:(b + 1) * P], router, start=True, stop=True)
            last.then_inc(logits, 1)
            for k in range(topk):
                pe.wait_ge(mask_ready, k + 1)
                flat = mask[:].rearrange("p b e -> p (b e)")
                nc.tensor.matmul(ps_c[:].rearrange("p b e -> p (b e)"), w["tri"], flat, start=True, stop=True)
                nc.tensor.matmul(ps_t[:].rearrange("p b e -> p (b e)"), w["ones"], flat, start=True, stop=True)\
                    .then_inc(counted, 1)

        zeros = sb("zeros", [P, 16 * P])

        @block.gpsimd
        def _(pool):
            nc.gpsimd.memset(zeros[:], 0.0).then_inc(zeroed, 1)

        @block.sync
        def _(sp):
            sp.wait_ge(zeroed, 1)
            out = x_slots.rearrange("(i p s) c -> p i (s c)", p=P, s=16)
            for i in range(n_slots // (16 * P)):
                sp.dma_start(out[:, i], zeros[:]).then_inc(filled, 16)
            sp.wait_ge(filled, n_slots // (16 * P) * 16)

        @block.scalar
        def _(act):
            act.wait_ge(exp_in, 1)
            nc.scalar.activation(sc[:], t1[:], ACT.Exp).then_inc(exp_done, 1)

        @block.vector
        def _(dve):
            ch = Chain(dve, chain)
            V = nc.vector
            dve.wait_ge(logits, 1)
            ch.then(V.tensor_reduce(mx[:], ps_l[:], AX, ALU.max))
            ch.then(V.tensor_tensor(t1[:], ps_l[:], over_e(mx[:]), ALU.subtract))
            dve.sem_inc(exp_in, 1)
            dve.wait_ge(exp_done, 1)
            ch.then(V.tensor_reduce(mx[:], sc[:], AX, ALU.add))
            ch.then(V.reciprocal(mx[:], mx[:]))
            ch.then(V.tensor_tensor(sc[:], sc[:], over_e(mx[:]), ALU.mult))
            for k in range(topk):
                ch.then(V.tensor_reduce(mx[:], sc[:], AX, ALU.max))
                ch.then(V.tensor_tensor(t1[:], sc[:], over_e(mx[:]), ALU.is_equal))
                ch.then(V.tensor_tensor(t1[:], t1[:], iota, ALU.mult))
                ch.then(V.tensor_reduce(ix[:], t1[:], AX, ALU.min))
                ch.then(V.tensor_tensor(mask[:], iota, over_e(ix[:]), ALU.is_equal))
                dve.sem_inc(mask_ready, 1)
                dve.wait_ge(counted, k + 1)
                ch.then(V.tensor_copy(tot[:], ps_t[:]))
                for e in range(E8):
                    ch.then(V.tensor_tensor_scan(run[:, :, e], w["ones"][:, 0:NBLK], tot[:, :, e], 0.0,
                                                 ALU.mult, ALU.add))
                ch.then(V.tensor_tensor(run[:], run[:], tot[:], ALU.subtract))
                ch.then(V.tensor_tensor(run[:], run[:], ps_c[:], ALU.add))
                two = (lambda ap: ap.rearrange("p b e -> p (b e)"))
                ch.then(V.tensor_scalar(two(t1[:]), two(run[:]), float(capacity), float(4 * n_slots), ALU.is_gt, ALU.mult))
                ch.then(V.tensor_tensor(run[:], run[:], t1[:], ALU.add))
                ch.then(V.scalar_tensor_tensor(out=run[:], in0=iota, scalar=float(topk * capacity), in1=run[:],
                                               op0=ALU.mult, op1=ALU.add))
                ch.then(V.tensor_tensor(run[:], run[:], mask[:], ALU.mult))
                ch.then(V.tensor_reduce(ix[:], run[:], AX, ALU.add))
                ch.then(V.tensor_scalar(ix[:], ix[:], float(n_slots + k * capacity - 1), None, ALU.add))
                ch.then(V.tensor_copy(slots[:, k * NBLK:(k + 1) * NBLK], ix[:]))
                if weight is not None:
                    ch.then(V.tensor_copy(weight[:, k * NBLK:(k + 1) * NBLK], mx[:]))
                if k + 1 < topk:
                    ch.then(V.scalar_tensor_tensor(out=two(sc[:]), in0=two(mask[:]), scalar=-2.0, in1=two(sc[:]),
                                                   op0=ALU.mult, op1=ALU.add))


def dispatch(nc, tag, w, x_in, tok, slots, x_slots):
    with ExitStack() as ctx:
        ps = ctx.enter_context(nc.psum_tensor(tag + "_ps", [P, 4, 4, P], F32))
        block, turned, copied, sent = ctx.enter_context(phase(nc, "turned copied sent"))
        choices = slots.shape[1] // NBLK
        last_slot = x_slots.shape[0] - 1

        @block.tensor
        def _(pe):
            for b in range(NBLK):
                if b % 4 == 0 and b >= 16:
                    pe.wait_ge(copied, b // 4 - 3)
                mm = nc.tensor.transpose(ps[:, b // 4 % 4, b % 4], x_in[:, b * P:(b + 1) * P], w["eye"])
                if b % 4 == 3:
                    mm.then_inc(turned, 1)

        @block.vector
        def _(dve):
            for g in range(NBLK // 4):
                dve.wait_ge(turned, g + 1)
                nc.vector.tensor_copy(tok[:, g * 4:g * 4 + 4], ps[:, g % 4]).then_inc(copied, 1)

        @block.gpsimd
        def _(pool):
            for b in range(NBLK):
                pool.wait_ge(copied, b // 4 + 1)
                for k in range(choices):
                    at = slots[:, k * NBLK + b:k * NBLK + b + 1]
                    nc.gpsimd.indirect_dma_start(x_slots, bass.IndirectOffsetOnAxis(ap=at, axis=0), tok[:, b], None,
                                                 bounds_check=last_slot, oob_is_err=False).then_inc(sent, 16)
            pool.wait_ge(sent, choices * NBLK * 16)


def experts_gelu(nc, w1, w2, eye, x_slots, y_slots):
    M = 4
    TPE = x_slots.shape[0] // (E8 * TILE)
    with ExitStack() as ctx:
        def sb(name, shape, dt=F32):
            return ctx.enter_context(nc.sbuf_tensor("xg_" + name, shape, dt))

        up = ctx.enter_context(nc.psum_tensor("xg_up", [P, M, TILE], F32))
        turn = ctx.enter_context(nc.psum_tensor("xg_turn", [P, TILE], F32))
        down = ctx.enter_context(nc.psum_tensor("xg_down", [P, 2, 4, P], F32))
        xg = sb("xg", [P, 4, 4, P])
        xf = sb("xf", [P, 2, TILE])
        h = sb("h", [P, 2, M, TILE])
        yo = sb("yo", [P, 2, 4, P])
        (block, turned, xf_ready, up_ready, gelu_ready, down_ready, y_ready, *rings) = ctx.enter_context(phase(
            nc, "turned xf_ready up_ready gelu_ready down_ready y_ready x_in0 x_in1 x_in2 x_in3 y_out0 y_out1"))
        x_in, y_out = rings[:4], rings[4:]
        xs_v = x_slots.rearrange("(v p s) c -> p v (s c)", p=P, s=4)
        ys_v = y_slots.rearrange("(v p s) c -> p v (s c)", p=P, s=4)

        @block.sync
        def _(sp):
            with sp.Fori(0, TPE) as i:
                for e in range(E8):
                    sp.wait_ge(turned, i * E8 + e + 1)
                    sp.dma_start(xg[:, e % 4].rearrange("p s c -> p (s c)"),
                                 xs_v[:, bass.ds(i + e * TPE, 1)].rearrange("p v c -> p (v c)")).then_inc(x_in[e % 4], 16)

        @block.gpsimd
        def _(pool):
            with pool.Fori(0, TPE) as i:
                for e in range(E8):
                    pool.wait_ge(y_ready, i * E8 + e + 1)
                    pool.dma_start(ys_v[:, bass.ds(i + e * TPE, 1)].rearrange("p v c -> p (v c)"),
                                   yo[:, e % 2].rearrange("p s c -> p (s c)")).then_inc(y_out[e % 2], 16)
            for n in range(2):
                pool.wait_ge(y_out[n], TPE * E8 // 2 * 16)

        @block.tensor
        def _(pe):
            def turn_tile(i, e):
                pe.wait_ge(x_in[e % 4], i * 32 + e // 4 * 16 + 16)
                pe.wait_ge(xf_ready, i * E8 + e)
                for s in range(4):
                    mm = nc.tensor.transpose(turn[:, s * P:(s + 1) * P], xg[:, e % 4, s], eye)
                mm.then_inc(turned, 1)

            def product(i, e):
                pe.wait_ge(gelu_ready, (i * E8 + e + 1) * M + 4)
                pe.wait_ge(y_ready, i * E8 + e - 1) if e >= 2 else pe.wait_ge(y_ready, i * E8)
                for s in range(4):
                    for m in range(M):
                        mm = nc.tensor.matmul(down[:, e % 2, s], h[:, e % 2, m, s * P:(s + 1) * P], w2[:, e * M + m],
                                              start=m == 0, stop=m == M - 1)
                mm.then_inc(down_ready, 1)

            with pe.Fori(0, TPE) as i:
                turn_tile(i, 0)
                for e in range(E8):
                    pe.wait_ge(xf_ready, i * E8 + e + 1)
                    for m in range(M):
                        pe.wait_ge(gelu_ready, (i * E8 + e) * M + m + 1)
                        nc.tensor.matmul(up[:, m], w1[:, (e * M + m) * P:(e * M + m + 1) * P], xf[:, e % 2],
                                         start=True, stop=True).then_inc(up_ready, 1)
                    if e + 1 < E8:
                        turn_tile(i, e + 1)
                    if e:
                        product(i, e - 1)
                product(i, E8 - 1)

        @block.scalar
        def _(act):
            act.sem_inc(gelu_ready, 4)
            act.sem_inc(down_ready, 2)
            with act.Fori(0, TPE) as i:
                for e in range(E8):
                    act.wait_ge(down_ready, i * E8 + e + 1)
                    for m in range(M):
                        act.wait_ge(up_ready, (i * E8 + e) * M + m + 1)
                        nc.scalar.activation(h[:, e % 2, m], up[:, m], ACT.Gelu_apprx_tanh).then_inc(gelu_ready, 1)

        @block.vector
        def _(dve):
            V = nc.vector
            dve.sem_inc(turned, 4)

            def copy_x(i, e):
                dve.wait_ge(turned, i * E8 + e + 5)
                V.tensor_copy(xf[:, e % 2], turn[:]).then_inc(xf_ready, 1)

            def copy_y(i, e):
                dve.wait_ge(down_ready, i * E8 + e + 3)
                dve.wait_ge(y_out[e % 2], i * 64 + e // 2 * 16)
                V.tensor_copy(yo[:, e % 2], down[:, e % 2]).then_inc(y_ready, 1)

            with dve.Fori(0, TPE) as i:
                copy_x(i, 0)
                for e in range(E8):
                    if e + 1 < E8:
                        copy_x(i, e + 1)
                    if e:
                        copy_y(i, e - 1)
                copy_y(i, E8 - 1)


def collect_gated(nc, w, y_slots, slots, weight, tok0, tok1, s, x):
    with ExitStack() as ctx:
        ps = ctx.enter_context(nc.psum_tensor("cg_ps", [P, 4, 4, P], F32))
        g = ctx.enter_context(nc.sbuf_tensor("cg_g", [P, 2, TILE], F32))
        names = " ".join(f"fetched{n}" for n in range(NBLK // 4))
        block, zeroed, chain, summed, turned, silu_ready, done, *fetched = ctx.enter_context(
            phase(nc, "zeroed chain summed turned silu_ready done " + names))
        last_slot = y_slots.shape[0] - 1

        @block.gpsimd
        def _(pool):
            pool.wait_ge(zeroed, 2)
            for b in range(NBLK):
                for k, tok in enumerate((tok0, tok1)):
                    at = slots[:, k * NBLK + b:k * NBLK + b + 1]
                    nc.gpsimd.indirect_dma_start(tok[:, b], None, y_slots, bass.IndirectOffsetOnAxis(ap=at, axis=0),
                                                 bounds_check=last_slot, oob_is_err=False).then_inc(fetched[b // 4], 16)

        @block.tensor
        def _(pe):
            for n in range(NBLK // 4):
                pe.wait_ge(summed, n + 1)
                if n >= 4:
                    pe.wait_ge(silu_ready, n - 3)
                for b in range(4):
                    mm = nc.tensor.transpose(ps[:, n % 4, b], tok0[:, n * 4 + b], w["eye"])
                mm.then_inc(turned, 1)

        @block.scalar
        def _(act):
            for n in range(NBLK // 4):
                act.wait_ge(turned, n + 1)
                if n >= 2:
                    act.wait_ge(done, n - 1)
                nc.scalar.activation(g[:, n % 2], ps[:, n % 4].rearrange("p b c -> p (b c)"), ACT.Silu,
                                     bias=w["moe_bias"]).then_inc(silu_ready, 1)

        @block.vector
        def _(dve):
            V = nc.vector
            ch = Chain(dve, chain)
            for tok in (tok0, tok1):
                V.memset(tok.rearrange("p b c -> p (b c)"), 0.0).then_inc(zeroed, 1)

            def finish(n):
                at = slice(n * TILE, (n + 1) * TILE)
                dve.wait_ge(silu_ready, n + 1)
                ch.then(V.tensor_tensor(g[:, n % 2], g[:, n % 2], s[:, at], ALU.mult))
                V.tensor_tensor(x[:, at], x[:, at], g[:, n % 2], ALU.add).then_inc(done, 1)

            for n in range(NBLK // 4):
                dve.wait_ge(fetched[n], 2 * 4 * 16)
                bs = slice(n * 4, n * 4 + 4)
                for k, tok in enumerate((tok0, tok1)):
                    by = weight[:, k * NBLK + n * 4:k * NBLK + n * 4 + 4].unsqueeze(2).broadcast_to([P, 4, P])
                    ch.then(V.tensor_tensor(tok[:, bs], tok[:, bs], by, ALU.mult))
                V.tensor_tensor(tok0[:, bs], tok0[:, bs], tok1[:, bs], ALU.add).then_inc(summed, 1)
                if n:
                    finish(n - 1)
            finish(NBLK // 4 - 1)


def layer1(nc, w0, groups, x, xn, s, x_slots, y_slots):
    layernorm(nc, "ln1", x, xn, w0)
    with ExitStack() as ctx:
        w = ctx.enter_context(weights(nc, groups, "l1", w0))

        def sb(name, shape, dt=F32):
            return ctx.enter_context(nc.sbuf_tensor("l1_" + name, shape, dt))

        xnn = sb("xnn", [P, N])
        cos_t, sin_t, decay = sb("cos", [P, CH]), sb("sin", [P, CH]), sb("decay", [P, TILE])
        wa, wb = sb("wa", [P, P]), sb("wb", [P, P])
        eigen_tables(nc, w, cos_t[:], sin_t[:], decay[:], wa[:], wb[:])
        layernorm(nc, "ln1a", xn, xnn, w, w["ln1_g"], w["ln1_b"])
        eigen_mixer(nc, w, xnn, xn, s, cos_t[:], sin_t[:], decay[:], wa[:], wb[:])
        layernorm(nc, "ln1b", s, xnn, w, w["ln2_g"], w["ln2_b"])
        silu_mlp(nc, "m1", w["w_mlp1T"], w["b_mlp1"], w["w_mlp2T"].rearrange("p (m c) -> p m c", m=4), w["b_mlp2"],
                 xnn, s)
    with ExitStack() as ctx:
        w = ctx.enter_context(weights(nc, groups, "route", w0))
        w = ctx.enter_context(weights(nc, groups, "experts1", w))
        slots = ctx.enter_context(nc.sbuf_tensor("l1_slots", [P, 2 * NBLK], mybir.dt.uint32))
        weight = ctx.enter_context(nc.sbuf_tensor("l1_weight", [P, 2 * NBLK], F32))
        tok = ctx.enter_context(nc.sbuf_tensor("l1_tok", [P, NBLK, P], F32))
        w2 = w["w2"].rearrange("p (m c) -> p m c", c=P)
        route(nc, "r1", w, w["router"], xn, 2, N // E8, slots, x_slots, weight)
        dispatch(nc, "ds1", w, xn, tok, slots, x_slots)
        experts_gelu(nc, w["w1"], w2, w["eye"], x_slots, y_slots)
        collect_gated(nc, w, y_slots, slots, weight, tok, xn.rearrange("p (b c) -> p b c", c=P), s, x)



DI = 2 * P
NSTATE = 16
TAPS = 4
PAD = TAPS - 1
TP = T + PAD
RT = TILE // T
SG = 2
GROUPS = NSTATE // SG
RING = 4
UNITS = 2 * GROUPS


def padded(ap):
    return ap[:, 0:B * TP].rearrange("p (b t) -> p b t", t=TP)


def padded_tile(ap, shift=PAD):
    return lambda i: padded(ap)[:, bass.ds(i * RT, RT), shift:shift + T]


def rows(ap):
    return ap.rearrange("p (r t) -> p r t", t=T)


def mamba_weights(nc, w, once, l3, hp, wconv, a_neg, diag_y, diag_d, sel, conv_bias, corr):
    with ExitStack() as ctx:
        raw = ctx.enter_context(nc.sbuf_tensor(f"mw{3 if l3 else 2}_raw", [P, TAPS * DI + 2 * NSTATE * P], F32))
        block, chain, a_exp, ready, raw_ready = ctx.enter_context(phase(nc, "chain a_exp ready raw_ready"))
        safe = ctx.enter_context(nc.sbuf_tensor(f"mw{3 if l3 else 2}_safe", [P, 2, 2 * NSTATE], F32))
        tmp = ctx.enter_context(nc.sbuf_tensor(f"mw{3 if l3 else 2}_tmp", [P, 2 * TAPS], F32))

        @block.sync
        def _(sp):
            sp.dma_start(raw[:], once).then_inc(raw_ready, 16)

        @block.gpsimd
        def _(pool):
            nc.gpsimd.memset(padded(hp)[:, :, 0:PAD], 0.0).then_inc(ready, 1)
            pool.wait_ge(ready, 1)

        @block.scalar
        def _(act):
            nc.scalar.activation(a_neg, w["A_log"], ACT.Exp).then_inc(a_exp, 1)

        @block.vector
        def _(dve):
            V = nc.vector
            ch = Chain(dve, chain)
            dve.wait_ge(raw_ready, 16)
            ch.then(V.tensor_copy(sel.rearrange("p s c -> p (s c)"), raw[:, TAPS * DI:]))
            for k in range(TAPS):
                ch.then(V.tensor_tensor(wconv[:, k], w["in_w"][:, 0:DI], raw[:, k * DI:(k + 1) * DI], ALU.mult))
            for h in range(2):
                ch.then(V.tensor_scalar(diag_d[:, h], w["eye"], w["D"][:, h:h + 1], None, ALU.mult))
            dve.wait_ge(a_exp, 1)
            ch.then(V.tensor_scalar(a_neg, a_neg, -1.0, None, ALU.mult))
            if l3:
                small, inv = safe[:, 0], safe[:, 1]
                ch.then(V.tensor_scalar(small, a_neg, -1e-6, None, ALU.is_gt))
                ch.then(V.tensor_scalar(inv, small, -1.0, 1.0, ALU.mult, ALU.add))
                ch.then(V.tensor_tensor(inv, inv, a_neg, ALU.mult))
                ch.then(V.tensor_tensor(inv, inv, small, ALU.add))
                ch.then(V.reciprocal(inv, inv))
                for n in range(2 * NSTATE):
                    ch.then(V.tensor_scalar(diag_y[:, n], w["eye"], inv[:, n:n + 1], None, ALU.mult))
                for h in range(2):
                    bw = tmp[:, h * TAPS:(h + 1) * TAPS]
                    ch.then(V.tensor_scalar(bw, w["conv_cols"][:, h * TAPS:(h + 1) * TAPS], w["in_b"][:, h:h + 1], None,
                                            ALU.mult))
                    for k in range(1, TAPS):
                        ch.then(V.tensor_tensor(bw[:, k:k + 1], bw[:, k:k + 1], bw[:, k - 1:k], ALU.add))
                    ch.then(V.tensor_tensor(conv_bias[:, h:h + 1], w["conv_b"][:, h:h + 1], bw[:, TAPS - 1:TAPS], ALU.add))
                    for t in range(PAD):
                        ch.then(V.tensor_scalar(corr[:, h, t:t + 1], bw[:, PAD - 1 - t:PAD - t], -1.0, None, ALU.mult))
            else:
                ch.then(V.tensor_copy(conv_bias, w["conv_b"]))


def mamba(nc, w, once, l3, hp, res, out):
    with ExitStack() as ctx:
        def sb(name, shape, dt=F32):
            return ctx.enter_context(nc.sbuf_tensor(("m3_" if l3 else "m2_") + name, shape, dt))

        wconv = sb("wconv", [P, TAPS, DI])
        a_neg = sb("a_neg", [P, 2 * NSTATE])
        diag_y = sb("diag_y", [P, 2 * NSTATE, P]) if l3 else None
        diag_d = sb("diag_d", [P, 2, P])
        sel = sb("sel", [P, 2 * NSTATE, P], BF16)
        conv_bias = sb("conv_bias", [P, 2])
        corr = sb("corr", [P, 2, PAD])
        mamba_weights(nc, w, once, l3, hp, wconv[:], a_neg[:], diag_y, diag_d, sel[:], conv_bias[:], corr)

        ps_b = ctx.enter_context(nc.psum_tensor(f"mb{3 if l3 else 2}_b", [P, SG, TILE], F32))
        ps_c = ctx.enter_context(nc.psum_tensor(f"mb{3 if l3 else 2}_c", [P, SG, TILE], F32))
        ps_y = ctx.enter_context(nc.psum_tensor(f"mb{3 if l3 else 2}_y", [P, 2, TILE], F32))
        ps_w = ctx.enter_context(nc.psum_tensor(f"mb{3 if l3 else 2}_w", [P, 2, TILE], F32))
        xs = sb("xs", [P, 2, 2, TILE])
        sg = sb("sg", [P, 2, 2, TILE])
        dt = sb("dt", [P, 2, 2, TILE])
        dtx = xs if l3 else sb("dtx", [P, 2, 2, TILE])
        bct = sb("bct", [P, 2, TILE], BF16)
        rest = sb("rest", [P, TILE])
        bcf = sb("bcf", [P, TILE])
        low = sb("low", [64, TILE]) if l3 else bcf
        sp = sb("sp", [P, 2, TILE])
        lin = sb("lin", [P, TILE])
        bsb = sb("bsb", [P, 2, SG, TILE])
        csb = sb("csb", [P, 2, SG, TILE])
        da = sb("da", [P, RING, SG, TILE])
        u = sb("u", [P, RING, SG, TILE])
        hs = sb("hs", [P, 2, SG, TILE])
        hc = sb("hc", [P, 2, SG, TILE])
        yg = sb("yg", [P, 2, TILE])
        (block, xs_in, xs_fixed, xs_ready, gate_in, sg_ready, bc_in, bc_split, low_in, bcf_ready, low_ready, dt_in, sp_step,
         sp_ready, dt_ready, dtx_ready, b_ready, c_ready, bsb_ready, csb_ready, da_ready, u_ready, h_ready,
         hc_ready, y_used, made, yg_ready, out_ready, x_done, chain) = ctx.enter_context(phase(
             nc, "xs_in xs_fixed xs_ready gate_in sg_ready bc_in bc_split low_in bcf_ready low_ready dt_in sp_step sp_ready "
             "dt_ready dtx_ready b_ready c_ready bsb_ready csb_ready da_ready u_ready h_ready hc_ready y_used "
             "made yg_ready out_ready x_done chain"))
        out_bank = 0 if l3 else 1

        @block.tensor
        def _(pe):
            def stage_a(a, first):
                def conv(h):
                    def run():
                        if not first:
                            if (h == 0) == (not l3):
                                pe.wait_ge(dt_ready, 2 * a)
                            else:
                                pe.wait_ge(x_done, a - 1)
                        for k in range(TAPS):
                            mm = nc.tensor.matmul(ps_w[:, h], wconv[:, k, h * P:(h + 1) * P], padded_tile(hp, k)(a),
                                                  start=k == 0, stop=k == TAPS - 1)
                        mm.then_inc(xs_in, 1)
                    return run

                def gate(h):
                    def run():
                        pe.wait_ge(xs_ready, 2 * a + 1 + h)
                        nc.tensor.matmul(ps_w[:, h], w["in_w"][:, DI + h * P:DI + (h + 1) * P], padded_tile(hp)(a),
                                         start=True, stop=True).then_inc(gate_in, 1)
                    return run

                def project(bank, name, rows_out, sem, par):
                    def run():
                        pe.wait_ge(sg_ready, 2 * a + 1 + bank)
                        for h in range(2):
                            mm = nc.tensor.matmul(ps_w[0:rows_out, bank], w[name][:, h * rows_out:(h + 1) * rows_out],
                                                  xs[:, par, h], start=h == 0, stop=h == 1)
                        mm.then_inc(sem, 1)
                    return run

                def step_size(h):
                    bank = h if l3 else 1 - h
                    K = 64 if l3 else NSTATE

                    def run():
                        pe.wait_ge(low_ready, a + 1)
                        if bank == 1 and not l3:
                            pe.wait_ge(sg_ready, 2 * a + 2)
                        nc.tensor.matmul(ps_w[:, bank], w["dt_w"][0:K, h * P:(h + 1) * P], low[0:K],
                                         start=True, stop=True).then_inc(dt_in, 1)
                    return run
                return conv, gate, project, step_size

            def pieces(a, par, first=False):
                conv, gate, project, step_size = stage_a(a, first)
                third = [project(0, "xp_bc", P, bc_in, par)] + ([project(1, "xp_low", 64, low_in, par)] if l3 else [])
                return {1: [conv(0), conv(1)], 2: [gate(0), gate(1)], 3: third, 5: [step_size(0), step_size(1)]}

            def spread_b(i, par, g):
                pe.wait_ge(bc_split, i + 1)
                pe.wait_ge(bsb_ready, i * GROUPS + g)
                for s in range(SG):
                    mm = nc.tensor.matmul(ps_b[:, s], sel[:, g * SG + s], bct[:, par], start=True, stop=True)
                mm.then_inc(b_ready, 1)

            def spread_c(i, par, g):
                pe.wait_ge(csb_ready, i * GROUPS + g)
                for s in range(SG):
                    mm = nc.tensor.matmul(ps_c[:, s], sel[:, NSTATE + g * SG + s], bct[:, par], start=True, stop=True)
                mm.then_inc(c_ready, 1)

            def spread(i, par, g):
                spread_b(i, par, g)
                spread_c(i, par, g)

            def sum_states(i, par, g, h):
                pe.wait_ge(hc_ready, i * UNITS + g * 2 + h + 5)
                for s in range(SG):
                    weight = diag_y[:, h * NSTATE + g * SG + s] if l3 else w["eye"]
                    mm = nc.tensor.matmul(ps_y[:, h], weight, hc[:, h, s], start=False, stop=g == GROUPS - 1 and s == SG - 1)
                mm.then_inc(y_used, 1)

            def project_out(i, before_next):
                pe.wait_ge(yg_ready, 2 * i + 2)
                if before_next:
                    pe.wait_ge(dt_ready, 2 * i + 3)
                else:
                    pe.wait_ge(x_done, i)
                for h in range(2):
                    mm = nc.tensor.matmul(ps_w[:, out_bank], w["out_w"][:, h * P:(h + 1) * P], yg[:, h],
                                          start=h == 0, stop=h == 1)
                mm.then_inc(out_ready, 1)

            def step(i, par, first, more):
                ahead = pieces(i + 1, 1 - par) if more else {}
                for g in range(GROUPS):
                    if g + 2 < GROUPS:
                        spread(i, par, g + 2)
                    elif more:
                        spread(i + 1, 1 - par, g + 2 - GROUPS)
                    if g == 0:
                        if not first:
                            project_out(i - 1, True)
                        for h in range(2):
                            nc.tensor.matmul(ps_y[:, h], diag_d[:, h], xs[:, par, h], start=True, stop=False)
                    for piece in ahead.get(g, []):
                        piece()
                    sum_states(i, par, g, 0)
                    sum_states(i, par, g, 1)

            for group in pieces(0, 0, True).values():
                for piece in group:
                    piece()
            spread(0, 0, 0)
            spread(0, 0, 1)
            step(0, 0, True, True)
            with pe.Fori(0, NT // 2 - 1) as ii:
                step(ii * 2 + 1, 1, False, True)
                step(ii * 2 + 2, 0, False, True)
            step(NT - 1, 1, False, False)
            project_out(NT - 1, False)

        @block.scalar
        def _(act):
            def pieces(a, par):
                def silu_xs(h):
                    def run():
                        act.wait_ge(x_done, a - 1) if not isinstance(a, int) or a > 1 else None
                        act.wait_ge(xs_fixed if l3 else xs_in, 2 * a + 1 + h)
                        nc.scalar.activation(xs[:, par, h], ps_w[:, h], ACT.Silu, bias=conv_bias[:, h:h + 1])\
                            .then_inc(xs_ready, 1)
                    return run

                def silu_gate(h):
                    def run():
                        act.wait_ge(gate_in, 2 * a + 1 + h)
                        nc.scalar.activation(sg[:, par, h], ps_w[:, h], ACT.Silu,
                                             bias=w["in_b"][:, 2 + h:3 + h] if l3 else 0.0).then_inc(sg_ready, 1)
                    return run

                def copy_low():
                    act.wait_ge(bc_split, a)
                    act.wait_ge(dt_in, 2 * a)
                    act.wait_ge(bc_in, a + 1)
                    ins = nc.scalar.copy(bcf[:], ps_w[:, 0])
                    if l3:
                        act.wait_ge(low_in, a + 1)
                        ins.then_inc(bcf_ready, 1)
                        ins = nc.scalar.copy(low[:], ps_w[0:64, 1])
                    ins.then_inc(low_ready, 1)

                def soft():
                    m = Marks(act, sp_step, a * 4)
                    for h in range(2):
                        bank = h if l3 else 1 - h
                        act.wait_ge(dt_in, 2 * a + 1 + h)
                        act.wait_ge(dt_ready, 2 * a)
                        m.mark(("abs", h), nc.scalar.activation(sp[:, h], ps_w[:, bank], ACT.Abs, bias=w["dt_b"][:, h:h + 1]))
                    for h in range(2):
                        m.need(("abs", h))
                        m.mark(("exp", h), nc.scalar.activation(sp[:, h], sp[:, h], ACT.Exp, scale=-1.0))
                    for h in range(2):
                        m.need(("exp", h))
                        nc.scalar.activation(sp[:, h], sp[:, h], ACT.Ln, bias=1.0).then_inc(sp_ready, 1)
                return {2: [silu_xs(0), silu_xs(1)], 3: [silu_gate(0), silu_gate(1)], 4: [copy_low],
                        6: [soft]}

            def copy_b(i, g):
                act.wait_ge(b_ready, i * GROUPS + g + 1)
                act.wait_ge(u_ready, (i * GROUPS + g) * 2)
                nc.scalar.copy(bsb[:, g % 2], ps_b[:]).then_inc(bsb_ready, 1)

            def copy_c(i, g):
                act.wait_ge(c_ready, i * GROUPS + g + 1)
                act.wait_ge(hc_ready, (i * GROUPS + g) * 2 + 2)
                nc.scalar.copy(csb[:, g % 2], ps_c[:]).then_inc(csb_ready, 1)

            def decay(i, par, g, h):
                act.wait_ge(h_ready, i * UNITS + g * 2 + h + 1)
                slot = (g * 2 + h) % RING
                for s in range(SG):
                    n = h * NSTATE + g * SG + s
                    ins = nc.scalar.activation(da[:, slot, s], dt[:, par, h], ACT.Exp, scale=a_neg[:, n:n + 1])
                ins.then_inc(da_ready, 1)

            def step(i, par, more):
                ahead = pieces(i + 1, 1 - par) if more else {}
                act.wait_ge(dt_ready, 2 * i + 2)
                for g in range(GROUPS):
                    decay(i, par, g, 0)
                    if g + 1 < GROUPS:
                        copy_b(i, g + 1)
                    elif more:
                        copy_b(i + 1, 0)
                    copy_c(i, g)
                    decay(i, par, g, 1)
                    for piece in ahead.get(g, []):
                        piece()

            for group in pieces(0, 0).values():
                for piece in group:
                    piece()
            copy_b(0, 0)
            step(0, 0, True)
            with act.Fori(0, NT // 2 - 1) as ii:
                step(ii * 2 + 1, 1, True)
                step(ii * 2 + 2, 0, True)
            step(NT - 1, 1, False)

        @block.gpsimd
        def _(pool):
            pool.sem_inc(u_ready, 2)

            def step(i, par):
                pool.wait_ge(dtx_ready, i + 1)
                for g in range(GROUPS):
                    pool.wait_ge(bsb_ready, i * GROUPS + g + 1)
                    for h in range(2):
                        pool.wait_ge(h_ready, i * UNITS + g * 2 + h + 1)
                        slot = (g * 2 + h) % RING
                        nc.gpsimd.tensor_tensor(u[:, slot], bsb[:, g % 2],
                                                dtx[:, par, h].unsqueeze(1).broadcast_to([P, SG, TILE]),
                                                ALU.mult).then_inc(u_ready, 1)

            with pool.Fori(0, NT // 2) as ii:
                step(ii * 2, 0)
                step(ii * 2 + 1, 1)

        @block.vector
        def _(dve):
            V = nc.vector
            dve.sem_inc(h_ready, RING)
            dve.sem_inc(y_used, 2)
            dve.sem_inc(hc_ready, 4)

            def pieces(a, par, m):
                def fix(h):
                    def run():
                        dve.wait_ge(xs_in, 2 * a + 1 + h)
                        at = rows(ps_w[:, h])[:, :, 0:PAD]
                        V.tensor_tensor(at, at, corr[:, h].unsqueeze(1).broadcast_to([P, RT, PAD]), ALU.add)\
                            .then_inc(xs_fixed, 1)
                    return run

                def split():
                    if not isinstance(a, int) or a > 1:
                        dve.wait_ge(x_done, a - 1)
                    dve.wait_ge(bcf_ready if l3 else low_ready, a + 1)
                    m.mark("hi", V.tensor_copy(bct[:, par], bcf[:]))
                    m.need("hi")
                    m.mark("r1", V.tensor_tensor(rest[64:], bcf[64:], bct[64:, par], ALU.subtract))
                    m.need("r1")
                    m.mark("mid", V.tensor_copy(bct[64:, par], rest[64:]))
                    m.need("mid")
                    m.mark("r2", V.tensor_tensor(rest[96:], rest[96:], bct[96:, par], ALU.subtract))
                    m.need("r2")
                    V.tensor_copy(bct[96:, par], rest[96:]).then_inc(bc_split, 1)

                def step_size(h):
                    bank = h if l3 else 1 - h

                    def run():
                        dve.wait_ge(sp_ready, 2 * a + 1 + h)
                        m.mark(("lin", h), V.tensor_scalar(lin[:], ps_w[:, bank], w["dt_b"][:, h:h + 1], 0.0,
                                                           ALU.add, ALU.max))
                        m.need(("lin", h))
                        V.tensor_tensor(dt[:, par, h], lin[:], sp[:, h], ALU.add).then_inc(dt_ready, 1)
                        dve.wait_ge(dt_ready, 2 * a + 1 + h)
                    return run

                def times_x():
                    if l3:
                        dve.sem_inc(dtx_ready, 1)
                        return
                    dve.wait_ge(xs_ready, 2 * a + 2)
                    V.tensor_tensor(dtx[:, par], dt[:, par], xs[:, par], ALU.mult).then_inc(dtx_ready, 1)
                return {1: [fix(0), fix(1)] if l3 else [], 4: [split], 6: [step_size(0), step_size(1), times_x]}

            def flat(ap):
                return ap.rearrange("p s t -> p (s t)")

            def make(i, n):
                q = i * UNITS + n
                dve.wait_ge(da_ready, q + 1)
                if l3:
                    dve.wait_ge(u_ready, q + 3)
                    V.scalar_tensor_tensor(out=flat(u[:, n % RING]), in0=flat(da[:, n % RING]), scalar=-1.0,
                                           in1=flat(u[:, n % RING]), op0=ALU.add, op1=ALU.mult).then_inc(made, 1)
                    dve.wait_ge(made, 2 * q + 1)
                V.memset(da[:, n % RING].rearrange("p s (r t) -> p (s r) t", t=T)[:, :, 0:1], 0.0).then_inc(made, 1)

            def scan(i, n):
                q = i * UNITS + n
                if l3:
                    dve.wait_ge(made, 2 * q + 2)
                else:
                    dve.wait_ge(u_ready, q + 3)
                    dve.wait_ge(made, q + 1)
                dve.wait_ge(hc_ready, q + 3)
                V.tensor_tensor_scan(flat(hs[:, n % 2]), flat(da[:, n % RING]), flat(u[:, n % RING]), 0.0,
                                     ALU.mult, ALU.add).then_inc(h_ready, 1)

            def times_c(i, n):
                q = i * UNITS + n
                dve.wait_ge(h_ready, q + RING + 1)
                dve.wait_ge(csb_ready, i * GROUPS + n // 2 + 1)
                dve.wait_ge(y_used, q + 1)
                V.tensor_tensor(hc[:, n % 2], hs[:, n % 2], csb[:, n // 2 % 2], ALU.mult).then_inc(hc_ready, 1)

            def gated(i, par):
                dve.wait_ge(out_ready, i)
                dve.wait_ge(y_used, (i + 1) * UNITS + 2)
                for h in range(2):
                    V.tensor_tensor(yg[:, h], ps_y[:, h], sg[:, par, h], ALU.mult).then_inc(yg_ready, 1)

            def finish(i):
                dve.wait_ge(out_ready, i + 1)
                if l3:
                    V.tensor_scalar(out[:, tile(i)], ps_w[:, out_bank], w["out_b"], None, ALU.add).then_inc(x_done, 1)
                else:
                    V.tensor_tensor(out[:, tile(i)], ps_w[:, out_bank], res[:, tile(i)], ALU.add).then_inc(x_done, 1)

            def step(i, par, first, more):
                ahead = pieces(i + 1, 1 - par, Marks(dve, chain, i * 6 + 6)) if more else {}
                for n in range(UNITS):
                    scan(i, n)
                    if n:
                        times_c(i, n - 1)
                    elif not first:
                        times_c(i - 1, UNITS - 1)
                    if n + 1 < UNITS:
                        make(i, n + 1)
                    elif more:
                        make(i + 1, 0)
                    if n == 1 and not first:
                        gated(i - 1, 1 - par)
                    if n == 4 and not first:
                        finish(i - 1)
                    if n % 2 == 0 and n:
                        for piece in ahead.get(n // 2 - 1, []):
                            piece()

            for group in pieces(0, 0, Marks(dve, chain, 0)).values():
                for piece in group:
                    piece()
            make(0, 0)
            step(0, 0, True, True)
            with dve.Fori(0, NT // 2 - 1) as ii:
                step(ii * 2 + 1, 1, False, True)
                step(ii * 2 + 2, 0, False, True)
            step(NT - 1, 1, False, False)
            times_c(NT - 1, UNITS - 1)
            gated(NT - 1, 1)
            finish(NT - 1)



NH, NKV, DH = 16, 4, 8
QPK = NH // NKV


def attention_inputs(nc, w, h, q, v_all):
    with ExitStack() as ctx:
        def sb(name, shape):
            return ctx.enter_context(nc.sbuf_tensor("ai_" + name, shape, F32))

        ps = ctx.enter_context(nc.psum_tensor("ai_ps", [P, 4, TILE], F32))
        ps_v = ctx.enter_context(nc.psum_tensor("ai_v", [P, TILE], F32))
        ps_t = ctx.enter_context(nc.psum_tensor("ai_t", [P, 4, P], F32))
        prod = sb("prod", [P, 4, TILE])
        vt = sb("vt", [P, TILE])
        block, in_ready, rotated, added, v_in, v_copied, v_turned, v_done = ctx.enter_context(
            phase(nc, "in_ready rotated added v_in v_copied v_turned v_done"))

        @block.tensor
        def _(pe):
            with pe.Fori(0, NT) as i:
                for n, name in enumerate(("q_w", "q_w_rot", "k_w", "k_w_rot")):
                    pe.wait_ge(rotated, i * 4 + n + 1)
                    nc.tensor.matmul(ps[:, n], w[name], h[:, tile(i)], start=True, stop=True).then_inc(in_ready, 1)
                pe.wait_ge(v_copied, i)
                nc.tensor.matmul(ps_v[:], w["v_w"], h[:, tile(i)], start=True, stop=True).then_inc(v_in, 1)
                pe.wait_ge(v_copied, i + 1)
                pe.wait_ge(v_done, i)
                for b in range(4):
                    mm = nc.tensor.transpose(ps_t[:, b], vt[:, b * P:(b + 1) * P], w["eye"])
                mm.then_inc(v_turned, 1)

        @block.scalar
        def _(act):
            with act.Fori(0, NT) as i:
                act.wait_ge(v_in, i + 1)
                nc.scalar.copy(vt[:], ps_v[:]).then_inc(v_copied, 1)
                act.wait_ge(v_turned, i + 1)
                nc.scalar.copy(v_all[:, bass.ds(i * 4, 4)], ps_t[:, :, 0:NKV * DH]).then_inc(v_done, 1)

        @block.vector
        def _(dve):
            dve.sem_inc(rotated, 4)
            with dve.Fori(0, NT) as i:
                dve.wait_ge(added, i * 2)
                for n, name in enumerate(("q_cos", "q_sin", "k_cos", "k_sin")):
                    dve.wait_ge(in_ready, i * 4 + n + 1)
                    nc.vector.tensor_tensor(rows(prod[:, n]), rows(ps[:, n]),
                                            w[name].unsqueeze(1).broadcast_to([P, RT, T]), ALU.mult).then_inc(rotated, 1)

        @block.gpsimd
        def _(pool):
            with pool.Fori(0, NT) as i:
                pool.wait_ge(rotated, i * 4 + 6)
                nc.gpsimd.tensor_tensor(q[:, tile(i)], prod[:, 0], prod[:, 1], ALU.add).then_inc(added, 1)
                pool.wait_ge(rotated, i * 4 + 8)
                pool.wait_ge(v_in, i + 1)
                nc.gpsimd.tensor_tensor(h[:, tile(i)], prod[:, 2], prod[:, 3], ALU.add).then_inc(added, 1)


def attention(nc, w, q, k, v_all, x):
    G = 4
    BLK = G * RT * 2
    HALVES = NKV * 2
    CU = [(n, g, kb) for n in range(BLK) for g in range(NKV) for kb in range(n % 2 + 1)]
    NU = len(CU)
    first = [min(u for u in range(NU) if CU[u][0] == n) for n in range(BLK)]
    last = [max(u for u in range(NU) if CU[u][0] == n) for n in range(BLK)]
    LAG = 2
    max_at = {}
    for n in range(1, BLK):
        steps = [0, 0, 0, 1, 1, 1, 2, 2] if n % 2 else [0, 1, 2, 3, 3, 4, 4, 5]
        for i, s in enumerate(steps):
            max_at.setdefault(first[n - 1] + s, []).append(n * HALVES + i)
    turn_at = {last[n - 1]: n for n in range(1, BLK)}
    copy_at = {last[n] + LAG: n for n in range(BLK)}
    sums_at = {last[n] + LAG + 1: n for n in range(BLK)}
    out_at = {last[n] + LAG + 6: n // 4 for n in range(3, BLK, 4)}
    spread_at = {first[j * 4 - 2] + c: (j, c) for j in range(1, G) for c in range(QPK)}
    STEPS = max(out_at) + 1
    divide_at = {sums_at_u + c: (n, c) for sums_at_u, n in sums_at.items() for c in range(QPK)}
    with ExitStack() as ctx:
        def sb(name, shape, dt=F32):
            return ctx.enter_context(nc.sbuf_tensor("at_" + name, shape, dt))

        ps_s = ctx.enter_context(nc.psum_tensor("at_ps_s", [P, 2, 2, T], F32))
        ps_t = ctx.enter_context(nc.psum_tensor("at_ps_t", [P, QPK, P], F32))
        ps_c = ctx.enter_context(nc.psum_tensor("at_ps_c", [P, 2, QPK, P], F32))
        ps_v = ctx.enter_context(nc.psum_tensor("at_ps_v", [P, QPK, P], F32))
        ps_x = ctx.enter_context(nc.psum_tensor("at_ps_x", [P, QPK, P], F32))
        ps_w = ctx.enter_context(nc.psum_tensor("at_ps_w", [P, TILE], F32))
        qm = sb("qm", [P, 2, QPK, TILE])
        kt = sb("kt", [P, 2, TILE])
        vt = sb("vt", [P, 2, 4, NKV, P])
        pt = sb("pt", [P, 4, QPK, P])
        mx = sb("mx", [P, QPK, P])
        ov = sb("ov", [P, QPK, P])
        rc = sb("rc", [P, QPK, P])
        on = sb("on", [P, QPK, TILE])
        maskb = sb("maskb", [P, 2, T], BF16)
        eyeb = sb("eyeb", [P, QPK, P], BF16)
        (block, consts, filled, spread_in, qm_ready, kv_ready, s_ready, max_ready, turned, less_max, c_ready, exp_ready, v_ready,
         ov_ready, sums_in, rc_ready, on_ready, out_ready, x_done) = ctx.enter_context(phase(
             nc, "consts filled spread_in qm_ready kv_ready s_ready max_ready turned less_max c_ready exp_ready v_ready "
             "ov_ready sums_in rc_ready on_ready out_ready x_done"))

        def flat(bank):
            return bank.rearrange("p a b -> p (a b)")

        def place(n):
            return n // 4 % 2, n % 4 * P, n % 4 // 2 * T

        @block.tensor
        def _(pe):
            pe.wait_ge(consts, 3)

            def spread(ii, j, c, bank):
                pe.wait_ge(qm_ready, (ii * G + j) * QPK + c)
                nc.tensor.matmul(bank, w["spread"][:, c * P:(c + 1) * P], q[:, tile(ii * G + j)], start=True, stop=True)\
                    .then_inc(spread_in, 1)

            def scores(ii, h):
                n, g, cp = h // HALVES, h % HALVES // 2, h % 2
                slot, col, row = place(n)
                if h % (4 * HALVES) == 0:
                    pe.wait_ge(qm_ready, (ii * G + n // 4 + 1) * QPK)
                    pe.wait_ge(kv_ready, ii * G + n // 4 + 1)
                pe.wait_ge(max_ready, ii * BLK * HALVES + h + 1)
                at, keys = slice(32 * g, 32 * g + 32), (n % 2 + 1) * P
                nc.tensor.matmul(ps_s[:, h % 2, :, 0:keys], eyeb[:, 0], maskb[:, :, T - keys:T], start=True, stop=False)
                for c in range(2):
                    mm = nc.tensor.matmul(ps_s[:, h % 2, c, 0:keys], qm[at, slot, cp * 2 + c, col:col + P],
                                          kt[at, slot, row:row + keys], start=False, stop=c == 1)
                mm.then_inc(s_ready, 1)

            def turn(ii, n):
                pe.wait_ge(max_ready, (ii * BLK + n + 1) * HALVES + 2)
                pe.wait_ge(less_max, ii * BLK + n)
                for c in range(QPK):
                    mm = nc.tensor.transpose(ps_t[:, c], mx[:, c], w["eye"])
                mm.then_inc(turned, 1)

            def scores_t(ii, u):
                n, g, kb = CU[u]
                slot, col, row = place(n)
                if u == first[n]:
                    pe.wait_ge(less_max, ii * BLK + n + 1)
                pe.wait_ge(exp_ready, ii * NU + u + 1)
                at, diagonal = slice(32 * g, 32 * g + 32), kb == n % 2
                mm = nc.tensor.matmul(ps_c[:, u % 2], kt[at, slot, row + kb * P:row + (kb + 1) * P],
                                      qm[at, slot, :, col:col + P], start=True, stop=not diagonal)
                if diagonal:
                    mm = nc.tensor.matmul(ps_c[:, u % 2], maskb[:, 0, P:T], eyeb[:], start=False, stop=True)
                mm.then_inc(c_ready, 1)

            def values(ii, u):
                n, g, kb = CU[u]
                pe.wait_ge(exp_ready, ii * NU + u + 3)
                if u == first[n]:
                    pe.wait_ge(ov_ready, ii * BLK + n + 4)
                nc.tensor.matmul(ps_v[:], vt[:, place(n)[0], n % 4 // 2 * 2 + kb, g], pt[:, u % 4],
                                 start=u == first[n], stop=u == last[n]).then_inc(v_ready, 1)

            def sums(ii, n):
                pe.wait_ge(ov_ready, ii * BLK + n + 5)
                pe.wait_ge(on_ready, ii * BLK + n)
                nc.tensor.matmul(ps_x[:], w["sum_rows"], ov[:], start=True, stop=True).then_inc(sums_in, 1)

            def project(ii, j):
                pe.wait_ge(on_ready, (ii * G + j + 1) * 4)
                pe.wait_ge(x_done, ii * G + j)
                pe.wait_ge(qm_ready, (ii * G + min(j + 2, G)) * QPK)
                for c in range(QPK):
                    mm = nc.tensor.matmul(ps_w[:], w["o_w"][:, c * P:(c + 1) * P], on[:, c],
                                          start=c == 0, stop=c == QPK - 1)
                mm.then_inc(out_ready, 1)

            with pe.Fori(0, NT // G) as ii:
                pe.wait_ge(on_ready, ii * BLK)
                for c, bank in enumerate((flat(ps_c[:, 0]), flat(ps_c[:, 1]), flat(ps_t[:]), flat(ps_x[:]))):
                    spread(ii, 0, c, bank)
                for h in range(HALVES):
                    scores(ii, h)
                turn(ii, 0)
                for u in range(STEPS):
                    if u < NU:
                        scores_t(ii, u)
                    for h in max_at.get(u, ()):
                        scores(ii, h)
                    if u in turn_at:
                        turn(ii, turn_at[u])
                    if LAG <= u < NU + LAG:
                        values(ii, u - LAG)
                    if u in sums_at:
                        sums(ii, sums_at[u])
                    if u in spread_at:
                        j, c = spread_at[u]
                        pe.wait_ge(x_done, ii * G + j - 1) if j > 1 else pe.wait_ge(x_done, ii * G)
                        spread(ii, j, c, ps_w[:])
                    if u in out_at:
                        project(ii, out_at[u])

        @block.scalar
        def _(act):
            act.sem_inc(ov_ready, 4)

            def copy_q(ii, j, c, bank):
                act.wait_ge(spread_in, (ii * G + j) * QPK + c + 1)
                nc.scalar.copy(qm[:, j % 2, c], bank).then_inc(qm_ready, 1)

            with act.Fori(0, NT // G) as ii:
                for c, bank in enumerate((flat(ps_c[:, 0]), flat(ps_c[:, 1]), flat(ps_t[:]), flat(ps_x[:]))):
                    copy_q(ii, 0, c, bank)
                for u in range(STEPS):
                    if u < NU:
                        act.wait_ge(c_ready, ii * NU + u + 1)
                        act.wait_ge(v_ready, ii * NU + u + 1)
                        nc.scalar.activation(pt[:, u % 4], ps_c[:, u % 2], ACT.Exp).then_inc(exp_ready, 1)
                    if u in copy_at:
                        n = copy_at[u]
                        act.wait_ge(v_ready, ii * NU + last[n] + 5)
                        act.wait_ge(on_ready, ii * BLK + n)
                        nc.scalar.copy(ov[:], ps_v[:]).then_inc(ov_ready, 1)
                    if u in spread_at:
                        copy_q(ii, *spread_at[u], ps_w[:])

        @block.gpsimd
        def _(pool):
            pool.wait_ge(consts, 3)
            with pool.Fori(0, NT // G) as ii:
                for j in range(G):
                    i = ii * G + j
                    pool.wait_ge(ov_ready, i * 4)
                    nc.gpsimd.tensor_tensor(kt[:, j % 2], k[:, tile(i)], w["ones_rows"].broadcast_to([P, TILE]), ALU.add)
                    for g in range(NKV):
                        ins = nc.gpsimd.tensor_copy(vt[:, j % 2, :, g, 32 * g + 1:32 * g + 1 + DH],
                                                    v_all[:, bass.ds(i * 4, 4), g * DH:(g + 1) * DH])
                    ins.then_inc(kv_ready, 1)

        @block.vector
        def _(dve):
            V = nc.vector
            V.memset(vt[:].rearrange("p j b g c -> p (j b g c)"), 0.0).then_inc(filled, 1)
            V.memset(mx[:].rearrange("p c q -> p (c q)"), 0.0).then_inc(filled, 1)
            V.memset(maskb[:, :, 0:P], 0.0)
            V.tensor_copy(maskb[:, :, P:T], w["causal"].unsqueeze(1).broadcast_to([P, 2, P])).then_inc(consts, 1)
            V.tensor_copy(eyeb[:], w["eye"].unsqueeze(1).broadcast_to([P, QPK, P])).then_inc(consts, 1)
            dve.wait_ge(filled, 2)
            for g in range(NKV):
                for j in range(2):
                    ins = V.memset(vt[:, j, :, g, 32 * g:32 * g + 1], 1.0)
            ins.then_inc(consts, 1)
            dve.sem_inc(max_ready, 2)
            dve.sem_inc(exp_ready, 2)
            dve.sem_inc(v_ready, 4)

            def biggest(ii, h):
                n, g, cp = h // HALVES, h % HALVES // 2, h % 2
                dve.wait_ge(s_ready, ii * BLK * HALVES + h + 1)
                V.tensor_reduce(mx[:, cp * 2:cp * 2 + 2, 32 * g], ps_s[:, h % 2, :, 0:(n % 2 + 1) * P], AX, ALU.max)\
                    .then_inc(max_ready, 1)

            def subtract(ii, n):
                slot, col, _row = place(n)
                dve.wait_ge(turned, ii * BLK + n + 1)
                V.tensor_tensor(qm[:, slot, :, col:col + P], qm[:, slot, :, col:col + P], ps_t[:], ALU.subtract)\
                    .then_inc(less_max, 1)

            def divide(ii, n, c):
                if c == 0:
                    dve.wait_ge(sums_in, ii * BLK + n + 1)
                    if n % 4 == 0:
                        dve.wait_ge(out_ready, ii * G + n // 4)
                V.reciprocal(rc[:, c], ps_x[:, c]).then_inc(rc_ready, 1)
                dve.wait_ge(rc_ready, (ii * BLK + n) * QPK + c + 1)
                ins = V.tensor_tensor(on[:, c, n % 4 * P:(n % 4 + 1) * P], ov[:, c], rc[:, c], ALU.mult)
                if c == QPK - 1:
                    ins.then_inc(on_ready, 1)

            with dve.Fori(0, NT // G) as ii:
                for h in range(HALVES):
                    biggest(ii, h)
                subtract(ii, 0)
                for u in range(STEPS):
                    for h in max_at.get(u, ()):
                        biggest(ii, h)
                    if u in turn_at:
                        subtract(ii, turn_at[u])
                    if u in divide_at:
                        divide(ii, *divide_at[u])
                    if u in out_at:
                        j = out_at[u]
                        dve.wait_ge(out_ready, ii * G + j + 1)
                        at = tile(ii * G + j)
                        V.tensor_tensor(x[:, at], ps_w[:], x[:, at], ALU.add).then_inc(x_done, 1)


def gated_mlp(nc, w, h, x):
    M = 4
    K = U * M
    with ExitStack() as ctx:
        up = ctx.enter_context(nc.psum_tensor("gm_up", [P, 2, 2, TILE], F32))
        down = ctx.enter_context(nc.psum_tensor("gm_down", [P, 2, TILE], F32))
        s = ctx.enter_context(nc.sbuf_tensor("gm_s", [P, 4, TILE], F32))
        hg = ctx.enter_context(nc.sbuf_tensor("gm_hg", [P, 4, TILE], F32))
        block, up_ready, silu_ready, gated, down_ready, done = ctx.enter_context(
            phase(nc, "up_ready silu_ready gated down_ready done"))
        lag = 2
        w2 = w["gm_w2"].rearrange("p (m c) -> p m c", m=M)

        @block.tensor
        def _(pe):
            with pe.Fori(0, NT // U) as i:
                for n in range(K + lag):
                    if n < K:
                        pe.wait_ge(gated, i * K + n + 1)
                        for a, name in enumerate(("gm_w1", "gm_w3")):
                            mm = nc.tensor.matmul(up[:, n % 2, a], w[name][:, (n % M) * P:(n % M + 1) * P],
                                                  h[:, tile(i * U + n // M)], start=True, stop=True)
                        mm.then_inc(up_ready, 1)
                    m = n - lag
                    if m >= 0:
                        pe.wait_ge(gated, i * K + m + 3)
                        if m % M == 0:
                            pe.wait_ge(done, i * U + m // M + 1)
                        nc.tensor.matmul(down[:, m // M % 2], w2[:, m % M], hg[:, m % 4],
                                         start=m % M == 0, stop=m % M == M - 1).then_inc(down_ready, 1)

        @block.scalar
        def _(act):
            act.sem_inc(down_ready, 4)
            with act.Fori(0, NT // U) as i:
                for n in range(K):
                    act.wait_ge(up_ready, i * K + n + 1)
                    if n >= 2:
                        act.wait_ge(gated, i * K + n - 1)
                    else:
                        act.wait_ge(gated, i * K + 1)
                    nc.scalar.activation(s[:, n % 4], up[:, n % 2, 0], ACT.Silu).then_inc(silu_ready, 1)

        @block.vector
        def _(dve):
            dve.sem_inc(gated, 2)
            dve.sem_inc(done, 2)
            with dve.Fori(0, NT // U) as i:
                for n in range(K + lag + 1):
                    if n < K:
                        dve.wait_ge(silu_ready, i * K + n + 1)
                        dve.wait_ge(down_ready, i * K + n + 1)
                        nc.vector.tensor_tensor(hg[:, n % 4], s[:, n % 4], up[:, n % 2, 1], ALU.mult).then_inc(gated, 1)
                    m = n - lag
                    if m > 0 and m % M == 0:
                        j = m // M - 1
                        dve.wait_ge(down_ready, (i * U + j + 1) * M + 4) if m < K else None
                        at = tile(i * U + j)
                        nc.vector.tensor_tensor(x[:, at], down[:, j % 2], x[:, at], ALU.add).then_inc(done, 1) \
                            if m < K else None
                dve.wait_ge(down_ready, (i * U + U) * M + 4)
                at = tile(i * U + U - 1)
                nc.vector.tensor_tensor(x[:, at], down[:, (U - 1) % 2], x[:, at], ALU.add).then_inc(done, 1)


def project_tokens(nc, w, xn, xf):
    with ExitStack() as ctx:
        ps = ctx.enter_context(nc.psum_tensor("pt_ps", [P, U, TILE], F32))
        block, ready, done = ctx.enter_context(phase(nc, "ready done"))

        @block.tensor
        def _(pe):
            with pe.Fori(0, NT // U) as i:
                for j in range(U):
                    pe.wait_ge(done, i * U + j + 1)
                    nc.tensor.matmul(ps[:, j], w["W_proj"], xn[:, tile(i * U + j)], start=True, stop=True).then_inc(ready, 1)

        @block.scalar
        def _(act):
            act.sem_inc(done, U)
            with act.Fori(0, NT // U) as i:
                for j in range(U):
                    act.wait_ge(ready, i * U + j + 1)
                    nc.scalar.activation(xf[:, tile(i * U + j)], ps[:, j], ACT.Identity, bias=w["b_proj"]).then_inc(done, 1)


def centre_experts(nc, w, w1, b1c):
    with ExitStack() as ctx:
        ps = ctx.enter_context(nc.psum_tensor("ce_ps", [P, E8, 4], F32))
        mean = ctx.enter_context(nc.sbuf_tensor("ce_mean", [P, E8], F32))
        block, chain, ready = ctx.enter_context(phase(nc, "chain ready"))

        @block.tensor
        def _(pe):
            nc.tensor.matmul(ps[:].rearrange("p e m -> p (e m)"), w["mean"], w["b1"], start=True, stop=True).then_inc(ready, 1)

        @block.vector
        def _(dve):
            V = nc.vector
            ch = Chain(dve, chain)
            wv = w1.rearrange("p (e f) -> p e f", e=E8)
            ch.then(V.tensor_reduce(mean[:], wv, AX, ALU.add))
            ch.then(V.tensor_scalar(mean[:], mean[:], 1.0 / 512, None, ALU.mult))
            ch.then(V.tensor_tensor(wv, wv, mean[:].unsqueeze(2).broadcast_to([P, E8, 512]), ALU.subtract))
            dve.wait_ge(ready, 1)
            ch.then(V.tensor_reduce(mean[:], ps[:], AX, ALU.add))
            ch.then(V.tensor_scalar(mean[:], mean[:], 0.25, None, ALU.mult))
            ch.then(V.tensor_tensor(b1c[:].rearrange("p (e m) -> p e m", m=4), w["b1"].rearrange("p (e m) -> p e m", m=4),
                                    mean[:].unsqueeze(2).broadcast_to([P, E8, 4]), ALU.subtract))


def collect(nc, w, y_slots, slots, tok, y):
    with ExitStack() as ctx:
        ps = ctx.enter_context(nc.psum_tensor("cl_ps", [P, 4, 4, P], F32))
        names = " ".join(f"fetched{g}" for g in range(NBLK // 4))
        block, zeroed, turned, copied, *fetched = ctx.enter_context(phase(nc, "zeroed turned copied " + names))
        last_slot = y_slots.shape[0] - 1

        @block.gpsimd
        def _(pool):
            pool.wait_ge(zeroed, 1)
            for b in range(NBLK):
                nc.gpsimd.indirect_dma_start(
                    tok[:, b], None, y_slots, bass.IndirectOffsetOnAxis(ap=slots[:, b:b + 1], axis=0),
                    bounds_check=last_slot, oob_is_err=False).then_inc(fetched[b // 4], 16)

        @block.tensor
        def _(pe):
            for b in range(NBLK):
                if b % 4 == 0:
                    pe.wait_ge(fetched[b // 4], 64)
                if b % 4 == 0 and b >= 16:
                    pe.wait_ge(copied, b // 4 - 3)
                mm = nc.tensor.transpose(ps[:, b // 4 % 4, b % 4], tok[:, b], w["eye"])
                if b % 4 == 3:
                    mm.then_inc(turned, 1)

        @block.vector
        def _(dve):
            nc.vector.memset(tok[:].rearrange("p b c -> p (b c)"), 0.0).then_inc(zeroed, 1)
            for g in range(NBLK // 4):
                dve.wait_ge(turned, g + 1)
                nc.vector.tensor_copy(y[:, g * TILE:(g + 1) * TILE], ps[:, g % 4].rearrange("p b c -> p (b c)"))\
                    .then_inc(copied, 1)


def experts_norm(nc, w, w1, b1c, w2, x_slots, y_slots):
    M = 4
    TPE = x_slots.shape[0] // (E8 * TILE)
    with ExitStack() as ctx:
        def sb(name, shape, dt=F32):
            return ctx.enter_context(nc.sbuf_tensor("xl_" + name, shape, dt))

        up = ctx.enter_context(nc.psum_tensor("xl_up", [P, M, TILE], F32))
        var = ctx.enter_context(nc.psum_tensor("xl_var", [P, TILE], F32))
        turn = ctx.enter_context(nc.psum_tensor("xl_turn", [P, TILE], F32))
        down = ctx.enter_context(nc.psum_tensor("xl_down", [P, 2, 4, P], F32))
        xg = sb("xg", [P, 4, 4, P])
        xf = sb("xf", [P, 2, TILE])
        sq = sb("sq", [P, M, TILE])
        lg = sb("lg", [P, TILE])
        ri = sb("ri", [P, TILE])
        hn = sb("hn", [P, M, TILE])
        hg = sb("hg", [P, M, TILE])
        yo = sb("yo", [P, 2, 4, P])
        (block, turned, xf_ready, up_ready, sq_ready, var_ready, lg_ready, ri_ready, hn_ready, hg_ready,
         down_ready, y_ready, *rings) = ctx.enter_context(phase(
             nc, "turned xf_ready up_ready sq_ready var_ready lg_ready ri_ready hn_ready hg_ready "
             "down_ready y_ready x_in0 x_in1 x_in2 x_in3 y_out0 y_out1"))
        x_in, y_out = rings[:4], rings[4:]
        xs_v = x_slots.rearrange("(v p s) c -> p v (s c)", p=P, s=4)
        ys_v = y_slots.rearrange("(v p s) c -> p v (s c)", p=P, s=4)

        @block.sync
        def _(sp):
            with sp.Fori(0, TPE) as i:
                for e in range(E8):
                    v = i * E8 + e
                    sp.wait_ge(turned, v + 1)
                    sp.dma_start(xg[:, e % 4].rearrange("p s c -> p (s c)"),
                                 xs_v[:, bass.ds(i + e * TPE, 1)].rearrange("p v c -> p (v c)")).then_inc(x_in[e % 4], 16)

        @block.gpsimd
        def _(pool):
            with pool.Fori(0, TPE) as i:
                for e in range(E8):
                    pool.wait_ge(y_ready, i * E8 + e + 1)
                    pool.dma_start(ys_v[:, bass.ds(i + e * TPE, 1)].rearrange("p v c -> p (v c)"),
                                   yo[:, e % 2].rearrange("p s c -> p (s c)")).then_inc(y_out[e % 2], 16)
            for n in range(2):
                pool.wait_ge(y_out[n], TPE * E8 // 2 * 16)

        @block.tensor
        def _(pe):
            def turn_tile(i, e):
                v = i * E8 + e
                pe.wait_ge(x_in[e % 4], i * 32 + e // 4 * 16 + 16)
                pe.wait_ge(xf_ready, v)
                for s in range(4):
                    mm = nc.tensor.transpose(turn[:, s * P:(s + 1) * P], xg[:, e % 4, s], w["eye"])
                mm.then_inc(turned, 1)

            def product(i, e):
                v = i * E8 + e
                pe.wait_ge(hg_ready, v * M + M + 4)
                if e >= 2:
                    pe.wait_ge(y_ready, v - 1)
                else:
                    pe.wait_ge(y_ready, i * E8)
                for s in range(4):
                    for m in range(M):
                        mm = nc.tensor.matmul(down[:, e % 2, s], hg[:, m, s * P:(s + 1) * P], w2[:, e * M + m],
                                              start=m == 0, stop=m == M - 1)
                mm.then_inc(down_ready, M)

            with pe.Fori(0, TPE) as i:
                turn_tile(i, 0)
                for e in range(E8):
                    v = i * E8 + e
                    pe.wait_ge(xf_ready, v + 1)
                    for m in range(M):
                        pe.wait_ge(hn_ready, v * M + m + 1)
                        nc.tensor.matmul(up[:, m], w1[:, (e * M + m) * P:(e * M + m + 1) * P], xf[:, e % 2],
                                         start=True, stop=True).then_inc(up_ready, 1)
                    for m in range(M):
                        pe.wait_ge(sq_ready, v * M + m + 1)
                        if m == 0:
                            pe.wait_ge(lg_ready, v)
                        mm = nc.tensor.matmul(var[:], w["mean"], sq[:, m], start=m == 0, stop=m == M - 1)
                    mm.then_inc(var_ready, 1)
                    if e + 1 < E8:
                        turn_tile(i, e + 1)
                    if e:
                        product(i, e - 1)
                product(i, E8 - 1)

        @block.scalar
        def _(act):
            act.sem_inc(hg_ready, 4)
            act.sem_inc(down_ready, 4)
            with act.Fori(0, TPE) as i:
                for e in range(E8):
                    v = i * E8 + e
                    act.wait_ge(var_ready, v)
                    for m in range(M):
                        n = e * M + m
                        act.wait_ge(up_ready, v * M + m + 1)
                        nc.scalar.activation(sq[:, m], up[:, m], ACT.Square, bias=b1c[:, n:n + 1]).then_inc(sq_ready, 1)
                    act.wait_ge(var_ready, v + 1)
                    nc.scalar.activation(lg[:], var[:], ACT.Ln, scale=0.25, bias=w["eps_col"]).then_inc(lg_ready, 1)
                    act.wait_ge(lg_ready, v + 1)
                    act.wait_ge(hn_ready, v * M + 4)
                    nc.scalar.activation(ri[:], lg[:], ACT.Exp, scale=-0.5).then_inc(ri_ready, 1)
                    for m in range(M):
                        n = e * M + m
                        act.wait_ge(hn_ready, v * M + m + 5)
                        act.wait_ge(down_ready, v * M + 4)
                        nc.scalar.activation(hg[:, m], hn[:, m], ACT.Gelu, scale=w["eg"][:, n:n + 1],
                                             bias=w["eb"][:, n:n + 1]).then_inc(hg_ready, 1)

        @block.vector
        def _(dve):
            V = nc.vector
            dve.sem_inc(hn_ready, 4)
            dve.sem_inc(turned, 4)

            def copy_x(i, e):
                dve.wait_ge(turned, i * E8 + e + 5)
                V.tensor_copy(xf[:, e % 2], turn[:]).then_inc(xf_ready, 1)

            def add_bias(i, e):
                v = i * E8 + e
                dve.wait_ge(down_ready, (v + 1) * M + 4)
                if e >= 2:
                    dve.wait_ge(y_out[e % 2], i * 64 + e // 2 * 16)
                else:
                    dve.wait_ge(y_out[e % 2], i * 64)
                V.tensor_tensor(yo[:, e % 2], down[:, e % 2],
                                w["eb2"][:, e * P:(e + 1) * P].unsqueeze(1).broadcast_to([P, 4, P]), ALU.add)\
                    .then_inc(y_ready, 1)

            with dve.Fori(0, TPE) as i:
                copy_x(i, 0)
                for e in range(E8):
                    v = i * E8 + e
                    if e + 1 < E8:
                        copy_x(i, e + 1)
                    dve.wait_ge(ri_ready, v + 1)
                    for m in range(M):
                        n = e * M + m
                        dve.wait_ge(hg_ready, v * M + m + 1)
                        V.scalar_tensor_tensor(out=hn[:, m], in0=up[:, m], scalar=b1c[:, n:n + 1], in1=ri[:],
                                               op0=ALU.add, op1=ALU.mult).then_inc(hn_ready, 1)
                    if e:
                        add_bias(i, e - 1)
                add_bias(i, E8 - 1)


def gate_with(nc, tag, x_old, s, g_old, x, x_out=None):
    with ExitStack() as ctx:
        xo = ctx.enter_context(nc.sbuf_tensor(tag + "_xo", [P, U, TILE], F32))
        go = ctx.enter_context(nc.sbuf_tensor(tag + "_go", [P, U, TILE], F32))
        names = " ".join(f"{k}{j}" for j in range(U) for k in ("x_in", "g_in"))
        block, silu_ready, chain, done, stored, *ins = ctx.enter_context(phase(nc, "silu_ready chain done stored " + names))

        @block.sync
        def _(sp):
            with sp.Fori(0, NT // U) as i:
                for j in range(U):
                    sp.wait_ge(done, i * U + j + 1)
                    sp.dma_start(xo[:, j], x_old[:, tile(i * U + j)]).then_inc(ins[2 * j], 16)
                    sp.dma_start(go[:, j], g_old[:, tile(i * U + j)]).then_inc(ins[2 * j + 1], 16)

        if x_out is not None:
            @block.gpsimd
            def _(pool):
                with pool.Fori(0, NT // U) as i:
                    pool.wait_ge(done, i * U + 2 * U)
                    at = bass.ds(i * (U * TILE), U * TILE)
                    pool.dma_start(x_out[:, at], x[:, at]).then_inc(stored, 16)
                pool.wait_ge(stored, NT // U * 16)

        @block.scalar
        def _(act):
            with act.Fori(0, NT // U) as i:
                for j in range(U):
                    act.wait_ge(ins[2 * j + 1], i * 16 + 16)
                    nc.scalar.activation(go[:, j], go[:, j], ACT.Silu).then_inc(silu_ready, 1)

        @block.vector
        def _(dve):
            dve.sem_inc(done, U)
            with dve.Fori(0, NT // U) as i:
                for j in range(U):
                    ch = Chain(dve, chain, i * U + j)
                    dve.wait_ge(silu_ready, i * U + j + 1)
                    ch.then(nc.vector.tensor_tensor(go[:, j], go[:, j], s[:, tile(i * U + j)], ALU.mult))
                    dve.wait_ge(ins[2 * j], i * 16 + 16)
                    nc.vector.tensor_tensor(x[:, tile(i * U + j)], go[:, j], xo[:, j], ALU.add).then_inc(done, 1)


def layer2(nc, w0, groups, r0, r1, x_d, g_d, x_slots, y_slots):
    x, xn = r0[:, 0:N], r1[:, 0:N]
    layernorm(nc, "ln2", x, xn, w0, keep=x_d)
    with ExitStack() as ctx:
        w = ctx.enter_context(weights(nc, groups, "route", w0))
        w = ctx.enter_context(weights(nc, groups, "experts2", w))
        b1c = ctx.enter_context(nc.sbuf_tensor("l2_b1c", [P, E8 * 4], F32))
        slots = ctx.enter_context(nc.sbuf_tensor("l2_slots", [P, NBLK], mybir.dt.uint32))
        tok = ctx.enter_context(nc.sbuf_tensor("l2_tok", [P, NBLK, P], F32))
        w2 = w["w2"].rearrange("p (m c) -> p m c", c=P)
        centre_experts(nc, w, w["w1"], b1c)
        project_tokens(nc, w, xn, x)
        route(nc, "r2", w, w["W_gate"], x, 1, 2 * N // E8, slots, x_slots)
        dispatch(nc, "ds2", w, x, tok, slots, x_slots)
        experts_norm(nc, w, w["w1"], b1c, w2, x_slots, y_slots)
        collect(nc, w, y_slots, slots, tok, x)
        layernorm(nc, "ln2m", x, x, w, w["moe_g"], w["moe_b"])
        load(nc, "g_kept", [(g_d, x)])
    with weights(nc, groups, "mamba2", w0) as w:
        layernorm(nc, "ln2a", xn, padded_tile(r0), w, w["ln1_g"], w["ln1_b"])
        mamba(nc, w, groups["once2"][0], False, r0, xn, xn)
    h = r0[:, 0:N]
    with weights(nc, groups, "attention2", w0) as w:
        layernorm(nc, "ln2b", xn, h, w, w["ln2_g"], w["ln2_b"])
        with ExitStack() as ctx:
            q = ctx.enter_context(nc.sbuf_tensor("l2_q", [P, N], F32))
            v_all = ctx.enter_context(nc.sbuf_tensor("l2_v", [P, NBLK, NKV * DH], F32))
            attention_inputs(nc, w, h, q, v_all)
            attention(nc, w, q, h, v_all, xn)
        layernorm(nc, "ln2c", xn, h, w, w["ln3_g"], w["ln3_b"])
        gated_mlp(nc, w, h, xn)
    gate_with(nc, "gw2", x_d, xn, g_d, x)



def ternary(nc, tag, w, pairs):
    with ExitStack() as ctx:
        ab = ctx.enter_context(nc.sbuf_tensor(tag + "_ab", [P, len(pairs)], F32))
        th = ctx.enter_context(nc.sbuf_tensor(tag + "_th", [P, 2, len(pairs)], F32))
        neg = ctx.enter_context(nc.sbuf_tensor(tag + "_neg", [P, 512], F32))
        ps = ctx.enter_context(nc.psum_tensor(tag + "_ps", [P, len(pairs)], F32))
        block, chain, summed, averaged = ctx.enter_context(phase(nc, "chain summed averaged"))

        @block.tensor
        def _(pe):
            pe.wait_ge(summed, 1)
            nc.tensor.matmul(ps[:], w["mean"], ab[:], start=True, stop=True).then_inc(averaged, 1)

        @block.vector
        def _(dve):
            V = nc.vector
            ch = Chain(dve, chain)
            for n, (src, dst) in enumerate(pairs):
                ch.then(V.tensor_reduce(ab[:, n:n + 1], src, AX, ALU.add, apply_absolute_value=True))
            dve.sem_inc(summed, 1)
            dve.wait_ge(averaged, 1)
            ch.then(V.tensor_scalar(th[:, 0], ps[:], 0.5 / 512, None, ALU.mult))
            ch.then(V.tensor_scalar(th[:, 1], ps[:], -0.5 / 512, None, ALU.mult))
            for n, (src, dst) in enumerate(pairs):
                ch.then(V.tensor_scalar(neg[:], src, th[:, 1, n:n + 1], None, ALU.is_lt))
                ch.then(V.scalar_tensor_tensor(out=dst, in0=src, scalar=th[:, 0, n:n + 1], in1=neg[:],
                                               op0=ALU.is_gt, op1=ALU.subtract))


def ffn3(nc, w, w_up, w_down, xn, g):
    M = 4
    with ExitStack() as ctx:
        def sb(name, shape):
            return ctx.enter_context(nc.sbuf_tensor("f3_" + name, shape, F32))

        up = ctx.enter_context(nc.psum_tensor("f3_up", [P, 2, TILE], F32))
        ms = ctx.enter_context(nc.psum_tensor("f3_ms", [P, 3, TILE], F32))
        down = ctx.enter_context(nc.psum_tensor("f3_down", [P, 2, TILE], F32))
        sqx = sb("sqx", [P, 2, TILE])
        rms = sb("rms", [P, 4, TILE])
        rin = sb("rin", [P, 4, TILE])
        hs = sb("hs", [P, M, TILE])
        h = sb("h", [P, M, TILE])
        sqh = sb("sqh", [P, M, TILE])
        (block, sqx_ready, msx_ready, rms_ready, eps_ready, rin_ready, up_ready, hs_ready, h_ready, sqh_ready, down_ready,
         msh_ready, done) = ctx.enter_context(phase(
             nc, "sqx_ready msx_ready rms_ready eps_ready rin_ready up_ready hs_ready h_ready sqh_ready down_ready "
             "msh_ready done"))

        @block.tensor
        def _(pe):
            with pe.Fori(0, NT // 2) as ii:
                for j in range(2):
                    pe.wait_ge(sqx_ready, ii * 2 + j + 1)
                    pe.wait_ge(rms_ready, ii * 4)
                    nc.tensor.matmul(ms[:, j], w["mean"], sqx[:, j], start=True, stop=True).then_inc(msx_ready, 1)
                for j in range(2):
                    i = ii * 2 + j
                    for m in range(M):
                        pe.wait_ge(hs_ready, i * M + m + 1)
                        nc.tensor.matmul(up[:, (j * M + m) % 2], w_up[:, m * P:(m + 1) * P],
                                         xn[:, tile(i)], start=True, stop=True).then_inc(up_ready, 1)
                    for m in range(M):
                        pe.wait_ge(h_ready, i * M + m + 1)
                        if m == 0:
                            pe.wait_ge(done, i + 1)
                        nc.tensor.matmul(down[:, j], w_down[:, m], h[:, m], start=m == 0, stop=m == M - 1)\
                            .then_inc(down_ready, 1)
                    pe.wait_ge(rms_ready, ii * 4 + (3 if j else 0))
                    for m in range(M):
                        pe.wait_ge(sqh_ready, i * M + m + 1)
                        mm = nc.tensor.matmul(ms[:, 2], w["mean"], sqh[:, m], start=m == 0, stop=m == M - 1)
                    mm.then_inc(msh_ready, 1)

        @block.scalar
        def _(act):
            with act.Fori(0, NT // 2) as ii:
                for j in range(2):
                    act.wait_ge(msx_ready, ii * 2)
                    nc.scalar.activation(sqx[:, j], xn[:, tile(ii * 2 + j)], ACT.Square).then_inc(sqx_ready, 1)
                for j in range(2):
                    act.wait_ge(msx_ready, ii * 2 + j + 1)
                    act.wait_ge(rin_ready, ii * 4)
                    nc.scalar.activation(rms[:, j], ms[:, j], ACT.Sqrt).then_inc(rms_ready, 1)
                for j in range(2):
                    i = ii * 2 + j
                    for m in range(M):
                        act.wait_ge(hs_ready, i * M + m + 3)
                        act.wait_ge(down_ready, i * M)
                        nc.scalar.activation(h[:, m], hs[:, m], ACT.Gelu).then_inc(h_ready, 1)
                    act.wait_ge(msh_ready, i)
                    for m in range(M):
                        act.wait_ge(h_ready, i * M + m + 1)
                        nc.scalar.activation(sqh[:, m], h[:, m], ACT.Square).then_inc(sqh_ready, 1)
                    act.wait_ge(msh_ready, i + 1)
                    nc.scalar.activation(rms[:, 2 + j], ms[:, 2], ACT.Sqrt, scale=0.25).then_inc(rms_ready, 1)

        @block.vector
        def _(dve):
            V = nc.vector
            dve.sem_inc(hs_ready, 2)
            dve.sem_inc(done, 2)
            with dve.Fori(0, NT // 2) as ii:
                def inverse(n):
                    dve.wait_ge(rms_ready, ii * 4 + n + 1)
                    V.tensor_scalar(rms[:, n], rms[:, n], 1e-8, None, ALU.add).then_inc(eps_ready, 1)
                    dve.wait_ge(eps_ready, ii * 4 + n + 1)
                    V.reciprocal(rin[:, n], rms[:, n]).then_inc(rin_ready, 1)
                    dve.wait_ge(rin_ready, ii * 4 + n + 1)

                for j in range(2):
                    i = ii * 2 + j
                    inverse(j)
                    for m in range(M):
                        dve.wait_ge(up_ready, i * M + m + 1)
                        dve.wait_ge(h_ready, (i - 1) * M + m + 1) if j else dve.wait_ge(h_ready, i * M)
                        V.tensor_tensor(hs[:, m], up[:, (j * M + m) % 2], rin[:, j], ALU.mult).then_inc(hs_ready, 1)
                for j in range(2):
                    i = ii * 2 + j
                    inverse(2 + j)
                    dve.wait_ge(down_ready, (i + 1) * M)
                    V.tensor_tensor(g[:, tile(i)], down[:, j], rin[:, 2 + j], ALU.mult).then_inc(done, 1)


def copy_padded(nc, src, dst):
    with phase(nc, "copied") as (block, copied):
        @block.vector
        def _(dve):
            for i in range(4):
                at = slice(i * B // 4, (i + 1) * B // 4)
                nc.vector.tensor_copy(padded(dst)[:, at, PAD:], src.rearrange("p (b t) -> p b t", t=T)[:, at])\
                    .then_inc(copied, 1)
            dve.wait_ge(copied, 4)


def layer3(nc, w0, groups, r0, r1, x_d, g_d, x_out):
    x, xn = r0[:, 0:N], r1[:, 0:N]
    layernorm(nc, "ln3", x, xn, w0, keep=x_d)
    with ExitStack() as ctx:
        w = ctx.enter_context(weights(nc, groups, "ffn3", w0))
        w_up = ctx.enter_context(nc.sbuf_tensor("l3_up", [P, 512], F32))
        w_down = ctx.enter_context(nc.sbuf_tensor("l3_down", [P, 4, P], F32))
        ternary(nc, "t3", w, [(w["w_upT"], w_up[:]), (w["w_downT"], w_down[:].rearrange("p m c -> p (m c)"))])
        ffn3(nc, w, w_up, w_down, xn, x)
        load(nc, "g_kept", [(g_d, x)])
    copy_padded(nc, xn, r0)
    with weights(nc, groups, "mamba3", w0) as w:
        mamba(nc, w, groups["once3"][0], True, r0, None, xn)
    gate_with(nc, "gw3", x_d, xn, g_d, x, x_out)



def common_pieces(np):
    return {
        "eye": np.eye(P, dtype=np.float32),
        "centre": (np.eye(P) - 1.0 / P).astype(np.float32),
        "mean": np.full((P, P), 1.0 / P, np.float32),
        "eps_col": np.full((P, 1), EPS, np.float32),
    }


def layer0_pieces(np, a):
    def padded_heads(m):
        out = np.zeros((m.shape[0], 4, 32), np.float32)
        out[:, :, 0:HL] = m.reshape(m.shape[0], 4, HL)
        return out.reshape(m.shape[0], P)

    return {
        "Wq": a["L0_attn_Wq"], "Wk": a["L0_attn_Wk"], "Wv": a["L0_attn_Wv"],
        "Wbeta": padded_heads(a["L0_attn_Wbeta"]), "Wo": a["L0_attn_Wo"],
        "bq": a["L0_attn_bq"][:, None], "bk": a["L0_attn_bk"][:, None], "bv": a["L0_attn_bv"][:, None],
        "bbeta": padded_heads(a["L0_attn_bbeta"][None]).T, "bo": a["L0_attn_bo"][:, None],
        "w_fc": a["L0_ffn_w_fc"].reshape(4, P, P).transpose(1, 0, 2).reshape(P, 512),
        "w_proj": a["L0_ffn_w_proj"], "uT": a["L0_ffn_u"].T, "v": a["L0_ffn_v"],
        "fast_bT": a["L0_ffn_fast_b"].T, "gate": np.full((P, 1), a["L0_ffn_gate"], np.float32),
    }


def routing_pieces(np):
    return {
        "tri": np.triu(np.ones((P, P), np.float32)),
        "ones": np.ones((P, P), np.float32),
        "iota8": np.tile(np.arange(-E8, 0, dtype=np.float32), (P, 1)),
    }


def layer1_pieces(np, a):
    K2 = 2 * KEIG
    swap = np.r_[KEIG:K2, 0:KEIG]
    couple = np.zeros((2, 4, 16, 2, 4, 16), np.float32)
    for r in range(2):
        for h in range(4):
            couple[r, h, :, r, h, :] = a["L1_attn_coupling"][h]
    couple = couple.reshape(K2, K2)
    inner = np.ones((P, TILE), np.float32)
    inner[:, 0::CH] = 0.0
    w_in = a["L1_attn_w_in"].T
    col = lambda v: v.reshape(-1, P).T
    return {
        "w_inT": w_in, "w_inT_sw": w_in[:, swap], "w_gateT": a["L1_attn_w_gate"].T, "b_gate": col(a["L1_attn_b_gate"]),
        "w_outT": a["L1_attn_w_out"].T, "couple": couple, "couple_sw": couple[:, swap],
        "frequency": np.tile(a["L1_attn_frequency"], 2)[:, None], "log_decay": np.tile(a["L1_attn_log_decay"], 2)[:, None],
        "steps": np.tile(np.arange(CH, dtype=np.float32), (P, 1)), "inner": inner,
        "sign": np.repeat(np.array([-1.0, 1.0], np.float32), KEIG)[:, None],
        "ln1_g": col(a["L1_attn_ln1_g"]), "ln1_b": col(a["L1_attn_ln1_b"]),
        "ln2_g": col(a["L1_attn_ln2_g"]), "ln2_b": col(a["L1_attn_ln2_b"]),
        "w_mlp1T": a["L1_attn_w_mlp1"].T, "b_mlp1": col(a["L1_attn_b_mlp1"]),
        "w_mlp2T": a["L1_attn_w_mlp2"].T.reshape(4, P, P).transpose(1, 0, 2).reshape(P, 512),
        "b_mlp2": col(a["L1_attn_b_mlp2"]),
    }


def expert_pieces(w1, w2):
    return {"w1": w1.transpose(1, 0, 2).reshape(P, E8 * 512),
            "w2": w2.reshape(E8, 4, P, P).transpose(2, 0, 1, 3).reshape(P, E8 * 512)}


def mamba_pieces(np, a, tag, l3):
    halves = lambda m: m.reshape(2, P, -1).transpose(1, 0, 2).reshape(P, -1)
    get = lambda name: a[f"{tag}_{name}"]
    conv = get("conv_w").reshape(DI, TAPS)
    if l3:
        in_w, xp, dt_w, out_w, a_log, d = (get("in_proj_w").T, get("x_proj_w").T, get("dt_proj_w").T,
                                           get("out_proj_w").T, get("A_log").T, get("D"))
        low, bc = xp[:, 0:64], xp[:, 64:]
    else:
        in_w, bc, dt_w, out_w, a_log, d = (get("in_proj_w"), get("x_proj_w"), get("dt_proj_w"), get("out_proj_w"),
                                           get("A_log"), get("D_skip"))
    spread = np.zeros((DI, 4, 2 * NSTATE), np.float32)
    spread[:, [0, 2, 3]] = bc[:, None]
    sel = np.zeros((P, 2 * NSTATE, P), np.float32)
    for first in (0, 64, 96):
        sel[first + np.arange(2 * NSTATE), np.arange(2 * NSTATE)] = 1.0
    out = {
        "in_w": in_w, "conv_b": halves(get("conv_b")),
        "xp_bc": halves(spread.reshape(DI, P)), "dt_w": dt_w, "dt_b": halves(get("dt_proj_b")),
        "A_log": halves(a_log), "D": halves(d), "out_w": halves(out_w),
    }
    once = {"conv_rows": np.tile(conv.T.reshape(1, TAPS * DI), (P, 1)), "sel_bc": sel.reshape(P, 2 * NSTATE * P)}
    if l3:
        out.update({"xp_low": halves(low), "in_b": get("in_proj_b").reshape(4, P).T, "conv_cols": halves(conv),
                    "out_b": get("out_proj_b")[:, None]})
    return out, once


def layer2_pieces(np, a):
    get = lambda name: a["L2_attn_" + name]
    inv = 1.0 / 10000.0 ** (np.arange(0, DH, 2, dtype=np.float32) / DH)
    emb = np.arange(T, dtype=np.float32)[:, None] * np.concatenate([inv, inv])[None].astype(np.float32)
    sign = np.where(np.arange(DH) < DH // 2, -1.0, 1.0)
    cos, sin = np.cos(emb).T, np.sin(emb).T * sign[:, None]
    heads = lambda m: np.tile(m, (NH, 1)).astype(np.float32)
    rot = np.arange(P).reshape(-1, 2, DH // 2)[:, ::-1].reshape(P)
    rows = np.arange(NKV)[:, None] * 32 + 1 + np.arange(DH)[None]
    swap = np.concatenate([np.arange(DH // 2, DH), np.arange(DH // 2)])

    def at_rows(m, axis=1):
        out = np.zeros((m.shape[0], P) if axis else (P, m.shape[1]), np.float32)
        out[(slice(None), rows.reshape(-1)) if axis else (rows.reshape(-1),)] = m
        return out

    k_w = get("k_w")
    k_rot = k_w.reshape(P, NKV, DH)[:, :, swap].reshape(P, NKV * DH)
    of_head = lambda c: ((np.arange(NKV)[:, None] * QPK + c) * DH + np.arange(DH)[None]).reshape(-1)
    eye = np.eye(P, dtype=np.float32)
    key_heads = lambda m: at_rows(np.tile(m, (NKV, 1)).astype(np.float32), 0)
    col = lambda v: v.reshape(-1, P).T
    scale = 1.0 / np.sqrt(np.float32(DH))
    return {
        "ln2_g": col(get("ln2_g")), "ln2_b": col(get("ln2_b")), "ln3_g": col(get("ln3_g")), "ln3_b": col(get("ln3_b")),
        "q_w": get("q_w"), "q_w_rot": get("q_w")[:, rot], "k_w": at_rows(k_w), "k_w_rot": at_rows(k_rot), "v_w": np.pad(get("v_w"), ((0, 0), (0, P - NKV * DH))),
        "o_w": np.concatenate([at_rows(get("o_w")[of_head(c)], 0) for c in range(QPK)], axis=1),
        "spread": np.concatenate([at_rows(eye[:, of_head(c)]) for c in range(QPK)], axis=1),
        "sum_rows": np.repeat(eye[:, 0:P:32], 32, axis=1), "ones_rows": eye[:, 0:P:32].sum(axis=1, keepdims=True),
        "q_cos": heads(cos * scale), "q_sin": heads(sin * scale), "k_cos": key_heads(cos), "k_sin": key_heads(sin),
        "causal": np.where(np.tril(np.ones((P, P), bool)), 0.0, -1e9).astype(np.float32),
        "gm_w1": get("w1"), "gm_w3": get("w3"), "gm_w2": get("w2").reshape(4, P, P).transpose(1, 0, 2).reshape(P, 512),
    }


def experts2_pieces(np, a):
    moe = lambda name: a["L2_ffn_" + name]
    col = lambda v: v.reshape(-1, P).T
    experts = lambda m: m.reshape(E8 * 4, P).T
    return {
        "W_proj": moe("W_proj"), "b_proj": col(moe("b_proj")), "W_gate": moe("W_gate"), "b1": experts(moe("b1")),
        "eg": experts(moe("ln1_g")), "eb": experts(moe("ln1_b")), "eb2": np.tile(moe("b2").reshape(1, E8 * P), (P, 1)),
        "moe_g": col(moe("ln_g")), "moe_b": col(moe("ln_b")),
    }


def layer3_pieces(np, a):
    return {"w_upT": a["L3_ffn_w_up"].T,
            "w_downT": a["L3_ffn_w_down"].T.reshape(4, P, P).transpose(1, 0, 2).reshape(P, 512)}


def pack(np, pieces):
    cols, at, n = {}, [], 0
    for name, piece in pieces.items():
        cols[name] = (n, n + piece.shape[1])
        n += piece.shape[1]
        full = np.zeros((P, piece.shape[1]), np.float32)
        full[0:piece.shape[0]] = piece
        at.append(full)
    return np.ascontiguousarray(np.concatenate(at, axis=1)), cols


def groups_of(np, a):
    col = lambda v: v.reshape(-1, P).T
    mamba2, once2 = mamba_pieces(np, a, "L2_attn", False)
    mamba3, once3 = mamba_pieces(np, a, "L3_attn", True)
    mamba2.update({"ln1_g": col(a["L2_attn_ln1_g"]), "ln1_b": col(a["L2_attn_ln1_b"])})
    experts1 = {"router": a["L1_ffn_router_w"], "moe_bias": a["L1_ffn_bias"].reshape(P, 1),
                **expert_pieces(a["L1_ffn_w1"], a["L1_ffn_w2"])}
    experts2 = {**experts2_pieces(np, a), **expert_pieces(a["L2_ffn_W1"], a["L2_ffn_W2"])}
    return {"common": common_pieces(np), "l0": layer0_pieces(np, a), "l1": layer1_pieces(np, a),
            "route": routing_pieces(np), "experts1": experts1, "experts2": experts2, "mamba2": mamba2, "once2": once2,
            "attention2": layer2_pieces(np, a), "mamba3": mamba3, "once3": once3, "ffn3": layer3_pieces(np, a)}


def build(nc, groups, x_in, x_out, x_d, g_d, x_slots, y_slots, layers=(0, 1, 2, 3)):
    with ExitStack() as ctx:
        r0 = ctx.enter_context(nc.sbuf_tensor("r0", [P, B * TP], F32))
        r1 = ctx.enter_context(nc.sbuf_tensor("r1", [P, B * TP], F32))
        w0 = ctx.enter_context(weights(nc, groups, "common", {}))
        if 0 in layers:
            with nc.sbuf_tensor("x0", [P, N], F32) as x0, nc.sbuf_tensor("s0", [P, N], F32) as s0:
                load(nc, "x_loaded", [(x0[:], x_in)])
                layer0(nc, w0, groups, x0[:], r1[:, 0:N], s0[:], r0[:, 0:N])
        else:
            load(nc, "x_loaded", [(r0[:, 0:N], x_in)])
        if 1 in layers:
            with nc.sbuf_tensor("s1", [P, N], F32) as s1:
                layer1(nc, w0, groups, r0[:, 0:N], r1[:, 0:N], s1[:], x_slots, y_slots)
        if 2 in layers:
            layer2(nc, w0, groups, r0, r1, x_d, g_d, x_slots, y_slots)
        if 3 in layers:
            layer3(nc, w0, groups, r0, r1, x_d, g_d, x_out)
        else:
            load(nc, "x_stored", [(x_out, r0[:, 0:N])])


def kernel(**inputs):
    import numpy as np
    import concourse.bacc as bacc
    from concourse.bass_utils import run_bass_kernel_spmd

    a = {k: np.asarray(v) for k, v in inputs.items()}
    nc = bacc.Bacc("TRN2", target_bir_lowering=False, num_devices=1)
    arrays, groups = {}, {}
    for name, pieces in groups_of(np, a).items():
        arrays["in_" + name], cols = pack(np, pieces)
        groups[name] = (nc.dram_tensor("in_" + name, arrays["in_" + name].shape, F32, kind="ExternalInput").ap(), cols)
    arrays["in_x"] = np.ascontiguousarray(a["L0_attn_x"].transpose(2, 1, 0).reshape(P, N))
    x_in = nc.dram_tensor("in_x", (P, N), F32, kind="ExternalInput").ap()
    x_out = nc.dram_tensor("out_x", (P, N), F32, kind="ExternalOutput").ap()
    x_d = nc.dram_tensor("kept_x", (P, N), F32).ap()
    g_d = nc.dram_tensor("kept_g", (P, N), F32).ap()
    x_slots = nc.dram_tensor("x_slots", (2 * N, P), F32).ap()
    y_slots = nc.dram_tensor("y_slots", (2 * N, P), F32).ap()
    build(nc, groups, x_in, x_out, x_d, g_d, x_slots, y_slots)
    r = run_bass_kernel_spmd(nc, [arrays], core_ids=[0])
    return np.ascontiguousarray(r.results[0]["out_x"].reshape(P, B, T).transpose(1, 2, 0))
```
